# Optimizing a Trainium2 kernel written in Bass

```python
import numpy as np
import jax
import jax.numpy as jnp

def _softmax(x, axis=-1):
    return jax.nn.softmax(x, axis=axis)

def _gelu(x):
    return jax.nn.gelu(x, approximate=True)

def _silu(x):
    return jax.nn.silu(x)

def _sigmoid(x):
    return jax.nn.sigmoid(x)

def _layernorm(x, axis=-1, eps=1e-05):
    m = jnp.mean(x, axis=axis, keepdims=True)
    v = jnp.var(x, axis=axis, keepdims=True)
    return (x - m) / jnp.sqrt(v + eps)

def _scatter_add(tgt, idx, src, axis=0):
    return tgt.at[idx].add(src)

def _segment_sum(src, seg, n):
    return jax.ops.segment_sum(src, seg, n)
kernel_name = 'mk_xattn_seq_d4_seqx_r4_6a656a'

def setup_inputs(seed: int=0):
    np.random.seed(seed)
    _w = jnp.asarray

    def _rec_inputs():
        import jax
        import jax.numpy as jnp
        _rk = jax.random.key(seed)
        x = -0.0002928 + 1 * jax.random.normal(jax.random.fold_in(_rk, 1), (16, 256, 256), jnp.float32)
        _lenS = 256 - jax.random.randint(jax.random.fold_in(_rk, 7), (16,), 0, max(1, 256 // 4) + 1, jnp.int32)
        _lenS2 = 120 - jax.random.randint(jax.random.fold_in(_rk, 8), (16,), 0, max(1, 120 // 4) + 1, jnp.int32)
        _ctx_1024P = jax.random.normal(jax.random.fold_in(_rk, 11), (16, 16, 256), jnp.float32)
        _ctx_1024c = jax.random.dirichlet(jax.random.fold_in(_rk, 511), 0.3 * jnp.ones((16,), jnp.float32), (16, 120))
        _ctx_1024t = jnp.einsum('bsk,bkd->bsd', _ctx_1024c, _ctx_1024P)
        _ctx_1024t = _ctx_1024t * jax.lax.rsqrt(jnp.mean(jnp.square(_ctx_1024t)) + 1e-12) * 0.953939
        ctx_1024 = -1.39393e-06 + 0.999914 * (_ctx_1024t + 0.3 * jax.random.normal(jax.random.fold_in(_rk, 611), (16, 120, 256), jnp.float32))
        itok_BxS_0_255 = jax.random.randint(jax.random.fold_in(_rk, 13), (16, 256), 0, 64, jnp.int32)
        _validS = jnp.arange(256)[None, :] < _lenS[:, None]
        _validS2 = jnp.arange(120)[None, :] < _lenS2[:, None]
        _causal = jnp.tril(jnp.ones((256, 256), dtype=bool))
        mask_BxS2_bf1 = jnp.ones((16, 120), dtype=bool)
        return (x, ctx_1024, itok_BxS_0_255, mask_BxS2_bf1)
    x, ctx_1024, itok_BxS_0_255, mask_BxS2_bf1 = _rec_inputs()

    def _L0_xattn_setup():
        import jax, jax.numpy as jnp
        import numpy as np
        EPS = 1e-06
        N_HEADS = 16

        def rmsnorm(x, g):
            return x * jax.lax.rsqrt(jnp.mean(x * x, axis=-1, keepdims=True) + EPS) * g
        key = jax.random.key(seed)
        ks = jax.random.split(key, 8)
        B, Tq, Tc, dq, dc, dm = (2, 512, 512, 256, 256, 256)
        query = jax.random.normal(ks[0], (B, Tq, dq), dtype=jnp.float32)
        context = jax.random.normal(ks[1], (B, Tc, dc), dtype=jnp.float32)
        context_mask = jnp.ones((B, Tc), dtype=bool)
        s = 0.02
        Wq = jax.random.normal(ks[2], (dq, dm), dtype=jnp.float32) * s
        Wk = jax.random.normal(ks[3], (dc, dm), dtype=jnp.float32) * s
        Wv = jax.random.normal(ks[4], (dc, dm), dtype=jnp.float32) * s
        Wo = jax.random.normal(ks[5], (dm, dq), dtype=jnp.float32) * s
        g_q = jnp.ones((dq,), dtype=jnp.float32)
        g_c = jnp.ones((dc,), dtype=jnp.float32)
        g_out = jnp.ones((dq,), dtype=jnp.float32)
        return dict(query=query, context=context, context_mask=context_mask, Wq=Wq, Wk=Wk, Wv=Wv, Wo=Wo, g_q=g_q, g_c=g_c, g_out=g_out)
    _L0_xattn_all = _L0_xattn_setup()
    _L0_xattn_in = {k: v for k, v in _L0_xattn_all.items() if k in ('Wq', 'Wk', 'Wv', 'Wo', 'g_q', 'g_c', 'g_out')}
    del _L0_xattn_all

    def _L1_xattn_setup():
        import jax, jax.numpy as jnp
        import numpy as np
        import math
        EPS_RMS = 1.1920929e-07
        EPS_DEN = 1e-06

        def rmsnorm(x, gamma):
            ms = jnp.mean(x * x, axis=-1, keepdims=True)
            return x * jax.lax.rsqrt(ms + EPS_RMS) * gamma
        key = jax.random.key(seed)
        ks = jax.random.split(key, 8)
        B, T, K, D = (4, 1024, 64, 256)
        x_tokens = jax.random.normal(ks[0], (B, T, D), dtype=jnp.float32)
        ctx = jax.random.normal(ks[1], (B, K, D), dtype=jnp.float32)
        idx = jnp.sort(jax.random.randint(ks[2], (B, T), 0, K), axis=-1)
        s = 1.0 / math.sqrt(D)
        Wq = jax.random.normal(ks[3], (D, D), dtype=jnp.float32) * s
        Wk = jax.random.normal(ks[4], (D, D), dtype=jnp.float32) * s
        Wv = jax.random.normal(ks[5], (D, D), dtype=jnp.float32) * s
        Wo = jax.random.normal(ks[6], (D, D), dtype=jnp.float32) * s
        return {'x_tokens': x_tokens, 'ctx': ctx, 'ctx_index_per_token': idx, 'gamma_q': jnp.ones((D,), jnp.float32), 'gamma_kv': jnp.ones((D,), jnp.float32), 'Wq': Wq, 'Wk': Wk, 'Wv': Wv, 'Wo': Wo}
    _L1_xattn_all = _L1_xattn_setup()
    _L1_xattn_in = {k: v for k, v in _L1_xattn_all.items() if k in ('gamma_q', 'gamma_kv', 'Wq', 'Wk', 'Wv', 'Wo')}
    del _L1_xattn_all

    def _L2_xattn_setup():
        import jax, jax.numpy as jnp
        import numpy as np
        D = 256
        H = 16
        KD = D // H
        FFN = 1024
        B = 4
        L_IMG = 128
        L_TXT = 256
        EPS = 1e-05

        def _ln(x, g, b):
            m = jnp.mean(x, axis=-1, keepdims=True)
            v = jnp.mean(jnp.square(x - m), axis=-1, keepdims=True)
            return (x - m) * jax.lax.rsqrt(v + EPS) * g + b

        def _attention(q, k, v, causal):
            scores = jnp.einsum('bhld,bhmd->bhlm', q, k) / np.sqrt(KD).astype(q.dtype)
            if causal:
                Lq = q.shape[2]
                mask = jnp.triu(jnp.ones((Lq, Lq), dtype=bool), k=1)
                scores = jnp.where(mask, -jnp.inf, scores)
            probs = jax.nn.softmax(scores, axis=-1)
            return jnp.einsum('bhlm,bhmd->bhld', probs, v)
        key = jax.random.key(seed)
        ks = jax.random.split(key, 12)
        s = 0.02
        inp = {'images': jax.random.normal(ks[0], (B, L_IMG, D), jnp.float32), 'text': jax.random.normal(ks[1], (B, L_TXT, D), jnp.float32), 'w_qkv': jax.random.normal(ks[2], (3 * D, D), jnp.float32) * s, 'w_sa_out': jax.random.normal(ks[3], (D, D), jnp.float32) * s, 'g1': jnp.ones((D,), jnp.float32), 'b1': jnp.zeros((D,), jnp.float32), 'wq': jax.random.normal(ks[4], (D, D), jnp.float32) * s, 'wk': jax.random.normal(ks[5], (D, D), jnp.float32) * s, 'wv': jax.random.normal(ks[6], (D, D), jnp.float32) * s, 'w_ca_out': jax.random.normal(ks[7], (D, D), jnp.float32) * s, 'g2': jnp.ones((D,), jnp.float32), 'b2': jnp.zeros((D,), jnp.float32), 'w_ff1': jax.random.normal(ks[8], (FFN, D), jnp.float32) * s, 'b_ff1': jnp.zeros((FFN,), jnp.float32), 'w_ff2': jax.random.normal(ks[9], (D, FFN), jnp.float32) * s, 'b_ff2': jnp.zeros((D,), jnp.float32), 'g3': jnp.ones((D,), jnp.float32), 'b3': jnp.zeros((D,), jnp.float32)}
        return inp
    _L2_xattn_all = _L2_xattn_setup()
    _L2_xattn_in = {k: v for k, v in _L2_xattn_all.items() if k in ('w_qkv', 'w_sa_out', 'g1', 'b1', 'wq', 'wk', 'wv', 'w_ca_out', 'g2', 'b2', 'w_ff1', 'b_ff1', 'w_ff2', 'b_ff2', 'g3', 'b3')}
    del _L2_xattn_all

    def _L3_xattn_setup():
        import jax, jax.numpy as jnp
        import numpy as np
        N_HEADS, D_MODEL, D_K, D_V = (16, 256, 64, 64)
        B, S = (2, 512)
        key = jax.random.key(seed)
        k = jax.random.split(key, 7)
        s = 1.0 / np.sqrt(D_MODEL)
        return {'input_Q': jax.random.normal(k[0], (B, S, D_MODEL), jnp.float32), 'input_K': jax.random.normal(k[1], (B, S, D_MODEL), jnp.float32), 'input_V': jax.random.normal(k[2], (B, S, D_MODEL), jnp.float32), 'W_Q': jax.random.normal(k[3], (D_MODEL, N_HEADS * D_K), jnp.float32) * s, 'W_K': jax.random.normal(k[4], (D_MODEL, N_HEADS * D_K), jnp.float32) * s, 'W_V': jax.random.normal(k[5], (D_MODEL, N_HEADS * D_V), jnp.float32) * s, 'W_O': jax.random.normal(k[6], (N_HEADS * D_V, D_MODEL), jnp.float32) * s}
    _L3_xattn_all = _L3_xattn_setup()
    _L3_xattn_in = {k: v for k, v in _L3_xattn_all.items() if k in ('W_Q', 'W_K', 'W_V', 'W_O')}
    del _L3_xattn_all
    return {'x': x, 'ctx_1024': ctx_1024, 'itok_BxS_0_255': itok_BxS_0_255, 'mask_BxS2_bf1': mask_BxS2_bf1, 'L0_xattn_Wq': _L0_xattn_in['Wq'], 'L0_xattn_Wk': _L0_xattn_in['Wk'], 'L0_xattn_Wv': _L0_xattn_in['Wv'], 'L0_xattn_Wo': _L0_xattn_in['Wo'], 'L0_xattn_g_q': _L0_xattn_in['g_q'], 'L0_xattn_g_c': _L0_xattn_in['g_c'], 'L0_xattn_g_out': _L0_xattn_in['g_out'], 'L1_xattn_gamma_q': _L1_xattn_in['gamma_q'], 'L1_xattn_gamma_kv': _L1_xattn_in['gamma_kv'], 'L1_xattn_Wq': _L1_xattn_in['Wq'], 'L1_xattn_Wk': _L1_xattn_in['Wk'], 'L1_xattn_Wv': _L1_xattn_in['Wv'], 'L1_xattn_Wo': _L1_xattn_in['Wo'], 'L2_xattn_w_qkv': _L2_xattn_in['w_qkv'], 'L2_xattn_w_sa_out': _L2_xattn_in['w_sa_out'], 'L2_xattn_g1': _L2_xattn_in['g1'], 'L2_xattn_b1': _L2_xattn_in['b1'], 'L2_xattn_wq': _L2_xattn_in['wq'], 'L2_xattn_wk': _L2_xattn_in['wk'], 'L2_xattn_wv': _L2_xattn_in['wv'], 'L2_xattn_w_ca_out': _L2_xattn_in['w_ca_out'], 'L2_xattn_g2': _L2_xattn_in['g2'], 'L2_xattn_b2': _L2_xattn_in['b2'], 'L2_xattn_w_ff1': _L2_xattn_in['w_ff1'], 'L2_xattn_b_ff1': _L2_xattn_in['b_ff1'], 'L2_xattn_w_ff2': _L2_xattn_in['w_ff2'], 'L2_xattn_b_ff2': _L2_xattn_in['b_ff2'], 'L2_xattn_g3': _L2_xattn_in['g3'], 'L2_xattn_b3': _L2_xattn_in['b3'], 'L3_xattn_W_Q': _L3_xattn_in['W_Q'], 'L3_xattn_W_K': _L3_xattn_in['W_K'], 'L3_xattn_W_V': _L3_xattn_in['W_V'], 'L3_xattn_W_O': _L3_xattn_in['W_O']}

def reference(x, ctx_1024, itok_BxS_0_255, mask_BxS2_bf1, L0_xattn_Wq, L0_xattn_Wk, L0_xattn_Wv, L0_xattn_Wo, L0_xattn_g_q, L0_xattn_g_c, L0_xattn_g_out, L1_xattn_gamma_q, L1_xattn_gamma_kv, L1_xattn_Wq, L1_xattn_Wk, L1_xattn_Wv, L1_xattn_Wo, L2_xattn_w_qkv, L2_xattn_w_sa_out, L2_xattn_g1, L2_xattn_b1, L2_xattn_wq, L2_xattn_wk, L2_xattn_wv, L2_xattn_w_ca_out, L2_xattn_g2, L2_xattn_b2, L2_xattn_w_ff1, L2_xattn_b_ff1, L2_xattn_w_ff2, L2_xattn_b_ff2, L2_xattn_g3, L2_xattn_b3, L3_xattn_W_Q, L3_xattn_W_K, L3_xattn_W_V, L3_xattn_W_O):
    import jax
    import jax.numpy as jnp

    def _L0_xattn_ref(query, context, context_mask, Wq, Wk, Wv, Wo, g_q, g_c, g_out):
        import jax, jax.numpy as jnp
        import numpy as np
        EPS = 1e-06
        N_HEADS = 16

        def rmsnorm(x, g):
            return x * jax.lax.rsqrt(jnp.mean(x * x, axis=-1, keepdims=True) + EPS) * g
        B, Tq, _ = query.shape
        Tc = context.shape[1]
        H = N_HEADS
        dm = Wq.shape[1]
        hd = dm // H
        scale = hd ** (-0.5)
        q_norm = rmsnorm(query, g_q)
        c_norm = rmsnorm(context, g_c)
        Q = (q_norm @ Wq).reshape(B, Tq, H, hd).transpose(0, 2, 1, 3)
        K = (c_norm @ Wk).reshape(B, Tc, H, hd).transpose(0, 2, 1, 3)
        V = (c_norm @ Wv).reshape(B, Tc, H, hd).transpose(0, 2, 1, 3)
        scores = jnp.einsum('bhqd,bhkd->bhqk', Q, K) * scale
        scores = jnp.where(context_mask[:, None, None, :], scores, -jnp.inf)
        attn = jax.nn.softmax(scores, axis=-1)
        attn = jnp.nan_to_num(attn, nan=0.0)
        out = jnp.einsum('bhqk,bhkd->bhqd', attn, V)
        out = out.transpose(0, 2, 1, 3).reshape(B, Tq, dm)
        out = out @ Wo
        return rmsnorm(query + out, g_out)

    def _L1_xattn_ref(x_tokens, ctx, ctx_index_per_token, gamma_q, gamma_kv, Wq, Wk, Wv, Wo):
        import jax, jax.numpy as jnp
        import numpy as np
        import math
        EPS_RMS = 1.1920929e-07
        EPS_DEN = 1e-06

        def rmsnorm(x, gamma):
            ms = jnp.mean(x * x, axis=-1, keepdims=True)
            return x * jax.lax.rsqrt(ms + EPS_RMS) * gamma
        B, T, D = x_tokens.shape
        K = ctx.shape[1]
        H = 16
        hd = D // H

        def split(x):
            return x.reshape(B, -1, H, hd).transpose(0, 2, 1, 3)
        q = split(rmsnorm(x_tokens, gamma_q) @ Wq.T)
        kn = rmsnorm(ctx, gamma_kv)
        k = split(kn @ Wk.T)
        v = split(kn @ Wv.T)
        ctx_pos = jnp.arange(K)[None, None, :]
        mask = (jnp.abs(ctx_pos - ctx_index_per_token[:, :, None]) <= 1)[:, None]
        scores = jnp.einsum('bhqd,bhkd->bhqk', q, k) / math.sqrt(hd)
        w = jnp.square(jax.nn.relu(scores))
        w = jnp.where(mask, w, 0.0)
        denom = jnp.maximum(w.sum(-1, keepdims=True), EPS_DEN)
        out = jnp.einsum('bhqk,bhkd->bhqd', w / denom, v)
        out = out.transpose(0, 2, 1, 3).reshape(B, T, D)
        return x_tokens + out @ Wo.T

    def _L2_xattn_ref(images, text, w_qkv, w_sa_out, g1, b1, wq, wk, wv, w_ca_out, g2, b2, w_ff1, b_ff1, w_ff2, b_ff2, g3, b3):
        import jax, jax.numpy as jnp
        import numpy as np
        D = 256
        H = 16
        KD = D // H
        FFN = 1024
        B = 4
        L_IMG = 128
        L_TXT = 256
        EPS = 1e-05

        def _ln(x, g, b):
            m = jnp.mean(x, axis=-1, keepdims=True)
            v = jnp.mean(jnp.square(x - m), axis=-1, keepdims=True)
            return (x - m) * jax.lax.rsqrt(v + EPS) * g + b

        def _attention(q, k, v, causal):
            scores = jnp.einsum('bhld,bhmd->bhlm', q, k) / np.sqrt(KD).astype(q.dtype)
            if causal:
                Lq = q.shape[2]
                mask = jnp.triu(jnp.ones((Lq, Lq), dtype=bool), k=1)
                scores = jnp.where(mask, -jnp.inf, scores)
            probs = jax.nn.softmax(scores, axis=-1)
            return jnp.einsum('bhlm,bhmd->bhld', probs, v)
        Bt, Lt, _ = text.shape
        Bi, Li, _ = images.shape
        qkv = text @ w_qkv.T
        q, k, v = jnp.split(qkv, 3, axis=-1)
        qh = q.reshape(Bt, H, Lt, KD)
        kh = k.reshape(Bt, H, Lt, KD)
        vh = v.reshape(Bt, H, Lt, KD)
        att = _attention(qh, kh, vh, causal=True)
        stage1 = att.transpose(0, 2, 1, 3).reshape(Bt, Lt, D) @ w_sa_out.T
        x = _ln(text + stage1, g1, b1)
        qc = (x @ wq.T).reshape(Bt, H, Lt, KD)
        kc = (images @ wk.T).reshape(Bi, H, Li, KD)
        vc = (images @ wv.T).reshape(Bi, H, Li, KD)
        attc = _attention(qc, kc, vc, causal=False)
        stage2 = attc.transpose(0, 2, 1, 3).reshape(Bt, Lt, D) @ w_ca_out.T
        y = _ln(x + stage2, g2, b2)
        h = jax.nn.relu(y @ w_ff1.T + b_ff1)
        ff = h @ w_ff2.T + b_ff2
        return _ln(y + ff, g3, b3)

    def _L3_xattn_ref(input_Q, input_K, input_V, W_Q, W_K, W_V, W_O):
        import jax, jax.numpy as jnp
        import numpy as np
        N_HEADS, D_MODEL, D_K, D_V = (16, 256, 64, 64)
        B, S = (2, 512)
        b = input_Q.shape[0]
        Q = (input_Q @ W_Q).reshape(b, -1, N_HEADS, D_K).transpose(0, 2, 1, 3)
        K = (input_K @ W_K).reshape(b, -1, N_HEADS, D_K).transpose(0, 2, 1, 3)
        V = (input_V @ W_V).reshape(b, -1, N_HEADS, D_V).transpose(0, 2, 1, 3)
        scores = jnp.einsum('bhqd,bhkd->bhqk', Q, K) / np.sqrt(D_K)
        attn = jax.nn.softmax(scores, axis=-1)
        context = jnp.einsum('bhqk,bhkd->bhqd', attn, V)
        context = context.transpose(0, 2, 1, 3).reshape(b, -1, N_HEADS * D_V)
        out = context @ W_O + input_Q
        mu = jnp.mean(out, axis=-1, keepdims=True)
        var = jnp.var(out, axis=-1, keepdims=True)
        return (out - mu) / jnp.sqrt(var + 1e-05)
    x = _L0_xattn_ref(x, ctx_1024, mask_BxS2_bf1, L0_xattn_Wq, L0_xattn_Wk, L0_xattn_Wv, L0_xattn_Wo, L0_xattn_g_q, L0_xattn_g_c, L0_xattn_g_out)
    x = _L1_xattn_ref(x, ctx_1024, itok_BxS_0_255, L1_xattn_gamma_q, L1_xattn_gamma_kv, L1_xattn_Wq, L1_xattn_Wk, L1_xattn_Wv, L1_xattn_Wo)
    x = _L2_xattn_ref(ctx_1024, x, L2_xattn_w_qkv, L2_xattn_w_sa_out, L2_xattn_g1, L2_xattn_b1, L2_xattn_wq, L2_xattn_wk, L2_xattn_wv, L2_xattn_w_ca_out, L2_xattn_g2, L2_xattn_b2, L2_xattn_w_ff1, L2_xattn_b_ff1, L2_xattn_w_ff2, L2_xattn_b_ff2, L2_xattn_g3, L2_xattn_b3)
    x = _L3_xattn_ref(x, ctx_1024, ctx_1024, L3_xattn_W_Q, L3_xattn_W_K, L3_xattn_W_V, L3_xattn_W_O)
    return x

_drawn_inputs = setup_inputs


def setup_inputs(seed=0):
    import zlib

    import numpy as np

    out = dict(_drawn_inputs(seed))
    spreads = {'L0_xattn_g_q': (1.0, 0.6),
     'L0_xattn_g_c': (1.0, 0.2),
     'L0_xattn_g_out': (1.0, 0.2),
     'L1_xattn_gamma_q': (1.0, 0.2),
     'L1_xattn_gamma_kv': (1.0, 0.2),
     'L2_xattn_g1': (1.0, 0.2),
     'L2_xattn_b1': (0.0, 0.1),
     'L2_xattn_g2': (1.0, 0.2),
     'L2_xattn_b2': (0.0, 0.1),
     'L2_xattn_b_ff1': (0.0, 0.274),
     'L2_xattn_b_ff2': (0.0, 0.1),
     'L2_xattn_g3': (1.0, 0.2),
     'L2_xattn_b3': (0.0, 0.1)}
    factors = {'L0_xattn_Wq': 4.584,
     'L0_xattn_Wk': 4.416,
     'L2_xattn_w_qkv': 4.292,
     'L2_xattn_w_sa_out': 4.277,
     'L2_xattn_wq': 8.0,
     'L2_xattn_wk': 8.0,
     'L2_xattn_wv': 4.905,
     'L2_xattn_w_ca_out': 5.04}
    for name, (base, spread) in spreads.items():
        noise = np.random.default_rng([zlib.crc32(name.encode()), seed]).standard_normal(out[name].shape)
        drawn = base * np.exp(spread * noise) if base else spread * noise
        out[name] = jnp.asarray(drawn.astype(out[name].dtype))
    for name, factor in factors.items():
        out[name] = (out[name] * factor).astype(out[name].dtype)
    return out
```

```python
from contextlib import ExitStack

import concourse.bass as bass
from concourse import mybir

F32 = mybir.dt.float32
BF16 = mybir.dt.bfloat16
U8 = mybir.dt.uint8
I32 = mybir.dt.int32
ALU = mybir.AluOpType
ACT = mybir.ActivationFunctionType
AX = mybir.AxisListType

B, T, D, C, H = 16, 256, 256, 120, 16
P = 128
KT_ = D // P
HD = D // H
F = 1024
D3 = 64
M3 = H * D3 // P
G = 4
RING = 4
BIG = float(2 ** 100)
EPS_OF = [1e-6, 1e-6, 1.1920929e-07, 1.1920929e-07, 1e-5, 1e-5]
DEN0, DEN1 = 1e-30, 1e-6

WIDTHS = [("q0", 512), ("k0", 512), ("v0", 512), ("o0", 512), ("q1", 512), ("k1", 512), ("v1", 512), ("o1", 512),
          ("qkv", 1536), ("so", 512), ("qc", 512), ("kvc", 1024), ("co", 512), ("f1", 2048), ("f2", 2048),
          ("Q3", 2048), ("K3", 2048), ("V3", 2048), ("O3", 2048)]
WCOLS = sum(w for _, w in WIDTHS)
ROWS = ["g_out", "g1", "b1", "g2", "b2", "b_ff2", "g3", "b3"]

COST = {
    "load": (0, 0, 0.0), "masks": (0, 0, 0.0), "cnorm": (0, 0, 0.0), "cT": (2, 0, 0.9),
    "xnorm": (0, 0, 0.2), "xT": (1, 0, 0.6), "k": (0, 1, 0.9), "v": (1, 0, 0.9), "q": (1, 0, 1.8),
    "km": (0, 0, 0.0), "S": (0, 1, 0.85), "E": (0, 0, 0.0), "N": (0, 0, 0.0), "T": (1, 0, 0.55), "PV": (0, 1, 0.6),
    "OTT": (0, 1, 0.3), "ONT": (1, 0, 0.55), "OUT": (0, 1, 1.8), "outnorm": (0, 0, 0.2),
    "ckv": (2, 0, 1.9), "cout": (0, 0, 0.0), "cin": (0, 0, 0.0), "ckT": (0, 1, 0.3),
    "qkv": (3, 0, 5.4), "sout": (0, 0, 0.0), "sin": (0, 0, 0.0), "qpT": (1, 0, 0.55), "kpT": (0, 1, 0.55),
    "qc": (1, 0, 1.8), "qout": (0, 0, 0.0), "qin": (0, 0, 0.0), "ln": (0, 0, 0.3),
    "f1": (4, 0, 7.3), "f2": (0, 1, 7.3), "k3": (0, 2, 3.9), "v3": (2, 0, 3.6), "q3": (4, 0, 7.3), "PV3": (1, 0, 1.0),
    "OUT3": (0, 1, 7.3), "store": (0, 0, 0.0),
}


def units(block):
    if block == "S":
        return [(g, qt, half) for g in range(G) for qt, half in ((0, 0), (1, 0), (1, 1))]
    if block == "1":
        return [(g, 0, half) for g in range(G) for half in range(2)]
    return [(g, qt, 0) for g in range(G) for qt in range(2)]


def attention(block):
    todo, n = [], len(units(block))
    group = [u[0] for u in units(block)]
    late = 2 if block == "1" else 4 if block == "3" else 3
    ends = {max(i for i in range(n) if group[i] == g): g for g in range(G)}

    def values(g):
        todo.append(("PV3" if block == "3" else "PV", block, g))
        if block != "3" and g >= 1:
            todo.append(("OTT", block, g - 1))

    todo += [("km", block, 0), ("km", block, 1)]
    for i in range(n + late + 1):
        t = i - late
        if 0 <= t < n:
            if block != "1":
                todo.append(("T", block, t))
            elif t in ends:
                values(ends[t])
        if i < n:
            todo.append(("S", block, i))
            if i in ends and ends[i] + 2 < G:
                todo.append(("km", block, ends[i] + 2))
        if 0 <= i - 1 < n:
            todo.append(("E", block, i - 1))
        if block == "3" and 0 <= i - 2 < n:
            todo.append(("N", block, i - 2))
        if block != "1" and t - 1 in ends:
            values(ends[t - 1])
    if block == "3":
        return todo + [("OUT3", block, 0)]
    return todo + [("OTT", block, G - 1), ("ONT", block, 0), ("OUT", block, 0)]


def sequence_steps():
    s = [("load", "0", 0), ("masks", "0", 0), ("cnorm", "0", 0), ("xnorm", "0", 0), ("cT", "0", 0), ("k", "0", 0),
         ("xT", "0", 0), ("v", "0", 0), ("q", "0", 0)]
    s += attention("0")
    s += [("outnorm", "0", 0), ("k", "1", 0), ("v", "1", 0), ("xnorm", "1", 0), ("ckv", "C", 0), ("cout", "C", 0),
          ("xT", "1", 0), ("q", "1", 0)]
    s += attention("1")
    s += [("cin", "C", 0), ("xT", "S", 0), ("qkv", "S", 0), ("sout", "S", 0), ("sin", "S", 0), ("qpT", "S", 0),
          ("kpT", "S", 0)]
    s += attention("S")
    s += [("ln", "S", 0), ("ckT", "C", 0), ("xT", "C", 0), ("qc", "C", 0), ("qout", "C", 0), ("qin", "C", 0),
          ("qpT", "C", 0)]
    s += attention("C")
    s += [("ln", "C", 0), ("k3", "3", 0), ("v3", "3", 0), ("xT", "F", 0), ("f1", "F", 0), ("f2", "F", 0), ("ln", "F", 0),
          ("xT", "3", 0), ("q3", "3", 0)]
    s += attention("3")
    s += [("ln", "3", 0), ("store", "3", 0)]
    return s


class Step:
    def __init__(self, name, block, i, slot, a, d):
        self.name, self.block, self.i, self.slot, self.a, self.d = name, block, i, slot, a, d


def merged_order(lag):
    seq = sequence_steps()
    at, clock, order, a, d = [0, 0], [0.0, float(lag)], [], 0, 0
    while min(at) < len(seq):
        s = 0 if at[1] == len(seq) or (at[0] < len(seq) and clock[0] <= clock[1]) else 1
        name, block, i = seq[at[s]]
        na, nd, cost = COST[name]
        order.append(Step(name, block, i, s, a, d))
        a, d = a + na, d + nd
        clock[s] += cost
        at[s] += 1
    return order, a, d


ORDER, NA, ND = merged_order(14.0)
assert NA % RING == 0 and ND % RING == 0
FIND = {(x.name, x.block, x.i, x.slot): x for x in ORDER}


def build(nc, x, ctx, idx, mask, wall, cols, rows, scratch, out):
    with ExitStack() as stack:
        def sb(name, shape, dt=F32):
            return stack.enter_context(nc.sbuf_tensor(name, shape, dt))

        def two(name, shape, dt=F32):
            return [sb(f"{name}{s}", shape, dt) for s in range(2)]

        def sem(name):
            return stack.enter_context(nc.semaphore(name))

        def sem2(name):
            return [sem(f"{name}{s}") for s in range(2)]

        W = sb("W", [P, WCOLS])
        COLS = sb("COLS", [P, 16])
        ROW = sb("ROW", [P, len(ROWS), D])
        ID = sb("ID", [P, P])
        IDB = sb("IDB", [P, P], BF16)
        CAUSAL = sb("CAUSAL", [P, P], BF16)
        HM = sb("HM", [P, 8])
        HM3 = sb("HM3", [P, 2])
        ONEB = sb("ONEB", [1, P], BF16)
        ONEF = sb("ONEF", [P, H])
        NHALF = sb("NHALF", [P, 2])
        EPS = sb("EPS", [P, len(EPS_OF)])
        KEY = sb("KEY", [P, 1])
        KEYI = sb("KEYI", [P, 1], I32)

        X = two("X", [P, 2, D])
        XN = two("XN", [P, 2, D])
        XT = two("XT", [P, 2, T])
        QT = two("QT", [P, 2, T])
        KT = two("KT", [P, M3, C])
        CX = two("CX", [C, D])
        CN = two("CN", [C, 2, D])
        CT = two("CT", [P, 6, C])
        KM = two("KM", [P, 2, 4 * T])
        VA = two("VA", [P, H, 32])
        VS = two("VS", [P, 2, H, 32])
        V3 = [k[:, :, 512:1024] for k in KM]
        PB = two("PB", [P, RING, 512])
        PT = two("PT", [P, 2, 4, 3, P])
        OT = two("OT", [P, 2, T])
        WIDE = two("WIDE", [P, 8 * T])
        KP = two("KP", [C, D])
        NM = two("NM", [P, RING, 4])
        SUM = two("SUM", [P, RING, 2, 4])
        REC = two("REC", [P, RING, 2, 4])
        SS = two("SS", [P, 8])
        RSTD = two("RSTD", [P, 2])
        VAR = two("VAR", [P, 2])
        BN = two("BN", [P, 2, 6])
        MV = two("MV", [P, 2, 2])
        IDX = two("IDX", [C, T], I32)
        BAND = two("BAND", [C, T])
        MROW = two("MROW", [1, C], U8)
        MCOL = two("MCOL", [C, 1], U8)
        BIAS = two("BIAS", [1, C], BF16)
        MASK = two("MASK", [C, 1])

        PA = stack.enter_context(nc.psum_tensor("PA", [P, RING, 512], F32))
        PD = stack.enter_context(nc.psum_tensor("PD", [P, RING, 512], F32))

        weights_in = sem("weights_in")
        consts = sem("consts")
        a_full, d_full = sem("a_full"), sem("d_full")
        a_empty, d_empty = sem("a_empty"), sem("d_empty")
        loaded = sem2("loaded")
        masks_ready = sem2("masks_ready")
        square_done = sem2("square_done")
        rstd_ready = sem2("rstd_ready")
        cn_ready = sem2("cn_ready")
        xn_ready = sem2("xn_ready")
        km_ready = sem2("km_ready")
        exp_done = sem2("exp_done")
        recip_ready = sem2("recip_ready")
        p_scaled = sem2("p_scaled")
        moments = sem2("moments")
        x_ready = sem2("x_ready")
        yb_ready = sem2("yb_ready")
        bounced_out = sem2("bounced_out")
        self_in, ckv_in, qc_in = sem2("self_in"), sem2("ckv_in"), sem2("qc_in")
        stored = sem2("stored")
        slot_free = sem2("slot_free")
        stats_done = sem("stats_done")
        vec = sem("vec")
        pool = sem("pool")

        offsets, at = {}, 0
        for name, w in WIDTHS:
            offsets[name] = (at, w)
            at += w

        def weight(name, width):
            o, w = offsets[name]
            return W[:, o:o + w].rearrange("p (k n) -> p k n", n=width)

        WQ = {"0": weight("q0", D), "1": weight("q1", D)}
        WK = {"0": weight("k0", D), "1": weight("k1", D)}
        WV = {"0": weight("v0", D), "1": weight("v1", D)}
        WO = {"0": weight("o0", D), "1": weight("o1", D), "S": weight("so", D), "C": weight("co", D)}
        WQKV, WQC, WKVC = weight("qkv", 3 * D), weight("qc", D), weight("kvc", 2 * D)
        W1, W2 = weight("f1", F), weight("f2", D)
        W3Q, W3K, W3V, W3O = weight("Q3", H * D3), weight("K3", H * D3), weight("V3", H * D3), weight("O3", D)

        def row(name):
            return ROW[:, ROWS.index(name), :]

        def kt(s, block):
            if block == "S":
                return KT[s][:, :, :].rearrange("p m n -> p (m n)")[:, 0:2 * T].rearrange("p (m n) -> p m n", n=T)
            return KT[s][:, :, :]

        def keys(block):
            return T if block == "S" else C

        def pv(s, block):
            return VS[s] if block == "S" else VA[s]

        def by_position(s, t, n):
            flat = scratch[s, t].rearrange("n c -> (n c)")[0:n * D]
            return flat.rearrange("(h n d) -> n h d", h=H, d=HD)

        block = stack.enter_context(nc.Block())

        class Nth:

            def __init__(self, it):
                self.it, self.n = it, {}

            def __call__(self, semaphore, per, unit=1):
                k = self.n.get(id(semaphore), 0) + 1
                self.n[id(semaphore)] = k
                assert k <= per, (semaphore, k, per)
                return self.it * (per * unit) + k * unit

        N_LOAD, N_KM, N_EXP, N_L3 = 5, 5 * G, 8 * 4 + 12, 8

        @block.sync
        def _(sp):
            for a, b in ((0, 2048), (2048, 4096), (4096, 6144), (6144, 8192), (8192, 12288), (12288, 16384), (16384, WCOLS)):
                if a == 0:
                    sp.dma_start(COLS[:, :], cols).then_inc(weights_in, 16)
                    sp.dma_start(ROW[:, :, :], rows.rearrange("(a r) c -> a r c", a=1).to_broadcast([P, len(ROWS), D]))\
                      .then_inc(weights_in, 16)
                sp.dma_start(W[:, a:b], wall[:, a:b]).then_inc(weights_in, 16)
            with sp.Fori(0, B // 2) as it:
                nth = Nth(it)
                for st in ORDER:
                    s, n = st.slot, it * 2 + st.slot
                    if st.name == "load":
                        sp.dma_start(CX[s][:, :], ctx[bass.ds(n, 1)].rearrange("a n c -> (a n) c")).then_inc(loaded[s], 16)
                        sp.dma_start(MROW[s][:, :], mask[bass.ds(n, 1), :]).then_inc(loaded[s], 16)
                        sp.dma_start(MCOL[s][:, :], mask[bass.ds(n, 1), :].rearrange("a n -> n a")).then_inc(loaded[s], 16)
                        sp.dma_start(X[s][:, :, :], x[bass.ds(n, 1)].rearrange("a (t p) c -> p (a t) c", p=P))\
                          .then_inc(loaded[s], 16)
                        sp.dma_start(IDX[s][:, :], idx[bass.ds(n, 1), :].to_broadcast([C, T])).then_inc(loaded[s], 16)
                    if st.name == "cout":
                        sp.wait_ge(a_empty, it * NA + FIND["ckv", "C", 0, s].a + 2 + RING)
                        for t in range(2):
                            sp.dma_start(scratch[s, 3 + t, 0:C, :], CN[s][:, t, :]).then_inc(bounced_out[s], 16)
                    if st.name == "cin":
                        sp.wait_ge(d_full, it * ND + FIND["OUT", "1", 0, s].d + 1)
                        sp.wait_ge(bounced_out[s], it * 96 + 32)
                        sp.dma_start(KP[s][:, :].rearrange("p (h d) -> p h d", d=HD), by_position(s, 3, C))\
                          .then_inc(ckv_in[s], 16)
                        sp.dma_start(VA[s][0:C, :, 0:HD], by_position(s, 4, C)).then_inc(ckv_in[s], 16)
                    if st.name == "sout":
                        sp.wait_ge(a_empty, it * NA + FIND["qkv", "S", 0, s].a + 3 + RING)
                        for t in range(3):
                            src = WIDE[s][:, 0:6 * D].rearrange("p (k t c) -> p k t c", k=2, t=3)[:, :, t, :]
                            sp.dma_start(scratch[s, t].rearrange("(k p) c -> p k c", p=P), src)\
                              .then_inc(bounced_out[s], 16)
                    if st.name == "sin":
                        sp.wait_ge(bounced_out[s], it * 96 + 80)
                        for t, dst in ((0, XT[s]), (1, XN[s])):
                            for k in range(2):
                                sp.dma_start(dst[:, k, :].rearrange("p (h d) -> p h d", d=HD),
                                             by_position(s, t, T)[k * P:(k + 1) * P]).then_inc(self_in[s], 16)
                        for k in range(2):
                            sp.dma_start(VS[s][:, k, :, 0:HD], by_position(s, 2, T)[k * P:(k + 1) * P])\
                              .then_inc(self_in[s], 16)
                    if st.name == "qout":
                        sp.wait_ge(a_empty, it * NA + FIND["qc", "C", 0, s].a + 1 + RING)
                        sp.dma_start(scratch[s, 0].rearrange("(k p) c -> p k c", p=P),
                                     WIDE[s][:, 0:2 * D].rearrange("p (k c) -> p k c", k=2)).then_inc(bounced_out[s], 16)
                    if st.name == "qin":
                        sp.wait_ge(bounced_out[s], it * 96 + 96)
                        for k in range(2):
                            sp.dma_start(XT[s][:, k, :].rearrange("p (h d) -> p h d", d=HD),
                                         by_position(s, 0, T)[k * P:(k + 1) * P]).then_inc(qc_in[s], 16)
                    if st.name == "store":
                        sp.wait_ge(x_ready[s], it * 5 + 5)
                        sp.dma_start(out[bass.ds(n, 1)].rearrange("a (t p) c -> p (a t) c", p=P), XN[s][:, :, :])\
                          .then_inc(stored[s], 16)
                        sp.wait_ge(stored[s], it * 16 + 16)
                        sp.sem_inc(slot_free[s], 1)

        @block.gpsimd
        def _(gp):
            gp.memset(ID[:, :], 0.0).then_inc(pool, 1)
            gp.memset(CAUSAL[:, :], 0.0).then_inc(pool, 1)
            gp.memset(HM[:, :], 1.0).then_inc(pool, 1)
            gp.memset(HM3[:, :], 1.0).then_inc(pool, 1)
            gp.iota(KEYI[:, :], pattern=[[0, 1]], base=0, channel_multiplier=-1).then_inc(pool, 1)
            gp.wait_ge(pool, 5)
            gp.affine_select(out=ID[:, :], in_=ID[:, :], compare_op=ALU.not_equal, fill=1.0, base=0,
                             pattern=[[-1, P]], channel_multiplier=1).then_inc(pool, 1)
            gp.affine_select(out=CAUSAL[:, :], in_=CAUSAL[:, :], compare_op=ALU.is_ge, fill=-BIG, base=0,
                             pattern=[[-1, P]], channel_multiplier=1).then_inc(consts, 1)
            gp.affine_select(out=HM[:, :], in_=HM[:, :], compare_op=ALU.is_ge, fill=0.0, base=0,
                             pattern=[[-HD, 8]], channel_multiplier=1).then_inc(pool, 1)
            gp.affine_select(out=HM3[:, :], in_=HM3[:, :], compare_op=ALU.is_ge, fill=0.0, base=0,
                             pattern=[[-D3, 2]], channel_multiplier=1).then_inc(pool, 1)
            gp.wait_ge(pool, 8)
            gp.affine_select(out=HM[:, :], in_=HM[:, :], compare_op=ALU.is_gt, fill=0.0, base=HD,
                             pattern=[[HD, 8]], channel_multiplier=-1).then_inc(consts, 1)
            gp.affine_select(out=HM3[:, :], in_=HM3[:, :], compare_op=ALU.is_gt, fill=0.0, base=D3,
                             pattern=[[D3, 2]], channel_multiplier=-1).then_inc(consts, 1)
            gp.tensor_copy(IDB[:, :], ID[:, :]).then_inc(consts, 1)
            gp.tensor_copy(KEY[:, :], KEYI[:, :]).then_inc(consts, 1)
            gp.memset(NHALF[:, :], -0.5).then_inc(consts, 1)
            for j, eps in enumerate(EPS_OF):
                gp.memset(EPS[:, j:j + 1], eps)
            gp.memset(ONEB[:, :], 1.0).then_inc(consts, 1)
            gp.memset(ONEF[:, :], 1.0).then_inc(consts, 1)
            gp.wait_ge(consts, 8)
            with gp.Fori(0, B // 2) as it:
                nth = Nth(it)
                base = 8
                steps_in_pass = [0]

                def own(ins):
                    steps_in_pass[0] += 1
                    ins.then_inc(pool, 1)
                    gp.wait_ge(pool, it * POOL_N + base + steps_in_pass[0])

                def rstd(s, n, src, eps):
                    w = src.shape[-1]
                    own(gp.tensor_tensor(VAR[s][0:n, 0:w], src, EPS[0:n, eps:eps + w], ALU.add))
                    gp.tensor_tensor(RSTD[s][0:n, 0:w], VAR[s][0:n, 0:w], NHALF[0:n, 0:w], ALU.pow)\
                      .then_inc(rstd_ready[s], 1)

                for st in ORDER:
                    s, blk, i = st.slot, st.block, st.i
                    if st.name == "cnorm":
                        gp.wait_ge(square_done[s], nth(square_done[s], 4))
                        rstd(s, C, SS[s][0:C, 0:1].to_broadcast([C, 2]), 1)
                    if st.name == "xnorm":
                        gp.wait_ge(square_done[s], nth(square_done[s], 4))
                        if blk == "0":
                            gp.wait_ge(cn_ready[s], nth(cn_ready[s], 1))
                        rstd(s, P, SS[s][:, 2:4], 0 if blk == "0" else 2)
                    if st.name == "outnorm":
                        gp.wait_ge(square_done[s], nth(square_done[s], 4))
                        rstd(s, P, SS[s][:, 2:4], 0)
                    if st.name == "ln":
                        gp.wait_ge(moments[s], nth(moments[s], 4))
                        rstd(s, P, MV[s][:, :, 1:2].rearrange("p a b -> p (a b)"), 4)
                        if blk == "C":
                            gp.wait_ge(x_ready[s], it * 5 + 3)
                            gp.tensor_tensor(XN[s][:, :, :], X[s][:, :, :],
                                             ROW[:, ROWS.index("b_ff2"):ROWS.index("b_ff2") + 1, :].to_broadcast([P, 2, D]),
                                             ALU.add).then_inc(yb_ready[s], 1)
                    if st.name == "km":
                        if i >= 2:
                            last = max(n for n, u in enumerate(units(blk)) if u[0] == i - 2)
                            gp.wait_ge(d_full, it * ND + FIND["S", blk, last, s].d + 1)
                        if i == 0:
                            src = FIND[{"0": "k", "1": "k", "S": "kpT", "C": "ckT", "3": "k3"}[blk], blk, 0, s]
                            gp.wait_ge(d_empty, it * ND + src.d + (2 if blk == "3" else 1) + RING)
                        n = keys(blk)
                        if blk == "3":
                            dst = KM[s][:, i % 2, 0:4 * n].rearrange("p (m h n) -> p m h n", m=2, h=2)
                            src = KT[s][:, 2 * i:2 * i + 2, None, :].to_broadcast([P, 2, 2, n])
                            sel = HM3[:, None, :, None].to_broadcast([P, 2, 2, n])
                        else:
                            dst = KM[s][:, i % 2, 0:4 * n].rearrange("p (h n) -> p h n", h=4)
                            src = kt(s, blk)[:, i // 2:i // 2 + 1, :].to_broadcast([P, 4, n])
                            sel = HM[:, (i % 2) * 4:(i % 2) * 4 + 4, None].to_broadcast([P, 4, n])
                        gp.tensor_tensor(dst, src, sel, ALU.mult).then_inc(km_ready[s], 1)
                    if st.name == "N":
                        gp.wait_ge(recip_ready[s], nth(recip_ready[s], N_L3))
                        p = PB[s][:, i % RING, 0:4 * C].rearrange("p (h n) -> p h n", h=4)
                        gp.tensor_tensor(p, p, REC[s][:, i % RING, 0, :, None].to_broadcast([P, 4, C]), ALU.mult)\
                          .then_inc(p_scaled[s], 1)
                assert steps_in_pass[0] == POOL_N, steps_in_pass

        @block.scalar
        def _(act):
            act.sem_inc(a_empty, RING)
            act.wait_ge(weights_in, 16 * 9)
            act.wait_ge(consts, 8)
            act.wait_ge(vec, 6)
            with act.Fori(0, B // 2) as it:
                nth = Nth(it)

                def bank(a):
                    act.wait_ge(a_full, it * NA + a + 1)
                    return PA[:, a % RING, :]

                for st in ORDER:
                    s, blk, i, a = st.slot, st.block, st.i, st.a
                    if st.name == "cnorm":
                        act.wait_ge(loaded[s], it * (16 * N_LOAD) + 16 * N_LOAD)
                        act.activation(CN[s][:, 0, :], CX[s][:, :], ACT.Square, scale=1 / 16, accum_out=SS[s][0:C, 0:1])\
                           .then_inc(square_done[s], 1)
                    if st.name == "xnorm" and blk == "0":
                        for t in range(2):
                            ins = act.activation(XN[s][:, t, :], X[s][:, t, :], ACT.Square, scale=1 / 16,
                                                 accum_out=SS[s][:, 2 + t:3 + t])
                        ins.then_inc(square_done[s], 1)
                        act.wait_ge(rstd_ready[s], it * 8 + 1)
                        act.activation(CN[s][:, 0, :], CX[s][:, :], ACT.Copy, scale=RSTD[s][0:C, 0:1])
                        act.activation(CN[s][:, 1, :], CX[s][:, :], ACT.Copy, scale=RSTD[s][0:C, 1:2])\
                           .then_inc(cn_ready[s], 1)
                        act.wait_ge(rstd_ready[s], it * 8 + 2)
                        for t in range(2):
                            ins = act.activation(XN[s][:, t, :], X[s][:, t, :], ACT.Copy, scale=RSTD[s][:, t:t + 1])
                        ins.then_inc(xn_ready[s], 1)
                    if st.name == "cT":
                        b = bank(a).rearrange("p (j n) -> p j n", n=P)
                        act.activation(CT[s][:, 0:2, :], b[:, 0:2, 0:C], ACT.Copy)
                        for k in range(2):
                            ins = act.activation(CT[s][:, 2 + k, :], b[:, 2 + k, 0:C], ACT.Copy, scale=COLS[:, 2 + k:3 + k])
                        ins.then_inc(a_empty, 1)
                        b = bank(a + 1).rearrange("p (j n) -> p j n", n=P)
                        for k in range(2):
                            ins = act.activation(CT[s][:, 4 + k, :], b[:, k, 0:C], ACT.Copy, scale=COLS[:, 6 + k:7 + k])
                        ins.then_inc(a_empty, 1)
                    if st.name == "xT":
                        b = bank(a).rearrange("p (k n) -> p k n", n=T)
                        if blk in "01":
                            c = 0 if blk == "0" else 4
                            for k in range(2):
                                ins = act.activation(XT[s][:, k, :], b[:, k, :], ACT.Copy, scale=COLS[:, c + k:c + k + 1])
                            ins.then_inc(a_empty, 1)
                        else:
                            act.activation(XT[s][:, :, :], b, ACT.Copy).then_inc(a_empty, 1)
                    if st.name == "q" or st.name == "qpT":
                        b = bank(a).rearrange("p (k n) -> p k n", n=T)
                        act.activation(QT[s][:, :, :], b, ACT.Copy).then_inc(a_empty, 1)
                    if st.name == "ONT":
                        b = bank(a).rearrange("p (k n) -> p k n", n=T)
                        act.activation(XT[s][:, :, :], b, ACT.Copy).then_inc(a_empty, 1)
                    if st.name == "v":
                        b = bank(a)[0:C, 0:D].rearrange("p (h d) -> p h d", d=HD)
                        if blk == "0":
                            act.wait_ge(masks_ready[s], nth(masks_ready[s], 1))
                            act.activation(VA[s][0:C, :, HD], ONEF[0:C, :], ACT.Copy, scale=MASK[s][:, 0:1])
                            act.activation(VA[s][0:C, :, 0:HD], b, ACT.Copy, scale=MASK[s][:, 0:1]).then_inc(a_empty, 1)
                        else:
                            act.activation(VA[s][0:C, :, HD], ONEF[0:C, :], ACT.Copy)
                            act.activation(VA[s][0:C, :, 0:HD], b, ACT.Copy).then_inc(a_empty, 1)
                    if st.name == "v3":
                        for j in range(2):
                            b = bank(a + j)
                            act.activation(V3[s][0:C, j, :], b[0:C, :], ACT.Copy).then_inc(a_empty, 1)
                    if st.name == "ckv":
                        for t in range(2):
                            b = bank(a + t)[0:C, 0:D]
                            act.activation(CN[s][:, t, :], b, ACT.Copy).then_inc(a_empty, 1)
                    if st.name == "qkv":
                        w = WIDE[s][:, 0:6 * D].rearrange("p (k c) -> p k c", k=2)
                        for t in range(2):
                            b = bank(a + t)
                            act.activation(w[:, t, 0:2 * D], b, ACT.Copy).then_inc(a_empty, 1)
                        b = bank(a + 2).rearrange("p (k c) -> p k c", k=2)
                        act.activation(w[:, :, 2 * D:3 * D], b, ACT.Copy).then_inc(a_empty, 1)
                    if st.name == "qc":
                        b = bank(a)
                        act.activation(WIDE[s][:, 0:2 * D], b, ACT.Copy).then_inc(a_empty, 1)
                    if st.name == "f1":
                        for j in range(4):
                            b = bank(a + j).rearrange("p (k n) -> p k n", n=T)
                            for k in range(2):
                                m = 2 * j + k
                                ins = act.activation(WIDE[s][:, m * T:(m + 1) * T], b[:, k, :], ACT.Relu,
                                                     bias=COLS[:, 8 + m:9 + m])
                            ins.then_inc(a_empty, 1)
                    if st.name == "q3":
                        for j in range(4):
                            b = bank(a + j)
                            act.activation(WIDE[s][:, j * 512:(j + 1) * 512], b, ACT.Copy).then_inc(a_empty, 1)
                    if st.name == "PV3":
                        b = bank(a)
                        act.activation(WIDE[s][:, i * 512:(i + 1) * 512], b, ACT.Copy).then_inc(a_empty, 1)
                    if st.name == "E":
                        g, qt, half = units(blk)[i]
                        act.wait_ge(d_empty, it * ND + FIND["S", blk, i, s].d + 1 + RING)
                        n = 4 * C if blk in "0C3" else 512
                        p = PB[s][:, i % RING, 0:n]
                        if blk == "1":
                            dst = PT[s][0:C, g % 2, 2 * half:2 * half + 2, 0:2, :].rearrange("p h q n -> p h (q n)")
                            act.activation(dst, PB[s][0:C, i % RING, :].rearrange("p (h n) -> p h n", h=2), ACT.Square,
                                           scale=0.25).then_inc(exp_done[s], 1)
                        else:
                            act.activation(p, p, ACT.Exp, scale=0.125 if blk == "3" else 0.25).then_inc(exp_done[s], 1)
                    if st.name == "T":
                        g, qt, half = units(blk)[i]
                        n = P if blk == "S" else C
                        b = bank(a)[0:n, :]
                        if blk == "S" and qt == 1:
                            dst = PT[s][:, g % 2, 2 * half:2 * half + 2, 1:3, :].rearrange("p h t n -> p h (t n)")
                            act.activation(dst, b.rearrange("p (h n) -> p h n", h=2), ACT.Copy).then_inc(a_empty, 1)
                        else:
                            act.activation(PT[s][0:n, g % 2, :, qt, :], b.rearrange("p (h n) -> p h n", h=4), ACT.Copy)\
                               .then_inc(a_empty, 1)
                    if st.name == "xnorm" and blk == "1" or st.name == "outnorm":
                        if st.name == "xnorm":
                            act.wait_ge(x_ready[s], nth(x_ready[s], 5))
                        else:
                            act.wait_ge(d_empty, it * ND + FIND["OUT", "0", 0, s].d + 1 + RING)
                        for t in range(2):
                            ins = act.activation(XN[s][:, t, :], X[s][:, t, :], ACT.Square, scale=1 / 16,
                                                 accum_out=SS[s][:, 2 + t:3 + t])
                        ins.then_inc(square_done[s], 1)
                        if st.name == "xnorm":
                            act.wait_ge(rstd_ready[s], it * 8 + 4)
                            for t in range(2):
                                ins = act.activation(XN[s][:, t, :], X[s][:, t, :], ACT.Copy, scale=RSTD[s][:, t:t + 1])
                            ins.then_inc(xn_ready[s], 1)

        @block.vector
        def _(dve):
            dve.sem_inc(d_empty, RING)
            for s in range(2):
                dve.memset(VA[s][:, :, :], 0.0).then_inc(vec, 1)
                dve.memset(VS[s][:, :, :, :], 0.0).then_inc(vec, 1)
            dve.wait_ge(weights_in, 16 * 9)
            dve.wait_ge(consts, 8)
            dve.wait_ge(vec, 4)
            for s in range(2):
                dve.memset(VS[s][:, :, :, HD], 1.0).then_inc(vec, 1)
            with dve.Fori(0, B // 2) as it:
                nth = Nth(it)
                steps_in_pass = [0]

                def own(ins):
                    steps_in_pass[0] += 1
                    ins.then_inc(vec, 1)
                    dve.wait_ge(vec, it * VEC_N + 6 + steps_in_pass[0])

                def bank(d):
                    dve.wait_ge(d_full, it * ND + d + 1)
                    return PD[:, d % RING, :]

                for st in ORDER:
                    s, blk, i, d = st.slot, st.block, st.i, st.d
                    if st.name == "masks":
                        dve.wait_ge(loaded[s], it * (16 * N_LOAD) + 16 * N_LOAD)
                        dve.tensor_scalar(BIAS[s][:, :], MROW[s][:, :], -1.0, BIG, ALU.add, ALU.mult)
                        dve.tensor_copy(MASK[s][:, :], MCOL[s][:, :])
                        own(dve.tensor_scalar(BAND[s][:, :], IDX[s][:, :], KEY[0:C, 0:1], None, ALU.add))
                        own(dve.tensor_tensor(BAND[s][:, :], BAND[s][:, :], BAND[s][:, :], ALU.mult))
                        dve.tensor_scalar(BAND[s][:, :], BAND[s][:, :], 1.0, None, ALU.is_le).then_inc(masks_ready[s], 1)
                    if st.name == "k" or st.name == "ckT":
                        b = bank(d).rearrange("p (k n) -> p k n", n=T)[:, :, 0:C]
                        dve.tensor_copy(KT[s][:, 0:2, :], b).then_inc(d_empty, 1)
                    if st.name == "kpT":
                        b = bank(d).rearrange("p (k n) -> p k n", n=T)
                        dve.tensor_copy(kt(s, "S"), b).then_inc(d_empty, 1)
                    if st.name == "k3":
                        for j in range(2):
                            b = bank(d + j)[:, 0:4 * C].rearrange("p (m n) -> p m n", m=4)
                            dve.tensor_copy(KT[s][:, 4 * j:4 * j + 4, :], b).then_inc(d_empty, 1)
                    if st.name == "S":
                        b = bank(d)
                        if blk == "1":
                            if i == 0:
                                dve.wait_ge(masks_ready[s], nth(masks_ready[s], 1))
                            for h in range(2):
                                ins = dve.scalar_tensor_tensor(
                                    out=PB[s][0:C, i % RING, h * T:(h + 1) * T], in0=b[0:C, h * T:(h + 1) * T],
                                    scalar=0.0, in1=BAND[s][:, :], op0=ALU.max, op1=ALU.mult)
                            ins.then_inc(d_empty, 1)
                        else:
                            g, qt, half = units(blk)[i]
                            nh = 2 if blk == "S" and qt == 1 else 4
                            n = C if blk != "S" else T if qt == 1 else P
                            b = b[:, 0:nh * n].rearrange("p (h n) -> p h n", h=nh)
                            own(dve.tensor_reduce(NM[s][:, i % RING, 0:nh], b, AX.X, ALU.max, negate=True))
                            dve.tensor_tensor(PB[s][:, i % RING, 0:nh * n].rearrange("p (h n) -> p h n", h=nh), b,
                                              NM[s][:, i % RING, 0:nh, None].to_broadcast([P, nh, n]), ALU.add)\
                               .then_inc(d_empty, 1)
                    if st.name == "N":
                        dve.wait_ge(exp_done[s], it * N_EXP + 36 + i + 1)
                        own(dve.tensor_reduce(SUM[s][:, i % RING, 0, :],
                                              PB[s][:, i % RING, 0:4 * C].rearrange("p (h n) -> p h n", h=4), AX.X, ALU.add))
                        dve.reciprocal(REC[s][:, i % RING, 0, :], SUM[s][:, i % RING, 0, :]).then_inc(recip_ready[s], 1)
                    if st.name == "PV":
                        b = bank(d)[:, 0:T]
                        dve.tensor_copy(OT[s][:, i % 2, :], b).then_inc(d_empty, 1)
                    if st.name == "OTT":
                        b = bank(d)[:, 0:2 * P].rearrange("p (t h c) -> p t h c", t=2, h=4)
                        own(dve.tensor_scalar(SUM[s][:, i, :, :], b[:, :, :, HD], DEN1 if blk == "1" else DEN0, None,
                                              ALU.max))
                        own(dve.reciprocal(REC[s][:, i, :, :], SUM[s][:, i, :, :]))
                        dve.tensor_tensor(XN[s][:, :, i * 64:(i + 1) * 64].rearrange("p t (h c) -> p t h c", h=4),
                                          b[:, :, :, 0:HD], REC[s][:, i, :, :, None].to_broadcast([P, 2, 4, HD]),
                                          ALU.mult).then_inc(d_empty, 1)
                    if st.name in ("OUT", "OUT3"):
                        b = bank(d).rearrange("p (t c) -> p t c", t=2)
                        dve.tensor_tensor(X[s][:, :, :], b, X[s][:, :, :], ALU.add).then_inc(d_empty, 1)
                    if st.name == "f2":
                        dve.wait_ge(yb_ready[s], nth(yb_ready[s], 1))
                        b = bank(d).rearrange("p (t c) -> p t c", t=2)
                        dve.tensor_tensor(X[s][:, :, :], b, XN[s][:, :, :], ALU.add).then_inc(d_empty, 1)
                    if st.name == "outnorm":
                        dve.wait_ge(rstd_ready[s], it * 8 + 3)
                        for t in range(2):
                            ins = dve.scalar_tensor_tensor(out=X[s][:, t, :], in0=X[s][:, t, :], scalar=RSTD[s][:, t:t + 1],
                                                           in1=row("g_out"), op0=ALU.mult, op1=ALU.mult)
                        ins.then_inc(x_ready[s], 1)
                    if st.name == "ln":
                        src = FIND[{"S": ("OUT", "S"), "C": ("OUT", "C"), "F": ("f2", "F"), "3": ("OUT3", "3")}[blk]
                                   + (0, s)]
                        dve.wait_ge(d_empty, it * ND + src.d + 1 + RING)
                        for t in range(2):
                            own(dve.bn_stats(BN[s][:, t, :], X[s][:, t, :]))
                        dve.sem_inc(stats_done, 1)
                        for t in range(2):
                            ins = dve.bn_aggr(MV[s][:, t, :], BN[s][:, t, :])
                        ins.then_inc(moments[s], 1)
                        dve.wait_ge(rstd_ready[s], it * 8 + {"S": 5, "C": 6, "F": 7, "3": 8}[blk])
                        dve.wait_ge(moments[s], nth(moments[s], 4))
                        if blk == "3":
                            for t in range(2):
                                ins = dve.tensor_scalar(XN[s][:, t, :], X[s][:, t, :], MV[s][:, t, 0:1],
                                                        RSTD[s][:, t:t + 1], ALU.subtract, ALU.mult)
                            ins.then_inc(x_ready[s], 1)
                        else:
                            gain, shift = {"S": ("g1", "b1"), "C": ("g2", "b2"), "F": ("g3", "b3")}[blk]
                            for t in range(2):
                                own(dve.scalar_tensor_tensor(out=X[s][:, t, :], in0=X[s][:, t, :],
                                                             scalar=MV[s][:, t, 0:1], in1=row(gain),
                                                             op0=ALU.subtract, op1=ALU.mult))
                            for t in range(2):
                                ins = dve.scalar_tensor_tensor(out=X[s][:, t, :], in0=X[s][:, t, :],
                                                               scalar=RSTD[s][:, t:t + 1], in1=row(shift),
                                                               op0=ALU.mult, op1=ALU.add)
                            ins.then_inc(x_ready[s], 1)
                assert steps_in_pass[0] == VEC_N, steps_in_pass

        @block.tensor
        def _(pe):
            pe.wait_ge(weights_in, 16 * 9)
            pe.wait_ge(consts, 8)
            pe.wait_ge(vec, 6)
            with pe.Fori(0, B // 2) as it:
                nth = Nth(it)

                def by_a(name, blk, i, s, k=1):
                    return FIND[name, blk, i, s].a + k + RING

                def by_d(name, blk, i, s, k=1):
                    return FIND[name, blk, i, s].d + k + RING

                def bank_a(a, *data):
                    pe.wait_ge(a_empty, it * NA + max([a + 1, *data]))
                    return PA[:, a % RING, :]

                def bank_d(d, *data):
                    pe.wait_ge(d_empty, it * ND + max([d + 1, *data]))
                    return PD[:, d % RING, :]

                def after_a(*counts):
                    pe.wait_ge(a_empty, it * NA + max(counts))

                def after_d(count):
                    pe.wait_ge(d_empty, it * ND + count)

                def product(out, lhs, rhs):
                    for k in range(len(lhs)):
                        ins = pe.matmul(out, lhs[k], rhs[k], start=(k == 0), stop=(k == len(lhs) - 1))
                    return ins

                for st in ORDER:
                    s, blk, i, a, d = st.slot, st.block, st.i, st.a, st.d
                    if st.name == "cT":
                        pe.wait_ge(cn_ready[s], nth(cn_ready[s], 1))
                        b = bank_a(a)
                        for j in range(4):
                            src = CX[s][:, (j % 2) * P:(j % 2 + 1) * P] if j < 2 else CN[s][:, 0, (j % 2) * P:(j % 2 + 1) * P]
                            ins = pe.transpose(b[:, j * P:j * P + C], src, ID[0:C, 0:C])
                        ins.then_inc(a_full, 1)
                        b = bank_a(a + 1)
                        for j in range(2):
                            ins = pe.transpose(b[:, j * P:j * P + C], CN[s][:, 1, j * P:(j + 1) * P], ID[0:C, 0:C])
                        ins.then_inc(a_full, 1)
                    if st.name == "xT":
                        if blk in "01":
                            pe.wait_ge(xn_ready[s], nth(xn_ready[s], 2))
                            src = XN[s]
                        else:
                            src = X[s]
                            if blk == "S":
                                after_d(by_d("OUT", "1", 0, s))
                            else:
                                pe.wait_ge(x_ready[s], it * 5 + {"C": 2, "F": 3, "3": 4}[blk])
                        b = bank_a(a)
                        for k in range(2):
                            for t in range(2):
                                ins = pe.transpose(b[:, k * T + t * P:k * T + (t + 1) * P], src[:, t, k * P:(k + 1) * P], ID[:, :])
                        ins.then_inc(a_full, 1)
                    if st.name == "k":
                        after_a(by_a("cT", "0", 0, s, 1 if blk == "0" else 2))
                        b = bank_d(d)
                        c = 2 if blk == "0" else 4
                        for m in range(2):
                            ins = product(b[:, m * T:m * T + C], [WK[blk][:, k, m * P:(m + 1) * P] for k in range(2)],
                                          [CT[s][:, c + k, :] for k in range(2)])
                        ins.then_inc(d_full, 1)
                    if st.name == "v":
                        b = bank_a(a, by_a("cT", "0", 0, s, 1 if blk == "0" else 2))
                        c = 2 if blk == "0" else 4
                        product(b[0:C, 0:D], [CT[s][:, c + k, :] for k in range(2)],
                                [WV[blk][:, k, :] for k in range(2)]).then_inc(a_full, 1)
                    if st.name == "q":
                        b = bank_a(a, by_a("xT", blk, 0, s))
                        for m in range(2):
                            ins = product(b[:, m * T:(m + 1) * T], [WQ[blk][:, k, m * P:(m + 1) * P] for k in range(2)],
                                          [XT[s][:, k, :] for k in range(2)])
                        ins.then_inc(a_full, 1)
                    if st.name == "ckv":
                        for t in range(2):
                            b = bank_a(a + t)
                            product(b[0:C, 0:D], [CT[s][:, k, :] for k in range(2)],
                                    [WKVC[:, k, t * D:(t + 1) * D] for k in range(2)]).then_inc(a_full, 1)
                    if st.name == "qkv":
                        for t in range(2):
                            b = bank_a(a + t, by_a("xT", blk, 0, s))
                            product(b, [XT[s][:, k, t * P:(t + 1) * P] for k in range(2)],
                                    [WQKV[:, k, 0:2 * D] for k in range(2)]).then_inc(a_full, 1)
                        b = bank_a(a + 2)
                        for t in range(2):
                            ins = product(b[:, t * D:(t + 1) * D], [XT[s][:, k, t * P:(t + 1) * P] for k in range(2)],
                                          [WQKV[:, k, 2 * D:3 * D] for k in range(2)])
                        ins.then_inc(a_full, 1)
                    if st.name == "qc":
                        b = bank_a(a, by_a("xT", blk, 0, s))
                        for t in range(2):
                            ins = product(b[:, t * D:(t + 1) * D], [XT[s][:, k, t * P:(t + 1) * P] for k in range(2)],
                                          [WQC[:, k, :] for k in range(2)])
                        ins.then_inc(a_full, 1)
                    if st.name == "qpT" or st.name == "kpT":
                        if st.name == "qpT":
                            if blk == "S":
                                pe.wait_ge(self_in[s], it * 96 + 96)
                            else:
                                pe.wait_ge(qc_in[s], it * 32 + 32)
                        src, b = (XT[s], bank_a(a)) if st.name == "qpT" else (XN[s], bank_d(d))
                        for m in range(2):
                            for t in range(2):
                                ins = pe.transpose(b[:, m * T + t * P:m * T + (t + 1) * P], src[:, t, m * P:(m + 1) * P], ID[:, :])
                        ins.then_inc(a_full if st.name == "qpT" else d_full, 1)
                    if st.name == "ckT":
                        pe.wait_ge(ckv_in[s], it * 32 + 32)
                        b = bank_d(d)
                        for m in range(2):
                            ins = pe.transpose(b[:, m * T:m * T + C], KP[s][:, m * P:(m + 1) * P], ID[0:C, 0:C])
                        ins.then_inc(d_full, 1)
                    if st.name == "S":
                        g, qt, half = units(blk)[i]
                        if i == 0:
                            if blk == "3":
                                after_a(by_a("q3", "3", 0, s, 4))
                            else:
                                after_a(by_a("q" if blk in "01" else "qpT", blk, 0, s))
                        if i == 0 or units(blk)[i - 1][0] != g:
                            pe.wait_ge(km_ready[s], nth(km_ready[s], N_KM))
                        b = bank_d(d)
                        if blk in "0C":
                            if blk == "0" and i == 0:
                                pe.wait_ge(masks_ready[s], nth(masks_ready[s], 1))
                            ins = pe.matmul(b[:, 0:4 * C], QT[s][:, g // 2, qt * P:(qt + 1) * P], KM[s][:, g % 2, 0:4 * C],
                                            start=True, stop=(blk == "C"))
                            if blk == "0":
                                ins = pe.matmul(b[:, 0:4 * C].rearrange("p (h n) -> p h n", h=4), ONEB[:, :],
                                                BIAS[s][:, None, :].to_broadcast([1, 4, C]), start=False, stop=True)
                        elif blk == "1":
                            for j in range(2):
                                h = 2 * half + j
                                ins = pe.matmul(b[0:C, j * T:(j + 1) * T], KM[s][:, g % 2, h * C:(h + 1) * C],
                                                QT[s][:, g // 2, :], start=True, stop=True)
                        elif blk == "3":
                            for j in range(2):
                                m = 2 * g + j
                                ins = pe.matmul(b[:, j * 2 * C:(j + 1) * 2 * C], WIDE[s][:, m * T + qt * P:m * T + (qt + 1) * P],
                                                KM[s][:, g % 2, j * 2 * C:(j + 1) * 2 * C], start=True, stop=True)
                        else:
                            k = KM[s][:, g % 2, :].rearrange("p (h n) -> p h n", h=4)
                            q = QT[s][:, g // 2, qt * P:(qt + 1) * P]
                            if qt == 0:
                                pe.matmul(b.rearrange("p (h n) -> p h n", h=4), q, k[:, :, 0:P], start=True, stop=False)
                                ins = pe.matmul(b.rearrange("p (h n) -> p h n", h=4), IDB[:, :],
                                                CAUSAL[:, None, :].to_broadcast([P, 4, P]), start=False, stop=True)
                            else:
                                pe.matmul(b.rearrange("p (h n) -> p h n", h=2), q, k[:, 2 * half:2 * half + 2, :],
                                          start=True, stop=False)
                                ins = pe.matmul(b.rearrange("p (h n) -> p h n", h=2)[:, :, P:T], IDB[:, :],
                                                CAUSAL[:, None, :].to_broadcast([P, 2, P]), start=False, stop=True)
                        ins.then_inc(d_full, 1)
                    if st.name == "T":
                        g, qt, half = units(blk)[i]
                        if blk == "3":
                            pe.wait_ge(p_scaled[s], nth(p_scaled[s], N_L3))
                        else:
                            pe.wait_ge(exp_done[s], it * N_EXP + {"0": 0, "S": 16, "C": 28}[blk] + i + 1)
                        n = P if blk == "S" else C
                        b = bank_a(a)
                        for j in range(4):
                            ins = pe.transpose(b[0:n, j * P:(j + 1) * P], PB[s][:, i % RING, j * n:(j + 1) * n], ID[:, :])
                        ins.then_inc(a_full, 1)
                    if st.name in ("PV", "PV3"):
                        if blk == "1":
                            pe.wait_ge(exp_done[s], it * N_EXP + 8 + 2 * i + 2)
                            ready = [by_a("v", blk, 0, s)]
                        else:
                            ready = [by_a("T", blk, max(n for n, u in enumerate(units(blk)) if u[0] == i), s)]
                        if blk == "3":
                            b = bank_a(a, *ready)
                            for j in range(4):
                                h, r = 4 * i + j, 64 * (j % 2)
                                ins = pe.matmul(b[r:r + D3, (j // 2) * T:(j // 2 + 1) * T], V3[s][0:C, h // 8, (h % 8) * D3:(h % 8 + 1) * D3],
                                                PT[s][0:C, i % 2, j, 0:2, :].rearrange("p t n -> p (t n)"),
                                                start=True, stop=True)
                            ins.then_inc(a_full, 1)
                        else:
                            after_a(*ready)
                            b = bank_d(d)
                            for j in range(4):
                                h, r = 4 * i + j, 32 * j
                                p = PT[s][:, i % 2, j, :, :]
                                if blk == "S":
                                    pe.matmul(b[r:r + 32, 0:T], VS[s][:, 0, h, :], p[:, 0:2, :].rearrange("p t n -> p (t n)"),
                                              start=True, stop=False)
                                    ins = pe.matmul(b[r:r + 32, P:T], VS[s][:, 1, h, :], p[:, 2, :], start=False, stop=True)
                                else:
                                    ins = pe.matmul(b[r:r + 32, 0:T], VA[s][0:C, h, :],
                                                    p[0:C, 0:2, :].rearrange("p t n -> p (t n)"), start=True, stop=True)
                            ins.then_inc(d_full, 1)
                    if st.name == "OTT":
                        b = bank_d(d, by_d("PV", blk, i, s))
                        for t in range(2):
                            ins = pe.transpose(b[:, t * P:(t + 1) * P], OT[s][:, i % 2, t * P:(t + 1) * P], ID[:, :])
                        ins.then_inc(d_full, 1)
                    if st.name == "ONT":
                        after_d(by_d("OTT", blk, G - 1, s))
                        b = bank_a(a)
                        for k in range(2):
                            for t in range(2):
                                ins = pe.transpose(b[:, k * T + t * P:k * T + (t + 1) * P], XN[s][:, t, k * P:(k + 1) * P], ID[:, :])
                        ins.then_inc(a_full, 1)
                    if st.name == "OUT":
                        after_a(by_a("ONT", blk, 0, s))
                        b = bank_d(d)
                        for t in range(2):
                            ins = product(b[:, t * D:(t + 1) * D], [XT[s][:, k, t * P:(t + 1) * P] for k in range(2)],
                                          [WO[blk][:, k, :] for k in range(2)])
                        ins.then_inc(d_full, 1)
                    if st.name == "f1" or st.name == "q3":
                        w = W1 if st.name == "f1" else W3Q
                        for j in range(4):
                            b = bank_a(a + j, by_a("xT", blk, 0, s))
                            for m in range(2):
                                ins = product(b[:, m * T:(m + 1) * T],
                                              [w[:, k, (2 * j + m) * P:(2 * j + m + 1) * P] for k in range(2)],
                                              [XT[s][:, k, :] for k in range(2)])
                            ins.then_inc(a_full, 1)
                    if st.name == "f2" or st.name == "OUT3":
                        if st.name == "f2":
                            after_a(by_a("f1", "F", 0, s, 4))
                        else:
                            after_a(by_a("PV3", "3", G - 1, s))
                        w = W2 if st.name == "f2" else W3O
                        b = bank_d(d)
                        for t in range(2):
                            ins = product(b[:, t * D:(t + 1) * D],
                                          [WIDE[s][:, k * T + t * P:k * T + (t + 1) * P] for k in range(8)],
                                          [w[:, k, :] for k in range(8)])
                        ins.then_inc(d_full, 1)
                    if st.name == "k3":
                        for j in range(2):
                            b = bank_d(d + j)
                            for m in range(4):
                                mm = 4 * j + m
                                ins = product(b[:, m * C:(m + 1) * C], [W3K[:, k, mm * P:(mm + 1) * P] for k in range(2)],
                                              [CT[s][:, k, :] for k in range(2)])
                            ins.then_inc(d_full, 1)
                    if st.name == "v3":
                        for j in range(2):
                            b = bank_a(a + j)
                            product(b[0:C, :], [CT[s][:, k, :] for k in range(2)],
                                    [W3V[:, k, j * 512:(j + 1) * 512] for k in range(2)]).then_inc(a_full, 1)


POOL_N = 2 * (1 + 3 + 4)
VEC_N = 2 * (2 + 8 + 12 + 8 + 8 + 8 + 4 * 8 + 4 * 2 + 3 * 2)


def kernel(**inputs):
    import numpy as np
    import concourse.bacc as bacc
    from concourse.bass_utils import run_bass_kernel_spmd as run

    v = {k: np.asarray(a) for k, a in inputs.items()}

    def tiles(w):
        k, n = w.shape
        return w.reshape(k // P, P, n).transpose(1, 0, 2).reshape(P, -1)

    L0, L1, L2, L3 = "L0_xattn_", "L1_xattn_", "L2_xattn_", "L3_xattn_"
    parts = [v[L0 + "Wq"], v[L0 + "Wk"], v[L0 + "Wv"], v[L0 + "Wo"],
             v[L1 + "Wq"].T, v[L1 + "Wk"].T, v[L1 + "Wv"].T, v[L1 + "Wo"].T,
             v[L2 + "w_qkv"].T, v[L2 + "w_sa_out"].T, v[L2 + "wq"].T,
             np.concatenate([v[L2 + "wk"].T, v[L2 + "wv"].T], axis=1), v[L2 + "w_ca_out"].T,
             v[L2 + "w_ff1"].T, v[L2 + "w_ff2"].T, v[L3 + "W_Q"], v[L3 + "W_K"], v[L3 + "W_V"], v[L3 + "W_O"]]
    wall = np.ascontiguousarray(np.concatenate([tiles(w) for w in parts], axis=1))
    cols = np.ascontiguousarray(np.concatenate(
        [v[n].reshape(-1, P).T for n in (L0 + "g_q", L0 + "g_c", L1 + "gamma_q", L1 + "gamma_kv", L2 + "b_ff1")], axis=1))
    rows = np.stack([v[n] for n in (L0 + "g_out", L2 + "g1", L2 + "b1", L2 + "g2", L2 + "b2", L2 + "b_ff2", L2 + "g3",
                                    L2 + "b3")])
    arrays = {"x": v["x"], "ctx": v["ctx_1024"], "idx": v["itok_BxS_0_255"], "mask": v["mask_BxS2_bf1"].view(np.uint8),
              "wall": wall, "cols": cols, "rows": rows}
    arrays = {k: np.ascontiguousarray(a) for k, a in arrays.items()}

    nc = bacc.Bacc("TRN2", target_bir_lowering=False, num_devices=1, dynamic_dma_scratch_size=1024)
    args = [nc.dram_tensor(n, a.shape, mybir.dt.from_np(a.dtype), kind="ExternalInput").ap() for n, a in arrays.items()]
    scratch = nc.dram_tensor("scratch", (2, 5, T, D), F32, kind="Internal").ap()
    out = nc.dram_tensor("out", (B, T, D), F32, kind="ExternalOutput").ap()
    build(nc, *args, scratch, out)
    r = run(nc, [arrays], core_ids=[0])
    return r.results[0]["out"]
```

```python
from contextlib import ExitStack

import concourse.bass as bass
from concourse import mybir

F32 = mybir.dt.float32
BF16 = mybir.dt.bfloat16
U8 = mybir.dt.uint8
I32 = mybir.dt.int32
ALU = mybir.AluOpType
ACT = mybir.ActivationFunctionType
AX = mybir.AxisListType

B, T, D, C, H = 16, 256, 256, 120, 16
P = 128
KT_ = D // P
HD = D // H
F = 1024
D3 = 64
M3 = H * D3 // P
G = 4
RING = 4
BIG = float(2 ** 100)
EPS_OF = [1e-6, 1e-6, 1.1920929e-07, 1.1920929e-07, 1e-5, 1e-5]
DEN0, DEN1 = 1e-30, 1e-6

WIDTHS = [("q0", 512), ("k0", 512), ("v0", 512), ("o0", 512), ("q1", 512), ("k1", 512), ("v1", 512), ("o1", 512),
          ("qkv", 1536), ("so", 512), ("qc", 512), ("kvc", 1024), ("co", 512), ("f1", 2048), ("f2", 2048),
          ("Q3", 2048), ("K3", 2048), ("V3", 2048), ("O3", 2048)]
BLOCK_WIDTHS = [("0", 2048), ("1", 2048), ("S", 2048), ("C", 2048), ("F", 4096), ("3", 8192)]
WCOLS = sum(w for _, w in WIDTHS)
ROWS = ["g_out", "g1", "b1", "g2", "b2", "b_ff2", "g3", "b3"]

COST = {
    "loadc": (0, 0, "M3.0"), "masks": (0, 0, "V1.2"), "cnorm": (0, 0, "A0.5 G0.9"), "cscale": (0, 0, "A0.9"),
    "cT": (2, 0, "P0.9 A1.4"), "v": (1, 0, "P0.9 A0.6"), "k": (0, 1, "P0.9 V0.5"), "load": (0, 0, "M3.0"),
    "xnorm": (0, 0, "A0.9 G0.9"), "xscale": (0, 0, "A0.9"), "xT": (1, 0, "P0.6 A0.7"), "q": (1, 0, "P1.8 A0.6"),
    "km": (0, 0, "G1.1"), "S": (0, 1, "P0.9 V1.3"), "E": (0, 0, "A0.6"), "N": (0, 0, "V0.8 G1.1"),
    "T": (1, 0, "P0.5 A0.6"), "PV": (0, 1, "P0.6 V0.4"), "OTT": (0, 1, "P0.3 V0.5"), "ONT": (1, 0, "P0.5 A0.6"),
    "OUT": (0, 1, "P1.8 V0.7"), "outnorm": (0, 0, "A0.9 G0.9"), "outscale": (0, 0, "V0.9"),
    "ckv": (2, 0, "P1.8 A0.7"), "cout": (0, 0, "M2.5"), "cin": (0, 0, "M2.5"), "ckT": (0, 1, "P0.3 V0.4"),
    "qkv": (3, 0, "P5.4 A0.9"), "sout": (0, 0, "M2.5"), "sin": (0, 0, "M3.0"), "qpT": (1, 0, "P0.5 A0.6"),
    "kpT": (0, 1, "P0.5 V0.7"), "qc": (1, 0, "P1.8 A0.6"), "qout": (0, 0, "M2.5"), "qin": (0, 0, "M2.5"),
    "ln": (0, 0, "V1.1 G0.9"), "scale": (0, 0, "V1.5"), "f1": (4, 0, "P7.0 A0.9"), "f2": (0, 1, "P7.0 V0.7"),
    "k3": (0, 2, "P3.5 V0.7"), "v3": (2, 0, "P3.6 A0.6"), "q3": (4, 0, "P7.0 A0.6"), "PV3": (1, 0, "P0.9 A0.6"),
    "OUT3": (0, 1, "P7.0 V0.7"), "store": (0, 0, "M2.5"),
}


def units(block):
    if block == "S":
        return [(g, qt, half) for g in range(G) for qt, half in ((0, 0), (1, 0), (1, 1))]
    if block == "1":
        return [(g, 0, half) for g in range(G) for half in range(2)]
    return [(g, qt, 0) for g in range(G) for qt in range(2)]


def attention(block):
    todo, n = [], len(units(block))
    group = [u[0] for u in units(block)]
    late = 2 if block == "1" else 4 if block == "3" else 3
    ends = {max(i for i in range(n) if group[i] == g): g for g in range(G)}

    def values(g):
        todo.append(("PV3" if block == "3" else "PV", block, g))
        if block != "3" and g >= 1:
            todo.append(("OTT", block, g - 1))

    todo += [("km", block, 0), ("km", block, 1)]
    for i in range(n + late + 1):
        t = i - late
        if 0 <= t < n:
            if block != "1":
                todo.append(("T", block, t))
            elif t in ends:
                values(ends[t])
        if i < n:
            todo.append(("S", block, i))
            if i in ends and ends[i] + 2 < G:
                todo.append(("km", block, ends[i] + 2))
        if 0 <= i - 1 < n:
            todo.append(("E", block, i - 1))
        if block == "3" and 0 <= i - 2 < n:
            todo.append(("N", block, i - 2))
        if block != "1" and t - 1 in ends:
            values(ends[t - 1])
    if block == "3":
        return todo + [("OUT3", block, 0)]
    return todo + [("OTT", block, G - 1), ("ONT", block, 0), ("OUT", block, 0)]


def sequence_steps():
    context = [("loadc", "0", 0), ("masks", "0", 0), ("cnorm", "0", 0), ("cscale", "0", 0), ("cT", "0", 0), ("v", "0", 0),
               ("k", "0", 0)]
    s = [("load", "0", 0), ("xnorm", "0", 0), ("xscale", "0", 0), ("xT", "0", 0), ("q", "0", 0)]
    s += attention("0")
    s += [("outnorm", "0", 0), ("k", "1", 0), ("v", "1", 0), ("outscale", "0", 0), ("xnorm", "1", 0), ("ckv", "C", 0),
          ("cout", "C", 0), ("xscale", "1", 0), ("xT", "1", 0), ("q", "1", 0)]
    s += attention("1")
    s += [("cin", "C", 0), ("xT", "S", 0), ("qkv", "S", 0), ("sout", "S", 0), ("sin", "S", 0), ("qpT", "S", 0),
          ("kpT", "S", 0)]
    s += attention("S")
    s += [("ln", "S", 0), ("ckT", "C", 0), ("scale", "S", 0), ("xT", "C", 0), ("qc", "C", 0), ("qout", "C", 0),
          ("qin", "C", 0), ("v3", "3", 0), ("qpT", "C", 0)]
    s += attention("C")
    s += [("ln", "C", 0), ("scale", "C", 0), ("xT", "F", 0), ("f1", "F", 0), ("f2", "F", 0), ("ln", "F", 0),
          ("k3", "3", 0), ("scale", "F", 0), ("xT", "3", 0), ("q3", "3", 0)]
    s += attention("3")
    s += [("ln", "3", 0), ("scale", "3", 0), ("store", "3", 0)]
    return context, s


CONTEXT, MAIN = sequence_steps()
SEQUENCE = CONTEXT + MAIN
CUT = [MAIN.index(("q3", "3", 0)), MAIN.index(("xT", "S", 0))]
CONTEXT_AT = {"loadc": ("km", "3", 0), "masks": ("S", "3", 1), "cnorm": ("S", "3", 2), "cscale": ("S", "3", 5),
              "cT": ("ln", "3", 0), "v": ("scale", "3", 0), "k": ("scale", "3", 0)}


def needs(x):
    name, blk, i = x
    u, last = units(blk) if blk != "F" else [], G - 1
    of = {
        "loadc": [("v3", "3", 0)], "masks": [("loadc", "0", 0)], "cnorm": [("loadc", "0", 0)], "cscale": [("cnorm", "0", 0)],
        "cT": [("cscale", "0", 0)], "v": [("cT", "0", 0)], "k": [("cT", "0", 0)], "load": [("scale", "3", 0)],
        "xnorm": [("load", "0", 0) if blk == "0" else ("outscale", "0", 0)], "xscale": [("xnorm", blk, 0)],
        "xT": [{"0": ("xscale", "0", 0), "1": ("xscale", "1", 0), "S": ("OUT", "1", 0), "C": ("scale", "S", 0),
                "F": ("scale", "C", 0), "3": ("scale", "F", 0)}.get(blk)],
        "q": [("xT", blk, 0)], "qkv": [("xT", "S", 0)], "qc": [("xT", "C", 0)], "q3": [("xT", "3", 0)],
        "f1": [("xT", "F", 0)], "f2": [("f1", "F", 0)], "outnorm": [("OUT", "0", 0)], "outscale": [("outnorm", "0", 0)],
        "cout": [("ckv", "C", 0)], "cin": [("cout", "C", 0), ("OUT", "1", 0)], "sout": [("qkv", "S", 0)],
        "sin": [("sout", "S", 0)], "qout": [("qc", "C", 0)], "qin": [("qout", "C", 0)], "kpT": [("sin", "S", 0)],
        "qpT": [("sin", "S", 0) if blk == "S" else ("qin", "C", 0)], "ckT": [("cin", "C", 0)],
        "km": [("S", blk, max(n for n, v in enumerate(u) if v[0] == i - 2))] if i >= 2 and name == "km"
        else [({"S": "kpT", "C": "ckT", "3": "k3"}.get(blk, "k"), blk, 0)],
        "S": [({"3": "q3", "S": "qpT", "C": "qpT"}.get(blk, "q"), blk, 0)]
        + ([("km", blk, u[i][0])] if name == "S" else []),
        "E": [("S", blk, i)], "N": [("E", blk, i)], "T": [("N" if blk == "3" else "E", blk, i)],
        "PV": [("T", blk, max([n for n, v in enumerate(u) if v[0] == i], default=0))] if blk != "1" else [("E", blk, 2 * i + 1)],
        "PV3": [("T", blk, 2 * i + 1)], "OTT": [("PV", blk, i)], "ONT": [("OTT", blk, last)], "OUT": [("ONT", blk, 0)],
        "OUT3": [("PV3", "3", last)], "ln": [({"F": "f2", "3": "OUT3"}.get(blk, "OUT"), blk, 0)], "scale": [("ln", blk, 0)],
        "store": [("scale", "3", 0)],
    }
    return of.get(name, [])


class Step:

    def __init__(self, name, block, i, slot, back, a, d, v, g):
        self.name, self.block, self.i, self.slot, self.back = name, block, i, slot, back
        self.a, self.d, self.v, self.g = a, d, v, g


VEC_OWN = {"masks": 2, "S": 1, "N": 1, "OTT": 2, "ln": 2, "scale": 2, ("S", "1"): 0, ("scale", "3"): 0}
POOL_OWN = {"cnorm": 1, "xnorm": 1, "outnorm": 1, "ln": 1}
NA, ND = 2 * sum(COST[x[0]][0] for x in SEQUENCE), 2 * sum(COST[x[0]][1] for x in SEQUENCE)
assert NA % RING == 0 and ND % RING == 0


def slot_steps(s):
    steps = []
    for x in MAIN[CUT[s]:]:
        steps += [(c, s, 0) for c in CONTEXT if CONTEXT_AT[c[0]] == x]
        steps.append((x, s, 1))
    return steps + [(x, s, 0) for x in MAIN[:CUT[s]]]


def merged():
    lists, at = [slot_steps(0), slot_steps(1)], [0, 0]
    free, done = dict.fromkeys("PAVG", 0.0), {}
    emptied = {"A": [0.0] * RING, "V": [0.0] * RING}

    def run(x, s, commit):
        t = max([0.0] + [done.get((s, n), 0.0) for n in needs(x)])
        banks = COST[x[0]][:2]
        for ring, n in zip("AV", banks):
            if n:
                t = max(t, emptied[ring][-RING])
        begin = None
        for n, work in enumerate(COST[x[0]][2].split()):
            engine, took = work[0], float(work[1:])
            if engine != "M":
                t = max(t, free[engine])
            begin = t if begin is None else begin
            t += took
            if commit and engine != "M":
                free[engine] = t
            t += 0.2
        if commit:
            done[s, x] = t
            for ring, n in zip("AV", banks):
                emptied[ring] += [t] * n
        return begin

    order = []
    while at != [len(x) for x in lists]:
        left = [s for s in range(2) if at[s] < len(lists[s])]
        s = min(left, key=lambda s: (run(lists[s][at[s]][0], s, False), at[s] / len(lists[s])))
        run(lists[s][at[s]][0], s, True)
        order.append(lists[s][at[s]])
        at[s] += 1
    return order


def numbered(order, a, d, v, g):
    steps = []
    for (name, block, i), slot, back in order:
        steps.append(Step(name, block, i, slot, back, a, d, v, g))
        a, d = a + COST[name][0], d + COST[name][1]
        v += VEC_OWN.get((name, block), VEC_OWN.get(name, 0))
        g += POOL_OWN.get(name, 0)
    return steps, a, d, v, g


ORDER = merged()
FIRST, A1, D1, V1, G1 = numbered([x for x in ORDER if not x[2]], 0, 0, 0, 0)
LOOP, _, _, V2, G2 = numbered(ORDER, NA, ND, V1, G1)
NV, NG = V2 - V1, G2 - G1
LAST, _, _, _, _ = numbered([x for x in ORDER if x[2]], NA, ND, V1, G1)
PASSES = B // 2


def table(steps):
    found = {}
    for x in LOOP:
        if not x.back:
            found[x.name, x.block, x.i, x.slot, 1] = (x.a - NA, x.d - ND)
    for x in steps:
        found[x.name, x.block, x.i, x.slot, x.back] = (x.a, x.d)
    return found


SQUARE_NO = {("xnorm", "0"): 1, ("outnorm", "0"): 2, ("xnorm", "1"): 3}
LN_NO = {"S": 1, "C": 2, "F": 3, "3": 4}
GROUP_NO = {"0": 0, "1": 4, "S": 8, "C": 12, "3": 16}
EXP_NO = {"0": 0, "1": 8, "S": 16, "C": 28, "3": 36}


def build(nc, x, ctx, idx, mask, wall, cols, rows, scratch, out):
    with ExitStack() as stack:
        def sb(name, shape, dt=F32):
            return stack.enter_context(nc.sbuf_tensor(name, shape, dt))

        def two(name, shape, dt=F32):
            return [sb(f"{name}{s}", shape, dt) for s in range(2)]

        def sem(name):
            return stack.enter_context(nc.semaphore(name))

        def sem2(name):
            return [sem(f"{name}{s}") for s in range(2)]

        W = sb("W", [P, WCOLS])
        COLS = sb("COLS", [P, 16])
        ROW = sb("ROW", [P, len(ROWS), D])
        ID = sb("ID", [P, P])
        IDB = sb("IDB", [P, P], BF16)
        CAUSAL = sb("CAUSAL", [P, P], BF16)
        HM = sb("HM", [P, 8])
        HM3 = sb("HM3", [P, 2])
        TOP = sb("TOP", [P, P], BF16)
        ONEF = sb("ONEF", [P, H])
        NHALF = sb("NHALF", [P, 2])
        EPS = sb("EPS", [P, len(EPS_OF)])
        KEY = sb("KEY", [P, 1])
        KEYI = sb("KEYI", [P, 1], I32)

        X = two("X", [P, 2, D])
        XN = two("XN", [P, 2, D])
        XT = two("XT", [P, 2, T])
        QT = two("QT", [P, 2, T])
        KT = two("KT", [P, M3, C])
        CX = two("CX", [C, D])
        CN = two("CN", [C, 2, D])
        CT = two("CT", [P, 6, C])
        KM = two("KM", [P, 2, 4 * T])
        VA = two("VA", [P, H, 32])
        VS = two("VS", [P, 2, H, 32])
        V3 = [k[:, :, 512:1024] for k in KM]
        PB = two("PB", [P, RING, 512])
        PT = two("PT", [P, 2, 4, 3, P])
        OT = two("OT", [P, 2, T])
        WIDE = two("WIDE", [P, 8 * T])
        KP = two("KP", [C, D])
        NM = two("NM", [P, RING, 4])
        SUM = two("SUM", [P, RING, 2, 4])
        REC = two("REC", [P, RING, 2, 4])
        SS = two("SS", [P, 8])
        RSTD = two("RSTD", [P, 2])
        CRSTD = two("CRSTD", [P, 2])
        VAR = two("VAR", [P, 2])
        BN = two("BN", [P, 2, 6])
        MV = two("MV", [P, 2, 2])
        IDX = two("IDX", [C, T], I32)
        BAND = two("BAND", [C, T])
        MROW = two("MROW", [1, C], U8)
        MCOL = two("MCOL", [C, 1], U8)
        BIAS = two("BIAS", [P, C], BF16)
        MASK = two("MASK", [C, 1])

        PA = stack.enter_context(nc.psum_tensor("PA", [P, RING, 512], F32))
        PD = stack.enter_context(nc.psum_tensor("PD", [P, RING, 512], F32))

        weights_in = {blk: sem(f"weights_in_{blk}") for blk, _ in BLOCK_WIDTHS}
        vectors_in = sem("vectors_in")
        consts = sem("consts")
        a_full, d_full = sem("a_full"), sem("d_full")
        a_empty, d_empty = sem("a_empty"), sem("d_empty")
        ctx_loaded = sem2("ctx_loaded")
        x_loaded = sem2("x_loaded")
        masks_ready = sem2("masks_ready")
        csquare_done = sem2("csquare_done")
        square_done = sem2("square_done")
        crstd_ready = sem2("crstd_ready")
        rstd_ready = sem2("rstd_ready")
        cn_ready = sem2("cn_ready")
        xn_ready = sem2("xn_ready")
        km_ready = sem2("km_ready")
        exp_done = sem2("exp_done")
        recip_ready = sem2("recip_ready")
        p_scaled = sem2("p_scaled")
        moments = sem2("moments")
        x_ready = sem2("x_ready")
        yb_ready = sem2("yb_ready")
        bounced_out = sem2("bounced_out")
        self_in, ckv_in, qc_in = sem2("self_in"), sem2("ckv_in"), sem2("qc_in")
        stored = sem2("stored")
        sync_turns = sem("sync_turns")
        stats_done = sem("stats_done")
        vec = sem("vec")
        pool = sem("pool")
        vec_own = sem("vec_own")
        var_ready = sem("var_ready")

        offsets, at = {}, 0
        for name, w in WIDTHS:
            offsets[name] = (at, w)
            at += w

        def weight(name, width):
            o, w = offsets[name]
            return W[:, o:o + w].rearrange("p (k n) -> p k n", n=width)

        WQ = {"0": weight("q0", D), "1": weight("q1", D)}
        WK = {"0": weight("k0", D), "1": weight("k1", D)}
        WV = {"0": weight("v0", D), "1": weight("v1", D)}
        WO = {"0": weight("o0", D), "1": weight("o1", D), "S": weight("so", D), "C": weight("co", D)}
        WQKV, WQC, WKVC = weight("qkv", 3 * D), weight("qc", D), weight("kvc", 2 * D)
        W1, W2 = weight("f1", F), weight("f2", D)
        W3Q, W3K, W3V, W3O = weight("Q3", H * D3), weight("K3", H * D3), weight("V3", H * D3), weight("O3", D)

        def row(name):
            return ROW[:, ROWS.index(name), :]

        def kt(s, block):
            if block == "S":
                return KT[s][:, :, :].rearrange("p m n -> p (m n)")[:, 0:2 * T].rearrange("p (m n) -> p m n", n=T)
            return KT[s][:, :, :]

        def keys(block):
            return T if block == "S" else C

        def pv(s, block):
            return VS[s] if block == "S" else VA[s]

        def by_position(s, t, n):
            flat = scratch[s, t].rearrange("n c -> (n c)")[0:n * D]
            return flat.rearrange("(h n d) -> n h d", h=H, d=HD)

        block = stack.enter_context(nc.Block())

        N_KM, N_EXP, N_L3, N_RSTD = 5 * G, 8 * 4 + 12, 8, 7

        def three_passes(eng, steps_of, after_first=lambda: None):
            steps_of(FIRST, 0, [0, 0], 0)
            after_first()
            own = [eng.alloc_register(f"pass_of_slot{s}") for s in range(2)]
            with eng.Fori(0, PASSES - 1) as it:
                for r in own:
                    eng.reg_mov(r, it)
                steps_of(LOOP, it, [eng.snap(r) for r in own], 1)
            steps_of(LAST, PASSES - 1, [PASSES - 1] * 2, 1)

        @block.sync
        def _(sp):
            def steps_of(steps, it, turn, before):
                found = table(steps)

                def seq(per, k):
                    return turn[st.slot] * per + (k + (before - st.back) * per)

                for st in steps:
                    s = st.slot
                    n = it * 2 + (s + 2 * (before - st.back))
                    if st.name == "loadc":
                        if steps is LOOP:
                            sp.wait_ge(a_empty, it * NA + found["v3", "3", 0, s, 1][0] + 2 + RING)
                            sp.sem_inc(sync_turns, 1)
                        sp.dma_start(CX[s][:, :], ctx[bass.ds(n, 1)].rearrange("a n c -> (a n) c")).then_inc(ctx_loaded[s], 16)
                        sp.dma_start(MROW[s][:, :], mask[bass.ds(n, 1), :]).then_inc(ctx_loaded[s], 16)
                        sp.dma_start(MCOL[s][:, :], mask[bass.ds(n, 1), :].rearrange("a n -> n a")).then_inc(ctx_loaded[s], 16)
                        sp.dma_start(IDX[s][:, :], idx[bass.ds(n, 1), :].to_broadcast([C, T])).then_inc(ctx_loaded[s], 16)
                    if st.name == "load":
                        if steps is LOOP:
                            sp.wait_ge(x_ready[s], turn[s] * 5 + 5)
                            sp.sem_inc(sync_turns, 1)
                        sp.dma_start(X[s][:, :, :], x[bass.ds(n, 1)].rearrange("a (t p) c -> p (a t) c", p=P))\
                          .then_inc(x_loaded[s], 16)
                    if st.name == "cout":
                        sp.wait_ge(a_empty, it * NA + found["ckv", "C", 0, s, st.back][0] + 2 + RING)
                        for t in range(2):
                            sp.dma_start(scratch[s, 3 + t, 0:C, :], CN[s][:, t, :]).then_inc(bounced_out[s], 16)
                    if st.name == "cin":
                        sp.wait_ge(d_full, it * ND + found["OUT", "1", 0, s, st.back][1] + 1)
                        sp.sem_inc(sync_turns, 1)
                        sp.wait_ge(bounced_out[s], seq(96, 32))
                        sp.dma_start(KP[s][:, :].rearrange("p (h d) -> p h d", d=HD), by_position(s, 3, C))\
                          .then_inc(ckv_in[s], 16)
                        sp.dma_start(VA[s][0:C, :, 0:HD], by_position(s, 4, C)).then_inc(ckv_in[s], 16)
                    if st.name == "sout":
                        sp.wait_ge(a_empty, it * NA + found["qkv", "S", 0, s, st.back][0] + 3 + RING)
                        for t in range(3):
                            src = WIDE[s][:, 0:6 * D].rearrange("p (k t c) -> p k t c", k=2, t=3)[:, :, t, :]
                            sp.dma_start(scratch[s, t].rearrange("(k p) c -> p k c", p=P), src)\
                              .then_inc(bounced_out[s], 16)
                    if st.name == "sin":
                        sp.wait_ge(bounced_out[s], seq(96, 80))
                        for t, dst in ((0, XT[s]), (1, XN[s])):
                            for k in range(2):
                                sp.dma_start(dst[:, k, :].rearrange("p (h d) -> p h d", d=HD),
                                             by_position(s, t, T)[k * P:(k + 1) * P]).then_inc(self_in[s], 16)
                        for k in range(2):
                            sp.dma_start(VS[s][:, k, :, 0:HD], by_position(s, 2, T)[k * P:(k + 1) * P])\
                              .then_inc(self_in[s], 16)
                    if st.name == "qout":
                        sp.wait_ge(a_empty, it * NA + found["qc", "C", 0, s, st.back][0] + 1 + RING)
                        sp.dma_start(scratch[s, 0].rearrange("(k p) c -> p k c", p=P),
                                     WIDE[s][:, 0:2 * D].rearrange("p (k c) -> p k c", k=2)).then_inc(bounced_out[s], 16)
                    if st.name == "qin":
                        sp.wait_ge(bounced_out[s], seq(96, 96))
                        for k in range(2):
                            sp.dma_start(XT[s][:, k, :].rearrange("p (h d) -> p h d", d=HD),
                                         by_position(s, 0, T)[k * P:(k + 1) * P]).then_inc(qc_in[s], 16)
                    if st.name == "store":
                        sp.wait_ge(x_ready[s], seq(5, 5))
                        sp.sem_inc(sync_turns, 1)
                        sp.dma_start(out[bass.ds(n, 1)].rearrange("a (t p) c -> p (a t) c", p=P), XN[s][:, :, :])\
                          .then_inc(stored[s], 16)

            three_passes(sp, steps_of)
            for s in range(2):
                sp.wait_ge(stored[s], PASSES * 16)

        @block.gpsimd
        def _(gp):
            gp.memset(ID[:, :], 0.0).then_inc(pool, 1)
            gp.memset(TOP[:, :], 0.0)
            gp.memset(CAUSAL[:, :], 0.0).then_inc(pool, 1)
            gp.memset(HM[:, :], 1.0).then_inc(pool, 1)
            gp.memset(HM3[:, :], 1.0).then_inc(pool, 1)
            gp.iota(KEYI[:, :], pattern=[[0, 1]], base=0, channel_multiplier=-1).then_inc(pool, 1)
            gp.wait_ge(pool, 5)
            gp.affine_select(out=ID[:, :], in_=ID[:, :], compare_op=ALU.not_equal, fill=1.0, base=0,
                             pattern=[[-1, P]], channel_multiplier=1).then_inc(pool, 1)
            gp.affine_select(out=CAUSAL[:, :], in_=CAUSAL[:, :], compare_op=ALU.is_ge, fill=-BIG, base=0,
                             pattern=[[-1, P]], channel_multiplier=1).then_inc(consts, 1)
            gp.affine_select(out=HM[:, :], in_=HM[:, :], compare_op=ALU.is_ge, fill=0.0, base=0,
                             pattern=[[-HD, 8]], channel_multiplier=1).then_inc(pool, 1)
            gp.affine_select(out=HM3[:, :], in_=HM3[:, :], compare_op=ALU.is_ge, fill=0.0, base=0,
                             pattern=[[-D3, 2]], channel_multiplier=1).then_inc(pool, 1)
            gp.wait_ge(pool, 8)
            gp.affine_select(out=HM[:, :], in_=HM[:, :], compare_op=ALU.is_gt, fill=0.0, base=HD,
                             pattern=[[HD, 8]], channel_multiplier=-1).then_inc(consts, 1)
            gp.affine_select(out=HM3[:, :], in_=HM3[:, :], compare_op=ALU.is_gt, fill=0.0, base=D3,
                             pattern=[[D3, 2]], channel_multiplier=-1).then_inc(consts, 1)
            gp.tensor_copy(IDB[:, :], ID[:, :]).then_inc(consts, 1)
            gp.tensor_copy(KEY[:, :], KEYI[:, :]).then_inc(consts, 1)
            gp.memset(NHALF[:, :], -0.5).then_inc(consts, 1)
            for j, eps in enumerate(EPS_OF):
                gp.memset(EPS[:, j:j + 1], eps)
            gp.memset(TOP[0:1, :], 1.0).then_inc(consts, 1)
            gp.memset(ONEF[:, :], 1.0).then_inc(consts, 1)
            gp.wait_ge(consts, 8)
            def steps_of(steps, it, turn, before):
                found = table(steps)

                def seq(per, k):
                    return turn[st.slot] * per + (k + (before - st.back) * per)


                def rstd(s, n, src, eps, dst, ready):
                    w = src.shape[-1]
                    gp.tensor_tensor(VAR[s][0:n, 0:w], src, EPS[0:n, eps:eps + w], ALU.add).then_inc(var_ready, 1)
                    gp.wait_ge(var_ready, it * NG + st.g + 1)
                    gp.tensor_tensor(dst[0:n, 0:w], VAR[s][0:n, 0:w], NHALF[0:n, 0:w], ALU.pow).then_inc(ready, 1)

                for st in steps:
                    s, blk, i = st.slot, st.block, st.i
                    if st.name == "cnorm":
                        gp.wait_ge(csquare_done[s], seq(1, 1))
                        rstd(s, C, SS[s][0:C, 0:1].to_broadcast([C, 2]), 1, CRSTD[s], crstd_ready[s])
                    if st.name == "xnorm":
                        gp.wait_ge(square_done[s], seq(3, SQUARE_NO[st.name, blk]))
                        rstd(s, P, SS[s][:, 2:4], 0 if blk == "0" else 2, RSTD[s], rstd_ready[s])
                    if st.name == "outnorm":
                        gp.wait_ge(square_done[s], seq(3, SQUARE_NO[st.name, blk]))
                        rstd(s, P, SS[s][:, 2:4], 0, RSTD[s], rstd_ready[s])
                    if st.name == "ln":
                        gp.wait_ge(moments[s], seq(4, LN_NO[blk]))
                        rstd(s, P, MV[s][:, :, 1:2].rearrange("p a b -> p (a b)"), 4, RSTD[s],
                             rstd_ready[s])
                    if st.name == "scale" and blk == "C":
                        gp.wait_ge(x_ready[s], seq(5, 3))
                        gp.tensor_tensor(XN[s][:, :, :], X[s][:, :, :],
                                         ROW[:, ROWS.index("b_ff2"):ROWS.index("b_ff2") + 1, :].to_broadcast([P, 2, D]),
                                         ALU.add).then_inc(yb_ready[s], 1)
                    if st.name == "km":
                        if i >= 2:
                            last = max(n for n, u in enumerate(units(blk)) if u[0] == i - 2)
                            gp.wait_ge(d_full, it * ND + found["S", blk, last, s, st.back][1] + 1)
                        if i == 0:
                            src = found[{"0": "k", "1": "k", "S": "kpT", "C": "ckT", "3": "k3"}[blk], blk, 0, s, st.back][1]
                            gp.wait_ge(d_empty, it * ND + src + (2 if blk == "3" else 1) + RING)
                        n = keys(blk)
                        if blk == "3":
                            dst = KM[s][:, i % 2, 0:4 * n].rearrange("p (m h n) -> p m h n", m=2, h=2)
                            src = KT[s][:, 2 * i:2 * i + 2, None, :].to_broadcast([P, 2, 2, n])
                            sel = HM3[:, None, :, None].to_broadcast([P, 2, 2, n])
                        else:
                            dst = KM[s][:, i % 2, 0:4 * n].rearrange("p (h n) -> p h n", h=4)
                            src = kt(s, blk)[:, i // 2:i // 2 + 1, :].to_broadcast([P, 4, n])
                            sel = HM[:, (i % 2) * 4:(i % 2) * 4 + 4, None].to_broadcast([P, 4, n])
                        gp.tensor_tensor(dst, src, sel, ALU.mult).then_inc(km_ready[s], 1)
                    if st.name == "N":
                        gp.wait_ge(recip_ready[s], seq(N_L3, i + 1))
                        p = PB[s][:, i % RING, 0:4 * C].rearrange("p (h n) -> p h n", h=4)
                        gp.tensor_tensor(p, p, REC[s][:, i % RING, 0, :, None].to_broadcast([P, 4, C]), ALU.mult)\
                          .then_inc(p_scaled[s], 1)

            three_passes(gp, steps_of)

        @block.scalar
        def _(act):
            act.dma_start(COLS[:, :], cols).then_inc(vectors_in, 16)
            at = 0
            for blk, width in BLOCK_WIDTHS:
                act.dma_start(W[:, at:at + width], wall[:, at:at + width]).then_inc(weights_in[blk], 16)
                at += width
                if blk == "0":
                    act.dma_start(ROW[:, :, :], rows.rearrange("(a r) c -> a r c", a=1).to_broadcast([P, len(ROWS), D]))\
                       .then_inc(vectors_in, 16)
            act.sem_inc(a_empty, RING)
            act.wait_ge(vectors_in, 32)
            act.wait_ge(consts, 8)
            act.wait_ge(vec, 6)

            def steps_of(steps, it, turn, before):
                found = table(steps)

                def seq(per, k):
                    return turn[st.slot] * per + (k + (before - st.back) * per)


                def bank(a):
                    act.wait_ge(a_full, it * NA + a + 1)
                    return PA[:, a % RING, :]

                for st in steps:
                    s, blk, i, a = st.slot, st.block, st.i, st.a
                    if st.name == "cnorm":
                        act.wait_ge(ctx_loaded[s], seq(64, 64))
                        act.activation(CN[s][:, 0, :], CX[s][:, :], ACT.Square, scale=1 / 16, accum_out=SS[s][0:C, 0:1])\
                           .then_inc(csquare_done[s], 1)
                    if st.name == "cscale":
                        act.wait_ge(crstd_ready[s], seq(1, 1))
                        act.activation(CN[s][:, 0, :], CX[s][:, :], ACT.Copy, scale=CRSTD[s][0:C, 0:1])
                        act.activation(CN[s][:, 1, :], CX[s][:, :], ACT.Copy, scale=CRSTD[s][0:C, 1:2])\
                           .then_inc(cn_ready[s], 1)
                    if st.name == "cT":
                        b = bank(a).rearrange("p (j n) -> p j n", n=P)
                        act.activation(CT[s][:, 0:2, :], b[:, 0:2, 0:C], ACT.Copy)
                        for k in range(2):
                            ins = act.activation(CT[s][:, 2 + k, :], b[:, 2 + k, 0:C], ACT.Copy, scale=COLS[:, 2 + k:3 + k])
                        ins.then_inc(a_empty, 1)
                        b = bank(a + 1).rearrange("p (j n) -> p j n", n=P)
                        for k in range(2):
                            ins = act.activation(CT[s][:, 4 + k, :], b[:, k, 0:C], ACT.Copy, scale=COLS[:, 6 + k:7 + k])
                        ins.then_inc(a_empty, 1)
                    if st.name == "xT":
                        b = bank(a).rearrange("p (k n) -> p k n", n=T)
                        if blk in "01":
                            c = 0 if blk == "0" else 4
                            for k in range(2):
                                ins = act.activation(XT[s][:, k, :], b[:, k, :], ACT.Copy, scale=COLS[:, c + k:c + k + 1])
                            ins.then_inc(a_empty, 1)
                        else:
                            act.activation(XT[s][:, :, :], b, ACT.Copy).then_inc(a_empty, 1)
                    if st.name == "q" or st.name == "qpT":
                        b = bank(a).rearrange("p (k n) -> p k n", n=T)
                        act.activation(QT[s][:, :, :], b, ACT.Copy).then_inc(a_empty, 1)
                    if st.name == "ONT":
                        b = bank(a).rearrange("p (k n) -> p k n", n=T)
                        act.activation(XT[s][:, :, :], b, ACT.Copy).then_inc(a_empty, 1)
                    if st.name == "v":
                        b = bank(a)[0:C, 0:D].rearrange("p (h d) -> p h d", d=HD)
                        if blk == "0":
                            act.wait_ge(masks_ready[s], seq(1, 1))
                            act.activation(VA[s][0:C, :, HD], ONEF[0:C, :], ACT.Copy, scale=MASK[s][:, 0:1])
                            act.activation(VA[s][0:C, :, 0:HD], b, ACT.Copy, scale=MASK[s][:, 0:1]).then_inc(a_empty, 1)
                        else:
                            act.activation(VA[s][0:C, :, HD], ONEF[0:C, :], ACT.Copy)
                            act.activation(VA[s][0:C, :, 0:HD], b, ACT.Copy).then_inc(a_empty, 1)
                    if st.name == "v3":
                        for j in range(2):
                            b = bank(a + j)
                            act.activation(V3[s][0:C, j, :], b[0:C, :], ACT.Copy).then_inc(a_empty, 1)
                    if st.name == "ckv":
                        for t in range(2):
                            b = bank(a + t)[0:C, 0:D]
                            act.activation(CN[s][:, t, :], b, ACT.Copy).then_inc(a_empty, 1)
                    if st.name == "qkv":
                        w = WIDE[s][:, 0:6 * D].rearrange("p (k c) -> p k c", k=2)
                        for t in range(2):
                            b = bank(a + t)
                            act.activation(w[:, t, 0:2 * D], b, ACT.Copy).then_inc(a_empty, 1)
                        b = bank(a + 2).rearrange("p (k c) -> p k c", k=2)
                        act.activation(w[:, :, 2 * D:3 * D], b, ACT.Copy).then_inc(a_empty, 1)
                    if st.name == "qc":
                        b = bank(a)
                        act.activation(WIDE[s][:, 0:2 * D], b, ACT.Copy).then_inc(a_empty, 1)
                    if st.name == "f1":
                        for j in range(4):
                            b = bank(a + j).rearrange("p (k n) -> p k n", n=T)
                            for k in range(2):
                                m = 2 * j + k
                                ins = act.activation(WIDE[s][:, m * T:(m + 1) * T], b[:, k, :], ACT.Relu,
                                                     bias=COLS[:, 8 + m:9 + m])
                            ins.then_inc(a_empty, 1)
                    if st.name == "q3":
                        for j in range(4):
                            b = bank(a + j)
                            act.activation(WIDE[s][:, j * 512:(j + 1) * 512], b, ACT.Copy).then_inc(a_empty, 1)
                    if st.name == "PV3":
                        b = bank(a)
                        act.activation(WIDE[s][:, i * 512:(i + 1) * 512], b, ACT.Copy).then_inc(a_empty, 1)
                    if st.name == "E":
                        g, qt, half = units(blk)[i]
                        act.wait_ge(d_empty, it * ND + found["S", blk, i, s, st.back][1] + 1 + RING)
                        n = 4 * C if blk in "0C3" else 512
                        p = PB[s][:, i % RING, 0:n]
                        if blk == "1":
                            dst = PT[s][0:C, g % 2, 2 * half:2 * half + 2, 0:2, :].rearrange("p h q n -> p h (q n)")
                            act.activation(dst, PB[s][0:C, i % RING, :].rearrange("p (h n) -> p h n", h=2), ACT.Square,
                                           scale=0.25).then_inc(exp_done[s], 1)
                        else:
                            act.activation(p, p, ACT.Exp, scale=0.125 if blk == "3" else 0.25).then_inc(exp_done[s], 1)
                    if st.name == "T":
                        g, qt, half = units(blk)[i]
                        n = P if blk == "S" else C
                        b = bank(a)[0:n, :]
                        if blk == "S" and qt == 1:
                            dst = PT[s][:, g % 2, 2 * half:2 * half + 2, 1:3, :].rearrange("p h t n -> p h (t n)")
                            act.activation(dst, b.rearrange("p (h n) -> p h n", h=2), ACT.Copy).then_inc(a_empty, 1)
                        else:
                            act.activation(PT[s][0:n, g % 2, :, qt, :], b.rearrange("p (h n) -> p h n", h=4), ACT.Copy)\
                               .then_inc(a_empty, 1)
                    if st.name in ("xnorm", "outnorm"):
                        if st.name == "outnorm":
                            act.wait_ge(d_empty, it * ND + found["OUT", "0", 0, s, st.back][1] + 1 + RING)
                        elif blk == "1":
                            act.wait_ge(x_ready[s], seq(5, 1))
                        else:
                            act.wait_ge(x_loaded[s], seq(16, 16))
                            if steps is LOOP:
                                act.wait_ge(stored[s], turn[s] * 16 + 16)
                        for t in range(2):
                            ins = act.activation(XN[s][:, t, :], X[s][:, t, :], ACT.Square, scale=1 / 16,
                                                 accum_out=SS[s][:, 2 + t:3 + t])
                        ins.then_inc(square_done[s], 1)
                    if st.name == "xscale":
                        act.wait_ge(rstd_ready[s], seq(N_RSTD, SQUARE_NO["xnorm", blk]))
                        for t in range(2):
                            ins = act.activation(XN[s][:, t, :], X[s][:, t, :], ACT.Copy, scale=RSTD[s][:, t:t + 1])
                        ins.then_inc(xn_ready[s], 1)

            def after_first():
                act.wait_ge(a_empty, A1 + RING)
                act.sem_inc(a_empty, NA - A1)

            three_passes(act, steps_of, after_first)

        @block.vector
        def _(dve):
            dve.sem_inc(d_empty, RING)
            for s in range(2):
                dve.memset(VA[s][:, :, :], 0.0).then_inc(vec, 1)
                dve.memset(BIAS[s][:, :], 0.0)
                dve.memset(VS[s][:, :, :, :], 0.0).then_inc(vec, 1)
            dve.wait_ge(vectors_in, 32)
            dve.wait_ge(consts, 8)
            dve.wait_ge(vec, 4)
            for s in range(2):
                dve.memset(VS[s][:, :, :, HD], 1.0).then_inc(vec, 1)

            def steps_of(steps, it, turn, before):
                found = table(steps)

                def seq(per, k):
                    return turn[st.slot] * per + (k + (before - st.back) * per)


                def own(ins):
                    count[0] += 1
                    ins.then_inc(vec_own, 1)
                    dve.wait_ge(vec_own, it * NV + count[0])

                def bank(d):
                    dve.wait_ge(d_full, it * ND + d + 1)
                    return PD[:, d % RING, :]

                for st in steps:
                    s, blk, i, d = st.slot, st.block, st.i, st.d
                    count = [st.v]
                    if st.name == "masks":
                        dve.wait_ge(ctx_loaded[s], seq(64, 64))
                        dve.tensor_scalar(BIAS[s][0:1, :], MROW[s][:, :], -1.0, BIG, ALU.add, ALU.mult)
                        dve.tensor_copy(MASK[s][:, :], MCOL[s][:, :])
                        own(dve.tensor_scalar(BAND[s][:, :], IDX[s][:, :], KEY[0:C, 0:1], None, ALU.add))
                        own(dve.tensor_tensor(BAND[s][:, :], BAND[s][:, :], BAND[s][:, :], ALU.mult))
                        dve.tensor_scalar(BAND[s][:, :], BAND[s][:, :], 1.0, None, ALU.is_le).then_inc(masks_ready[s], 1)
                    if st.name == "k" or st.name == "ckT":
                        b = bank(d).rearrange("p (k n) -> p k n", n=T)[:, :, 0:C]
                        dve.tensor_copy(KT[s][:, 0:2, :], b).then_inc(d_empty, 1)
                    if st.name == "kpT":
                        b = bank(d).rearrange("p (k n) -> p k n", n=T)
                        dve.tensor_copy(kt(s, "S"), b).then_inc(d_empty, 1)
                    if st.name == "k3":
                        for j in range(2):
                            b = bank(d + j)[:, 0:4 * C].rearrange("p (m n) -> p m n", m=4)
                            dve.tensor_copy(KT[s][:, 4 * j:4 * j + 4, :], b).then_inc(d_empty, 1)
                    if st.name == "S":
                        b = bank(d)
                        if blk == "1":
                            if i == 0:
                                dve.wait_ge(masks_ready[s], seq(1, 1))
                            for h in range(2):
                                ins = dve.scalar_tensor_tensor(
                                    out=PB[s][0:C, i % RING, h * T:(h + 1) * T], in0=b[0:C, h * T:(h + 1) * T],
                                    scalar=0.0, in1=BAND[s][:, :], op0=ALU.max, op1=ALU.mult)
                            ins.then_inc(d_empty, 1)
                        else:
                            g, qt, half = units(blk)[i]
                            nh = 2 if blk == "S" and qt == 1 else 4
                            n = C if blk != "S" else T if qt == 1 else P
                            b = b[:, 0:nh * n].rearrange("p (h n) -> p h n", h=nh)
                            own(dve.tensor_reduce(NM[s][:, i % RING, 0:nh], b, AX.X, ALU.max, negate=True))
                            dve.tensor_tensor(PB[s][:, i % RING, 0:nh * n].rearrange("p (h n) -> p h n", h=nh), b,
                                              NM[s][:, i % RING, 0:nh, None].to_broadcast([P, nh, n]), ALU.add)\
                               .then_inc(d_empty, 1)
                    if st.name == "N":
                        dve.wait_ge(exp_done[s], seq(N_EXP, 36 + i + 1))
                        own(dve.tensor_reduce(SUM[s][:, i % RING, 0, :],
                                              PB[s][:, i % RING, 0:4 * C].rearrange("p (h n) -> p h n", h=4), AX.X, ALU.add))
                        dve.reciprocal(REC[s][:, i % RING, 0, :], SUM[s][:, i % RING, 0, :]).then_inc(recip_ready[s], 1)
                    if st.name == "PV":
                        b = bank(d)[:, 0:T]
                        dve.tensor_copy(OT[s][:, i % 2, :], b).then_inc(d_empty, 1)
                    if st.name == "OTT":
                        b = bank(d)[:, 0:2 * P].rearrange("p (t h c) -> p t h c", t=2, h=4)
                        own(dve.tensor_scalar(SUM[s][:, i, :, :], b[:, :, :, HD], DEN1 if blk == "1" else DEN0, None,
                                              ALU.max))
                        own(dve.reciprocal(REC[s][:, i, :, :], SUM[s][:, i, :, :]))
                        dve.tensor_tensor(XN[s][:, :, i * 64:(i + 1) * 64].rearrange("p t (h c) -> p t h c", h=4),
                                          b[:, :, :, 0:HD], REC[s][:, i, :, :, None].to_broadcast([P, 2, 4, HD]),
                                          ALU.mult).then_inc(d_empty, 1)
                    if st.name in ("OUT", "OUT3"):
                        b = bank(d).rearrange("p (t c) -> p t c", t=2)
                        dve.tensor_tensor(X[s][:, :, :], b, X[s][:, :, :], ALU.add).then_inc(d_empty, 1)
                    if st.name == "f2":
                        dve.wait_ge(yb_ready[s], seq(1, 1))
                        b = bank(d).rearrange("p (t c) -> p t c", t=2)
                        dve.tensor_tensor(X[s][:, :, :], b, XN[s][:, :, :], ALU.add).then_inc(d_empty, 1)
                    if st.name == "outscale":
                        dve.wait_ge(rstd_ready[s], seq(N_RSTD, 2))
                        for t in range(2):
                            ins = dve.scalar_tensor_tensor(out=X[s][:, t, :], in0=X[s][:, t, :], scalar=RSTD[s][:, t:t + 1],
                                                           in1=row("g_out"), op0=ALU.mult, op1=ALU.mult)
                        ins.then_inc(x_ready[s], 1)
                    if st.name == "ln":
                        src = found[{"S": "OUT", "C": "OUT", "F": "f2", "3": "OUT3"}[blk], blk, 0, s, st.back][1]
                        dve.wait_ge(d_empty, it * ND + src + 1 + RING)
                        for t in range(2):
                            own(dve.bn_stats(BN[s][:, t, :], X[s][:, t, :]))
                        dve.sem_inc(stats_done, 1)
                        for t in range(2):
                            ins = dve.bn_aggr(MV[s][:, t, :], BN[s][:, t, :])
                        ins.then_inc(moments[s], 1)
                    if st.name == "scale":
                        dve.wait_ge(rstd_ready[s], seq(N_RSTD, 3 + LN_NO[blk]))
                        dve.wait_ge(moments[s], seq(4, LN_NO[blk]))
                        if blk == "3":
                            for t in range(2):
                                ins = dve.tensor_scalar(XN[s][:, t, :], X[s][:, t, :], MV[s][:, t, 0:1],
                                                        RSTD[s][:, t:t + 1], ALU.subtract, ALU.mult)
                            ins.then_inc(x_ready[s], 1)
                        else:
                            gain, shift = {"S": ("g1", "b1"), "C": ("g2", "b2"), "F": ("g3", "b3")}[blk]
                            for t in range(2):
                                own(dve.scalar_tensor_tensor(out=X[s][:, t, :], in0=X[s][:, t, :],
                                                             scalar=MV[s][:, t, 0:1], in1=row(gain),
                                                             op0=ALU.subtract, op1=ALU.mult))
                            for t in range(2):
                                ins = dve.scalar_tensor_tensor(out=X[s][:, t, :], in0=X[s][:, t, :],
                                                               scalar=RSTD[s][:, t:t + 1], in1=row(shift),
                                                               op0=ALU.mult, op1=ALU.add)
                            ins.then_inc(x_ready[s], 1)

            def after_first():
                dve.wait_ge(d_empty, D1 + RING)
                dve.sem_inc(d_empty, ND - D1)

            three_passes(dve, steps_of, after_first)

        @block.tensor
        def _(pe):
            pe.wait_ge(consts, 8)
            pe.wait_ge(vec, 6)

            def steps_of(steps, it, turn, before):
                found = table(steps)

                def seq(per, k):
                    return turn[st.slot] * per + (k + (before - st.back) * per)


                def by_a(name, blk, i, s, k=1):
                    return found[name, blk, i, s, st.back][0] + k + RING

                def by_d(name, blk, i, s, k=1):
                    return found[name, blk, i, s, st.back][1] + k + RING

                def bank_a(a, *data):
                    pe.wait_ge(a_empty, it * NA + max([a + 1, *data]))
                    return PA[:, a % RING, :]

                def bank_d(d, *data):
                    pe.wait_ge(d_empty, it * ND + max([d + 1, *data]))
                    return PD[:, d % RING, :]

                def after_a(*counts):
                    pe.wait_ge(a_empty, it * NA + max(counts))

                def after_d(count):
                    pe.wait_ge(d_empty, it * ND + count)

                def product(out, lhs, rhs):
                    for k in range(len(lhs)):
                        ins = pe.matmul(out, lhs[k], rhs[k], start=(k == 0), stop=(k == len(lhs) - 1))
                    return ins

                waited = set()
                for st in steps:
                    s, blk, i, a, d = st.slot, st.block, st.i, st.a, st.d
                    if steps is FIRST and blk not in waited:
                        pe.wait_ge(weights_in[blk], 16)
                        waited.add(blk)
                    if st.name == "cT":
                        pe.wait_ge(cn_ready[s], seq(1, 1))
                        b = bank_a(a)
                        for j in range(4):
                            src = CX[s][:, (j % 2) * P:(j % 2 + 1) * P] if j < 2 else CN[s][:, 0, (j % 2) * P:(j % 2 + 1) * P]
                            ins = pe.transpose(b[:, j * P:j * P + C], src, ID[0:C, 0:C])
                        ins.then_inc(a_full, 1)
                        b = bank_a(a + 1)
                        for j in range(2):
                            ins = pe.transpose(b[:, j * P:j * P + C], CN[s][:, 1, j * P:(j + 1) * P], ID[0:C, 0:C])
                        ins.then_inc(a_full, 1)
                    if st.name == "xT":
                        if blk in "01":
                            pe.wait_ge(xn_ready[s], seq(2, 1 + (blk == "1")))
                            src = XN[s]
                        else:
                            src = X[s]
                            if blk == "S":
                                after_d(by_d("OUT", "1", 0, s))
                            else:
                                pe.wait_ge(x_ready[s], seq(5, {"C": 2, "F": 3, "3": 4}[blk]))
                        b = bank_a(a)
                        for k in range(2):
                            for t in range(2):
                                ins = pe.transpose(b[:, k * T + t * P:k * T + (t + 1) * P], src[:, t, k * P:(k + 1) * P], ID[:, :])
                        ins.then_inc(a_full, 1)
                    if st.name == "k":
                        after_a(by_a("cT", "0", 0, s, 1 if blk == "0" else 2))
                        b = bank_d(d)
                        c = 2 if blk == "0" else 4
                        for m in range(2):
                            ins = product(b[:, m * T:m * T + C], [WK[blk][:, k, m * P:(m + 1) * P] for k in range(2)],
                                          [CT[s][:, c + k, :] for k in range(2)])
                        ins.then_inc(d_full, 1)
                    if st.name == "v":
                        b = bank_a(a, by_a("cT", "0", 0, s, 1 if blk == "0" else 2))
                        c = 2 if blk == "0" else 4
                        product(b[0:C, 0:D], [CT[s][:, c + k, :] for k in range(2)],
                                [WV[blk][:, k, :] for k in range(2)]).then_inc(a_full, 1)
                    if st.name == "q":
                        b = bank_a(a, by_a("xT", blk, 0, s))
                        for m in range(2):
                            ins = product(b[:, m * T:(m + 1) * T], [WQ[blk][:, k, m * P:(m + 1) * P] for k in range(2)],
                                          [XT[s][:, k, :] for k in range(2)])
                        ins.then_inc(a_full, 1)
                    if st.name == "ckv":
                        for t in range(2):
                            b = bank_a(a + t)
                            product(b[0:C, 0:D], [CT[s][:, k, :] for k in range(2)],
                                    [WKVC[:, k, t * D:(t + 1) * D] for k in range(2)]).then_inc(a_full, 1)
                    if st.name == "qkv":
                        for t in range(2):
                            b = bank_a(a + t, by_a("xT", blk, 0, s))
                            product(b, [XT[s][:, k, t * P:(t + 1) * P] for k in range(2)],
                                    [WQKV[:, k, 0:2 * D] for k in range(2)]).then_inc(a_full, 1)
                        b = bank_a(a + 2)
                        for t in range(2):
                            ins = product(b[:, t * D:(t + 1) * D], [XT[s][:, k, t * P:(t + 1) * P] for k in range(2)],
                                          [WQKV[:, k, 2 * D:3 * D] for k in range(2)])
                        ins.then_inc(a_full, 1)
                    if st.name == "qc":
                        b = bank_a(a, by_a("xT", blk, 0, s))
                        for t in range(2):
                            ins = product(b[:, t * D:(t + 1) * D], [XT[s][:, k, t * P:(t + 1) * P] for k in range(2)],
                                          [WQC[:, k, :] for k in range(2)])
                        ins.then_inc(a_full, 1)
                    if st.name == "qpT" or st.name == "kpT":
                        if st.name == "qpT":
                            if blk == "S":
                                pe.wait_ge(self_in[s], seq(96, 96))
                            else:
                                pe.wait_ge(qc_in[s], seq(32, 32))
                        src, b = (XT[s], bank_a(a)) if st.name == "qpT" else (XN[s], bank_d(d))
                        for m in range(2):
                            for t in range(2):
                                ins = pe.transpose(b[:, m * T + t * P:m * T + (t + 1) * P], src[:, t, m * P:(m + 1) * P], ID[:, :])
                        ins.then_inc(a_full if st.name == "qpT" else d_full, 1)
                    if st.name == "ckT":
                        pe.wait_ge(ckv_in[s], seq(32, 32))
                        b = bank_d(d)
                        for m in range(2):
                            ins = pe.transpose(b[:, m * T:m * T + C], KP[s][:, m * P:(m + 1) * P], ID[0:C, 0:C])
                        ins.then_inc(d_full, 1)
                    if st.name == "S":
                        g, qt, half = units(blk)[i]
                        if i == 0:
                            if blk == "3":
                                after_a(by_a("q3", "3", 0, s, 4))
                            else:
                                after_a(by_a("q" if blk in "01" else "qpT", blk, 0, s))
                        if i == 0 or units(blk)[i - 1][0] != g:
                            pe.wait_ge(km_ready[s], seq(N_KM, GROUP_NO[blk] + g + 1))
                        b = bank_d(d)
                        if blk in "0C":
                            if blk == "0" and i == 0:
                                pe.wait_ge(masks_ready[s], seq(1, 1))
                            ins = pe.matmul(b[:, 0:4 * C], QT[s][:, g // 2, qt * P:(qt + 1) * P], KM[s][:, g % 2, 0:4 * C],
                                            start=True, stop=(blk == "C"))
                            if blk == "0":
                                ins = pe.matmul(b[:, 0:4 * C].rearrange("p (h n) -> p h n", h=4), TOP[:, :],
                                                BIAS[s][:, None, :].to_broadcast([P, 4, C]), start=False, stop=True)
                        elif blk == "1":
                            for j in range(2):
                                h = 2 * half + j
                                ins = pe.matmul(b[0:C, j * T:(j + 1) * T], KM[s][:, g % 2, h * C:(h + 1) * C],
                                                QT[s][:, g // 2, :], start=True, stop=True)
                        elif blk == "3":
                            for j in range(2):
                                m = 2 * g + j
                                ins = pe.matmul(b[:, j * 2 * C:(j + 1) * 2 * C], WIDE[s][:, m * T + qt * P:m * T + (qt + 1) * P],
                                                KM[s][:, g % 2, j * 2 * C:(j + 1) * 2 * C], start=True, stop=True)
                        else:
                            k = KM[s][:, g % 2, :].rearrange("p (h n) -> p h n", h=4)
                            q = QT[s][:, g // 2, qt * P:(qt + 1) * P]
                            if qt == 0:
                                pe.matmul(b.rearrange("p (h n) -> p h n", h=4), q, k[:, :, 0:P], start=True, stop=False)
                                ins = pe.matmul(b.rearrange("p (h n) -> p h n", h=4), IDB[:, :],
                                                CAUSAL[:, None, :].to_broadcast([P, 4, P]), start=False, stop=True)
                            else:
                                pe.matmul(b.rearrange("p (h n) -> p h n", h=2), q, k[:, 2 * half:2 * half + 2, :],
                                          start=True, stop=False)
                                ins = pe.matmul(b.rearrange("p (h n) -> p h n", h=2)[:, :, P:T], IDB[:, :],
                                                CAUSAL[:, None, :].to_broadcast([P, 2, P]), start=False, stop=True)
                        ins.then_inc(d_full, 1)
                    if st.name == "T":
                        g, qt, half = units(blk)[i]
                        if blk == "3":
                            pe.wait_ge(p_scaled[s], seq(N_L3, i + 1))
                        else:
                            pe.wait_ge(exp_done[s], seq(N_EXP, EXP_NO[blk] + i + 1))
                        n = P if blk == "S" else C
                        b = bank_a(a)
                        for j in range(4):
                            ins = pe.transpose(b[0:n, j * P:(j + 1) * P], PB[s][:, i % RING, j * n:(j + 1) * n], ID[:, :])
                        ins.then_inc(a_full, 1)
                    if st.name in ("PV", "PV3"):
                        if blk == "1":
                            pe.wait_ge(exp_done[s], seq(N_EXP, 8 + 2 * i + 2))
                            ready = [by_a("v", blk, 0, s)]
                        else:
                            ready = [by_a("T", blk, max(n for n, u in enumerate(units(blk)) if u[0] == i), s)]
                        if blk == "3":
                            b = bank_a(a, *ready)
                            for j in range(4):
                                h, r = 4 * i + j, 64 * (j % 2)
                                ins = pe.matmul(b[r:r + D3, (j // 2) * T:(j // 2 + 1) * T], V3[s][0:C, h // 8, (h % 8) * D3:(h % 8 + 1) * D3],
                                                PT[s][0:C, i % 2, j, 0:2, :].rearrange("p t n -> p (t n)"),
                                                start=True, stop=True)
                            ins.then_inc(a_full, 1)
                        else:
                            after_a(*ready)
                            b = bank_d(d)
                            for j in range(4):
                                h, r = 4 * i + j, 32 * j
                                p = PT[s][:, i % 2, j, :, :]
                                if blk == "S":
                                    pe.matmul(b[r:r + 32, 0:T], VS[s][:, 0, h, :], p[:, 0:2, :].rearrange("p t n -> p (t n)"),
                                              start=True, stop=False)
                                    ins = pe.matmul(b[r:r + 32, P:T], VS[s][:, 1, h, :], p[:, 2, :], start=False, stop=True)
                                else:
                                    ins = pe.matmul(b[r:r + 32, 0:T], VA[s][0:C, h, :],
                                                    p[0:C, 0:2, :].rearrange("p t n -> p (t n)"), start=True, stop=True)
                            ins.then_inc(d_full, 1)
                    if st.name == "OTT":
                        b = bank_d(d, by_d("PV", blk, i, s))
                        for t in range(2):
                            ins = pe.transpose(b[:, t * P:(t + 1) * P], OT[s][:, i % 2, t * P:(t + 1) * P], ID[:, :])
                        ins.then_inc(d_full, 1)
                    if st.name == "ONT":
                        after_d(by_d("OTT", blk, G - 1, s))
                        b = bank_a(a)
                        for k in range(2):
                            for t in range(2):
                                ins = pe.transpose(b[:, k * T + t * P:k * T + (t + 1) * P], XN[s][:, t, k * P:(k + 1) * P], ID[:, :])
                        ins.then_inc(a_full, 1)
                    if st.name == "OUT":
                        after_a(by_a("ONT", blk, 0, s))
                        b = bank_d(d)
                        for t in range(2):
                            ins = product(b[:, t * D:(t + 1) * D], [XT[s][:, k, t * P:(t + 1) * P] for k in range(2)],
                                          [WO[blk][:, k, :] for k in range(2)])
                        ins.then_inc(d_full, 1)
                    if st.name == "f1" or st.name == "q3":
                        w = W1 if st.name == "f1" else W3Q
                        for j in range(4):
                            b = bank_a(a + j, by_a("xT", blk, 0, s))
                            for m in range(2):
                                ins = product(b[:, m * T:(m + 1) * T],
                                              [w[:, k, (2 * j + m) * P:(2 * j + m + 1) * P] for k in range(2)],
                                              [XT[s][:, k, :] for k in range(2)])
                            ins.then_inc(a_full, 1)
                    if st.name == "f2" or st.name == "OUT3":
                        if st.name == "f2":
                            after_a(by_a("f1", "F", 0, s, 4))
                        else:
                            after_a(by_a("PV3", "3", G - 1, s))
                        w = W2 if st.name == "f2" else W3O
                        b = bank_d(d)
                        for t in range(2):
                            ins = product(b[:, t * D:(t + 1) * D],
                                          [WIDE[s][:, k * T + t * P:k * T + (t + 1) * P] for k in range(8)],
                                          [w[:, k, :] for k in range(8)])
                        ins.then_inc(d_full, 1)
                    if st.name == "k3":
                        for j in range(2):
                            b = bank_d(d + j)
                            for m in range(4):
                                mm = 4 * j + m
                                ins = product(b[:, m * C:(m + 1) * C], [W3K[:, k, mm * P:(mm + 1) * P] for k in range(2)],
                                              [CT[s][:, k, :] for k in range(2)])
                            ins.then_inc(d_full, 1)
                    if st.name == "v3":
                        for j in range(2):
                            b = bank_a(a + j)
                            product(b[0:C, :], [CT[s][:, k, :] for k in range(2)],
                                    [W3V[:, k, j * 512:(j + 1) * 512] for k in range(2)]).then_inc(a_full, 1)

            def after_first():
                pe.wait_ge(a_full, A1)
                pe.sem_inc(a_full, NA - A1)
                pe.wait_ge(d_full, D1)
                pe.sem_inc(d_full, ND - D1)

            three_passes(pe, steps_of, after_first)


def kernel(**inputs):
    import numpy as np
    import concourse.bacc as bacc
    from concourse.bass_utils import run_bass_kernel_spmd as run

    v = {k: np.asarray(a) for k, a in inputs.items()}

    def tiles(w):
        k, n = w.shape
        return w.reshape(k // P, P, n).transpose(1, 0, 2).reshape(P, -1)

    L0, L1, L2, L3 = "L0_xattn_", "L1_xattn_", "L2_xattn_", "L3_xattn_"
    parts = [v[L0 + "Wq"], v[L0 + "Wk"], v[L0 + "Wv"], v[L0 + "Wo"],
             v[L1 + "Wq"].T, v[L1 + "Wk"].T, v[L1 + "Wv"].T, v[L1 + "Wo"].T,
             v[L2 + "w_qkv"].T, v[L2 + "w_sa_out"].T, v[L2 + "wq"].T,
             np.concatenate([v[L2 + "wk"].T, v[L2 + "wv"].T], axis=1), v[L2 + "w_ca_out"].T,
             v[L2 + "w_ff1"].T, v[L2 + "w_ff2"].T, v[L3 + "W_Q"], v[L3 + "W_K"], v[L3 + "W_V"], v[L3 + "W_O"]]
    wall = np.ascontiguousarray(np.concatenate([tiles(w) for w in parts], axis=1))
    cols = np.ascontiguousarray(np.concatenate(
        [v[n].reshape(-1, P).T for n in (L0 + "g_q", L0 + "g_c", L1 + "gamma_q", L1 + "gamma_kv", L2 + "b_ff1")], axis=1))
    rows = np.stack([v[n] for n in (L0 + "g_out", L2 + "g1", L2 + "b1", L2 + "g2", L2 + "b2", L2 + "b_ff2", L2 + "g3",
                                    L2 + "b3")])
    arrays = {"x": v["x"], "ctx": v["ctx_1024"], "idx": v["itok_BxS_0_255"], "mask": v["mask_BxS2_bf1"].view(np.uint8),
              "wall": wall, "cols": cols, "rows": rows}
    arrays = {k: np.ascontiguousarray(a) for k, a in arrays.items()}

    nc = bacc.Bacc("TRN2", target_bir_lowering=False, num_devices=1, dynamic_dma_scratch_size=1024)
    args = [nc.dram_tensor(n, a.shape, mybir.dt.from_np(a.dtype), kind="ExternalInput").ap() for n, a in arrays.items()]
    scratch = nc.dram_tensor("scratch", (2, 5, T, D), F32, kind="Internal").ap()
    out = nc.dram_tensor("out", (B, T, D), F32, kind="ExternalOutput").ap()
    build(nc, *args, scratch, out)
    r = run(nc, [arrays], core_ids=[0])
    return r.results[0]["out"]
```

```python
from contextlib import ExitStack

import concourse.bass as bass
from concourse import mybir

F32 = mybir.dt.float32
BF16 = mybir.dt.bfloat16
U8 = mybir.dt.uint8
I32 = mybir.dt.int32
ALU = mybir.AluOpType
ACT = mybir.ActivationFunctionType
AX = mybir.AxisListType

B, T, D, C, H = 16, 256, 256, 120, 16
P = 128
HD = D // H
F = 1024
D3 = 64
M3 = H * D3 // P
G = 4
RING = 4
BIG = float(2 ** 100)
EPS_OF = [1e-6, 1e-6, 1.1920929e-07, 1.1920929e-07, 1e-5, 1e-5]
DEN0, DEN1 = 1e-30, 1e-6

WIDTHS = [("q0", 512), ("k0", 512), ("v0", 512), ("o0", 512), ("q1", 512), ("k1", 512), ("v1", 512), ("o1", 512),
          ("qkv", 1536), ("so", 512), ("qc", 512), ("kvc", 1024), ("co", 512), ("f1", 2048), ("f2", 2048),
          ("Q3", 2048), ("K3", 2048), ("V3", 2048), ("O3", 2048)]
BLOCK_WIDTHS = [("0", 2048), ("1", 2048), ("S", 2048), ("C", 2048), ("F", 4096), ("3", 8192)]
WCOLS = sum(w for _, w in WIDTHS)
ROWS = ["g_out", "g1", "b1", "g2", "b2", "b_ff2", "g3", "b3"]

BANKS = {
    "loadc": (0, 0), "masks": (0, 0), "cnorm": (0, 0), "cscale": (0, 0), "cT": (2, 0), "v": (1, 0), "k": (0, 1),
    "load": (0, 0), "xnorm": (0, 0), "xscale": (0, 0), "xT": (1, 0), "q": (1, 0), "km": (0, 0), "S": (0, 1),
    "E": (0, 0), "N": (0, 0), "T": (1, 0), "PV": (0, 1), "OTT": (0, 1), "ONT": (1, 0), "OUT": (0, 1),
    "outnorm": (0, 0), "outscale": (0, 0), "ckv": (1, 0), "cout": (0, 0), "cin": (0, 0), "ckT": (0, 1), "qkv": (1, 0),
    "sout": (0, 0), "sin": (0, 0), "qpT": (1, 0), "kpT": (0, 1), "qc": (1, 0), "qout": (0, 0), "qin": (0, 0),
    "ln": (0, 0), "scale": (0, 0), "f1": (1, 0), "f2": (0, 1), "k3": (0, 1), "v3": (1, 0), "q3": (1, 0),
    "PV3": (1, 0), "OUT3": (0, 1), "store": (0, 0),
}


def units(block):
    if block == "S":
        return [(g, qt, half) for g in range(G) for qt, half in ((0, 0), (1, 0), (1, 1))]
    if block == "1":
        return [(g, 0, half) for g in range(G) for half in range(2)]
    return [(g, qt, 0) for g in range(G) for qt in range(2)]


def attention(block):
    todo, n = [], len(units(block))
    group = [u[0] for u in units(block)]
    late = 3 if block == "1" else 4 if block == "3" else 3
    ends = {max(i for i in range(n) if group[i] == g): g for g in range(G)}

    def values(g):
        todo.append(("PV3" if block == "3" else "PV", block, g))
        if block != "3" and g >= 1:
            todo.append(("OTT", block, g - 1))

    todo += [("km", block, 0), ("km", block, 1)]
    for i in range(n + late + 1):
        t = i - late
        if 0 <= t < n:
            if block != "1":
                todo.append(("T", block, t))
            elif t in ends:
                values(ends[t])
        if i < n:
            if block == "3" and i % 2 == 0:
                todo.append(("q3", block, group[i]))
            todo.append(("S", block, i))
            if i in ends and ends[i] + 2 < G:
                todo.append(("km", block, ends[i] + 2))
        if 0 <= i - 1 < n:
            todo.append(("E", block, i - 1))
        if block == "3" and 0 <= i - 2 < n:
            todo.append(("N", block, i - 2))
        if block != "1" and t - 1 in ends:
            values(ends[t - 1])
    if block == "3":
        return todo + [("OUT3", block, 0), ("OUT3", block, 1)]
    return todo + [("OTT", block, G - 1), ("ONT", block, 0), ("OUT", block, 0)]


def sequence_steps():
    context = [("loadc", "0", 0), ("masks", "0", 0), ("cnorm", "0", 0), ("cscale", "0", 0), ("cT", "0", 0), ("v", "0", 0),
               ("k", "0", 0)]
    s = [("load", "0", 0), ("xnorm", "0", 0), ("xscale", "0", 0), ("xT", "0", 0), ("q", "0", 0)]
    s += attention("0")
    s += [("outnorm", "0", 0), ("k", "1", 0), ("v", "1", 0), ("outscale", "0", 0), ("xnorm", "1", 0), ("ckv", "C", 0),
          ("ckv", "C", 1), ("cout", "C", 0), ("xscale", "1", 0), ("xT", "1", 0), ("q", "1", 0)]
    s += attention("1")
    s += [("cin", "C", 0), ("xT", "S", 0), ("qkv", "S", 0), ("qkv", "S", 1), ("qkv", "S", 2), ("sout", "S", 0),
          ("sin", "S", 0), ("qpT", "S", 0),
          ("kpT", "S", 0)]
    s += attention("S")
    s += [("ln", "S", 0), ("ckT", "C", 0), ("scale", "S", 0), ("xT", "C", 0), ("qc", "C", 0), ("qout", "C", 0),
          ("qin", "C", 0), ("v3", "3", 0), ("v3", "3", 1), ("qpT", "C", 0)]
    s += attention("C")
    s += [("ln", "C", 0), ("scale", "C", 0), ("xT", "F", 0), *[("f1", "F", j) for j in range(4)],
          ("f2", "F", 0), ("f2", "F", 1), ("ln", "F", 0), ("k3", "3", 0), ("k3", "3", 1), ("scale", "F", 0), ("xT", "3", 0)]
    s += attention("3")
    s += [("ln", "3", 0), ("scale", "3", 0), ("store", "3", 0)]
    return context, s


CONTEXT, MAIN = sequence_steps()
SEQUENCE = CONTEXT + MAIN
CUT = [MAIN.index(("T", "C", 5)), MAIN.index(("S", "C", 0))]
CONTEXT_AT = {"loadc": ("km", "3", 0), "masks": ("S", "3", 1), "cnorm": ("S", "3", 2), "cscale": ("S", "3", 5),
              "cT": ("ln", "3", 0), "v": ("scale", "3", 0), "k": ("scale", "3", 0)}


class Step:

    def __init__(self, name, block, i, slot, back, a, d, v, g):
        self.name, self.block, self.i, self.slot, self.back = name, block, i, slot, back
        self.a, self.d, self.v, self.g = a, d, v, g


VEC_OWN = {"masks": 2, "S": 1, "N": 1, "OTT": 2, "ln": 2, "scale": 2, ("S", "1"): 0, ("scale", "3"): 0}
POOL_OWN = {"cnorm": 1, "xnorm": 1, "outnorm": 1, "ln": 1}
NA, ND = 2 * sum(BANKS[x[0]][0] for x in SEQUENCE), 2 * sum(BANKS[x[0]][1] for x in SEQUENCE)
assert NA % RING == 0 and ND % RING == 0


def slot_steps(s):
    steps = []
    for x in MAIN[CUT[s]:]:
        steps += [(c, s, 0) for c in CONTEXT if CONTEXT_AT[c[0]] == x]
        steps.append((x, s, 1))
    return steps + [(x, s, 0) for x in MAIN[:CUT[s]]]


TURNS = [
    3, 1, 3, 3, 1, 1, 1, 2, 1, 6, 1, 2, 1, 3, 1, 1, 1, 10, 1, 2, 1, 2, 1, 1, 1, 1, 1, 2, 1, 1, 3, 1, 1, 1, 1, 1, 3, 1,
    2, 1, 6, 1, 3, 1, 1, 4, 6, 1, 1, 1, 1, 3, 4, 4, 2, 3, 2, 5, 2, 1, 5, 2, 1, 1, 3, 3, 1, 1, 1, 1, 1, 1, 1, 2, 1, 1,
    1, 1, 1, 8, 1, 6, 1, 1, 1, 1, 1, 1, 1, 1, 3, 1, 1, 1, 3, 2, 1, 1, 4, 1, 2, 1, 1, 1, 4, 1, 4, 1, 4, 1, 4, 1, 6, 1,
    1, 1, 1, 1, 1, 1, 1, 2, 2, 4, 1, 4, 1, 1, 1, 1, 3, 1, 2, 1, 1, 3, 1, 1, 2, 3, 1, 5, 1, 1, 1, 3, 4, 1, 3, 1, 1, 1,
    7, 1, 6, 1, 6, 2, 1, 2, 1, 2, 2, 3, 1, 1, 2, 9, 1, 14, 1, 3, 2, 1, 1, 3, 2, 2, 1, 1, 2, 1, 3, 2, 8, 1, 9, 1, 9, 1,
    1, 1, 4, 1, 1, 1, 3, 1, 1, 6, 2, 3, 1, 3, 1, 3, 2, 5, 2, 11, 1, 3, 1, 1, 1, 5, 2, 2, 1, 1, 3, 2, 1, 1, 1, 1, 1, 1,
    2, 1, 2, 1, 5, 1, 3, 1, 2, 3, 8, 4,
]


def merged():
    lists, at, order = [slot_steps(0), slot_steps(1)], [0, 0], []
    for n, count in enumerate(TURNS):
        order += lists[n % 2][at[n % 2]:at[n % 2] + count]
        at[n % 2] += count
    assert at == [len(x) for x in lists]
    return order


def numbered(order, a, d, v, g):
    steps = []
    for (name, block, i), slot, back in order:
        steps.append(Step(name, block, i, slot, back, a, d, v, g))
        a, d = a + BANKS[name][0], d + BANKS[name][1]
        v += VEC_OWN.get((name, block), VEC_OWN.get(name, 0))
        g += POOL_OWN.get(name, 0)
    return steps, a, d, v, g


ORDER = merged()
FIRST, A1, D1, V1, G1 = numbered([x for x in ORDER if not x[2]], 0, 0, 0, 0)
LOOP, _, _, V2, G2 = numbered(ORDER, NA, ND, V1, G1)
NV, NG = V2 - V1, G2 - G1
LAST, _, _, _, _ = numbered([x for x in ORDER if x[2]], NA, ND, V1, G1)
PASSES = B // 2


def table(steps):
    found = {}
    for x in LOOP:
        if not x.back:
            found[x.name, x.block, x.i, x.slot, 1] = (x.a - NA, x.d - ND)
    for x in steps:
        found[x.name, x.block, x.i, x.slot, x.back] = (x.a, x.d)
    return found


SQUARE_NO = {("xnorm", "0"): 1, ("outnorm", "0"): 2, ("xnorm", "1"): 3}
LN_NO = {"S": 1, "C": 2, "F": 3, "3": 4}
GROUP_NO = {"0": 0, "1": 4, "S": 8, "C": 12, "3": 16}
EXP_NO = {"0": 0, "1": 8, "S": 16, "C": 28, "3": 36}


def build(nc, x, ctx, idx, mask, wall, cols, rows, scratch, out):
    with ExitStack() as stack:
        def sb(name, shape, dt=F32):
            return stack.enter_context(nc.sbuf_tensor(name, shape, dt))

        def two(name, shape, dt=F32):
            return [sb(f"{name}{s}", shape, dt) for s in range(2)]

        def sem(name):
            return stack.enter_context(nc.semaphore(name))

        def sem2(name):
            return [sem(f"{name}{s}") for s in range(2)]

        W = sb("W", [P, WCOLS])
        COLS = sb("COLS", [P, 16])
        ROW = sb("ROW", [P, len(ROWS), D])
        ID = sb("ID", [P, P])
        IDB = sb("IDB", [P, P], BF16)
        CAUSAL = sb("CAUSAL", [P, P], BF16)
        HM = sb("HM", [P, 8])
        HM3 = sb("HM3", [P, 2])
        TOP = sb("TOP", [P, P], BF16)
        ONEF = sb("ONEF", [P, H])
        NHALF = sb("NHALF", [P, 2])
        EPS = sb("EPS", [P, len(EPS_OF)])
        KEY = sb("KEY", [P, 1])
        KEYI = sb("KEYI", [P, 1], I32)

        X = two("X", [P, 2, D])
        XN = two("XN", [P, 2, D])
        XT = two("XT", [P, 2, T])
        QT = two("QT", [P, 2, T])
        KT = two("KT", [P, M3, C])
        CX = two("CX", [C, D])
        CN = two("CN", [C, 2, D])
        CT = two("CT", [P, 6, C])
        KM = two("KM", [P, 2, 4 * T])
        VA = two("VA", [P, H, 32])
        VS = two("VS", [P, 2, H, 32])
        V3 = [k[:, :, 512:1024] for k in KM]
        PB = two("PB", [P, RING, 512])
        PT = two("PT", [P, 2, 4, 3, P])
        OT = two("OT", [P, 2, T])
        WIDE = two("WIDE", [P, 8 * T])
        KP = two("KP", [C, D])
        NM = two("NM", [P, RING, 4])
        SUM = two("SUM", [P, RING, 2, 4])
        REC = two("REC", [P, RING, 2, 4])
        SS = two("SS", [P, 8])
        RSTD = two("RSTD", [P, 2])
        CRSTD = two("CRSTD", [P, 2])
        VAR = two("VAR", [P, 2])
        BN = two("BN", [P, 2, 6])
        MV = two("MV", [P, 2, 2])
        IDX = two("IDX", [C, T], I32)
        BAND = two("BAND", [C, T])
        MROW = two("MROW", [1, C], U8)
        MCOL = two("MCOL", [C, 1], U8)
        BIAS = two("BIAS", [P, C], BF16)
        MASK = two("MASK", [C, 1])

        PA = stack.enter_context(nc.psum_tensor("PA", [P, RING, 512], F32))
        PD = stack.enter_context(nc.psum_tensor("PD", [P, RING, 512], F32))

        weights_in = {blk: sem(f"weights_in_{blk}") for blk, _ in BLOCK_WIDTHS}
        cols_in, rows_in = sem("cols_in"), sem("rows_in")
        consts = sem("consts")
        a_full, d_full = sem("a_full"), sem("d_full")
        a_empty, d_empty = sem("a_empty"), sem("d_empty")
        ctx_loaded = sem2("ctx_loaded")
        x_loaded = sem2("x_loaded")
        masks_ready = sem2("masks_ready")
        csquare_done = sem2("csquare_done")
        square_done = sem2("square_done")
        crstd_ready = sem2("crstd_ready")
        rstd_ready = sem2("rstd_ready")
        cn_ready = sem2("cn_ready")
        xn_ready = sem2("xn_ready")
        km_ready = sem2("km_ready")
        exp_done = sem2("exp_done")
        recip_ready = sem2("recip_ready")
        p_scaled = sem2("p_scaled")
        moments = sem2("moments")
        x_ready = sem2("x_ready")
        yb_ready = sem2("yb_ready")
        bounced_out = sem2("bounced_out")
        self_in, ckv_in, qc_in = sem2("self_in"), sem2("ckv_in"), sem2("qc_in")
        stored = sem2("stored")
        sync_turns = sem("sync_turns")
        stats_done = sem("stats_done")
        vec = sem("vec")
        pool = sem("pool")
        vec_own = sem("vec_own")
        var_ready = sem("var_ready")

        offsets, at = {}, 0
        for name, w in WIDTHS:
            offsets[name] = (at, w)
            at += w

        def weight(name, width):
            o, w = offsets[name]
            return W[:, o:o + w].rearrange("p (k n) -> p k n", n=width)

        WQ = {"0": weight("q0", D), "1": weight("q1", D)}
        WK = {"0": weight("k0", D), "1": weight("k1", D)}
        WV = {"0": weight("v0", D), "1": weight("v1", D)}
        WO = {"0": weight("o0", D), "1": weight("o1", D), "S": weight("so", D), "C": weight("co", D)}
        WQKV, WQC, WKVC = weight("qkv", 3 * D), weight("qc", D), weight("kvc", 2 * D)
        W1, W2 = weight("f1", F), weight("f2", D)
        W3Q, W3K, W3V, W3O = weight("Q3", H * D3), weight("K3", H * D3), weight("V3", H * D3), weight("O3", D)

        def row(name):
            return ROW[:, ROWS.index(name), :]

        def kt(s, block):
            if block == "S":
                return KT[s][:, :, :].rearrange("p m n -> p (m n)")[:, 0:2 * T].rearrange("p (m n) -> p m n", n=T)
            return KT[s][:, :, :]

        def keys(block):
            return T if block == "S" else C

        def pv(s, block):
            return VS[s] if block == "S" else VA[s]

        def by_position(s, t, n):
            flat = scratch[s, t].rearrange("n c -> (n c)")[0:n * D]
            return flat.rearrange("(h n d) -> n h d", h=H, d=HD)

        block = stack.enter_context(nc.Block())

        N_KM, N_EXP, N_L3, N_RSTD = 5 * G, 8 * 4 + 12, 8, 7

        def three_passes(eng, steps_of, after_first=lambda: None):
            steps_of(FIRST, 0, [0, 0], 0)
            after_first()
            own = [eng.alloc_register(f"pass_of_slot{s}") for s in range(2)]
            with eng.Fori(0, PASSES - 1) as it:
                for r in own:
                    eng.reg_mov(r, it)
                steps_of(LOOP, it, [eng.snap(r) for r in own], 1)
            steps_of(LAST, PASSES - 1, [PASSES - 1] * 2, 1)

        @block.sync
        def _(sp):
            def steps_of(steps, it, turn, before):
                found = table(steps)

                def seq(per, k):
                    return turn[st.slot] * per + (k + (before - st.back) * per)

                if steps is FIRST:
                    steps = sorted(steps, key=lambda st: st.name not in ("loadc", "load"))
                for st in steps:
                    s = st.slot
                    n = it * 2 + (s + 2 * (before - st.back))
                    if st.name == "loadc":
                        if before:
                            sp.wait_ge(a_empty, it * NA + found["v3", "3", 1, s, 1][0] + 1 + RING)
                            sp.sem_inc(sync_turns, 1)
                        sp.dma_start(CX[s][:, :], ctx[bass.ds(n, 1)].rearrange("a n c -> (a n) c")).then_inc(ctx_loaded[s], 16)
                        sp.dma_start(MROW[s][:, :], mask[bass.ds(n, 1), :]).then_inc(ctx_loaded[s], 16)
                        sp.dma_start(MCOL[s][:, :], mask[bass.ds(n, 1), :].rearrange("a n -> n a")).then_inc(ctx_loaded[s], 16)
                        sp.dma_start(IDX[s][:, :], idx[bass.ds(n, 1), :].to_broadcast([C, T])).then_inc(ctx_loaded[s], 16)
                    if st.name == "load":
                        if before:
                            sp.wait_ge(x_ready[s], turn[s] * 5 + 5)
                            sp.sem_inc(sync_turns, 1)
                        sp.dma_start(X[s][:, :, :], x[bass.ds(n, 1)].rearrange("a (t p) c -> p (a t) c", p=P))\
                          .then_inc(x_loaded[s], 16)
                    if st.name == "cout":
                        sp.wait_ge(a_empty, it * NA + found["ckv", "C", 1, s, st.back][0] + 1 + RING)
                        for t in range(2):
                            sp.dma_start(scratch[s, 3 + t, 0:C, :], CN[s][:, t, :]).then_inc(bounced_out[s], 16)
                    if st.name == "cin":
                        sp.wait_ge(d_full, it * ND + found["OUT", "1", 0, s, st.back][1] + 1)
                        sp.sem_inc(sync_turns, 1)
                        sp.wait_ge(bounced_out[s], seq(96, 32))
                        sp.dma_start(KP[s][:, :].rearrange("p (h d) -> p h d", d=HD), by_position(s, 3, C))\
                          .then_inc(ckv_in[s], 16)
                        sp.dma_start(VA[s][0:C, :, 0:HD], by_position(s, 4, C)).then_inc(ckv_in[s], 16)
                    if st.name == "sout":
                        sp.wait_ge(a_empty, it * NA + found["qkv", "S", 2, s, st.back][0] + 1 + RING)
                        for t in range(3):
                            src = WIDE[s][:, 0:6 * D].rearrange("p (k t c) -> p k t c", k=2, t=3)[:, :, t, :]
                            sp.dma_start(scratch[s, t].rearrange("(k p) c -> p k c", p=P), src)\
                              .then_inc(bounced_out[s], 16)
                    if st.name == "sin":
                        sp.wait_ge(bounced_out[s], seq(96, 80))
                        for t, dst in ((0, XT[s]), (1, XN[s])):
                            for k in range(2):
                                sp.dma_start(dst[:, k, :].rearrange("p (h d) -> p h d", d=HD),
                                             by_position(s, t, T)[k * P:(k + 1) * P]).then_inc(self_in[s], 16)
                        for k in range(2):
                            sp.dma_start(VS[s][:, k, :, 0:HD], by_position(s, 2, T)[k * P:(k + 1) * P])\
                              .then_inc(self_in[s], 16)
                    if st.name == "qout":
                        sp.wait_ge(a_empty, it * NA + found["qc", "C", 0, s, st.back][0] + 1 + RING)
                        sp.dma_start(scratch[s, 0].rearrange("(k p) c -> p k c", p=P),
                                     WIDE[s][:, 0:2 * D].rearrange("p (k c) -> p k c", k=2)).then_inc(bounced_out[s], 16)
                    if st.name == "qin":
                        sp.wait_ge(bounced_out[s], seq(96, 96))
                        for k in range(2):
                            sp.dma_start(XT[s][:, k, :].rearrange("p (h d) -> p h d", d=HD),
                                         by_position(s, 0, T)[k * P:(k + 1) * P]).then_inc(qc_in[s], 16)
                    if st.name == "store":
                        sp.wait_ge(x_ready[s], seq(5, 5))
                        sp.sem_inc(sync_turns, 1)
                        sp.dma_start(out[bass.ds(n, 1)].rearrange("a (t p) c -> p (a t) c", p=P), XN[s][:, :, :])\
                          .then_inc(stored[s], 16)

            three_passes(sp, steps_of)
            for s in range(2):
                sp.wait_ge(stored[s], PASSES * 16)

        @block.gpsimd
        def _(gp):
            gp.memset(ID[:, :], 0.0).then_inc(pool, 1)
            gp.memset(TOP[:, :], 0.0)
            gp.memset(CAUSAL[:, :], 0.0).then_inc(pool, 1)
            gp.memset(HM[:, :], 1.0).then_inc(pool, 1)
            gp.memset(HM3[:, :], 1.0).then_inc(pool, 1)
            gp.iota(KEYI[:, :], pattern=[[0, 1]], base=0, channel_multiplier=-1).then_inc(pool, 1)
            gp.wait_ge(pool, 5)
            gp.affine_select(out=ID[:, :], in_=ID[:, :], compare_op=ALU.not_equal, fill=1.0, base=0,
                             pattern=[[-1, P]], channel_multiplier=1).then_inc(pool, 1)
            gp.affine_select(out=CAUSAL[:, :], in_=CAUSAL[:, :], compare_op=ALU.is_ge, fill=-BIG, base=0,
                             pattern=[[-1, P]], channel_multiplier=1).then_inc(consts, 1)
            gp.affine_select(out=HM[:, :], in_=HM[:, :], compare_op=ALU.is_ge, fill=0.0, base=0,
                             pattern=[[-HD, 8]], channel_multiplier=1).then_inc(pool, 1)
            gp.affine_select(out=HM3[:, :], in_=HM3[:, :], compare_op=ALU.is_ge, fill=0.0, base=0,
                             pattern=[[-D3, 2]], channel_multiplier=1).then_inc(pool, 1)
            gp.wait_ge(pool, 8)
            gp.affine_select(out=HM[:, :], in_=HM[:, :], compare_op=ALU.is_gt, fill=0.0, base=HD,
                             pattern=[[HD, 8]], channel_multiplier=-1).then_inc(consts, 1)
            gp.affine_select(out=HM3[:, :], in_=HM3[:, :], compare_op=ALU.is_gt, fill=0.0, base=D3,
                             pattern=[[D3, 2]], channel_multiplier=-1).then_inc(consts, 1)
            gp.tensor_copy(IDB[:, :], ID[:, :]).then_inc(consts, 1)
            gp.tensor_copy(KEY[:, :], KEYI[:, :]).then_inc(consts, 1)
            gp.memset(NHALF[:, :], -0.5).then_inc(consts, 1)
            for j, eps in enumerate(EPS_OF):
                gp.memset(EPS[:, j:j + 1], eps)
            gp.memset(TOP[0:1, :], 1.0).then_inc(consts, 1)
            gp.memset(ONEF[:, :], 1.0).then_inc(consts, 1)
            gp.wait_ge(consts, 8)
            def steps_of(steps, it, turn, before):
                found = table(steps)

                def seq(per, k):
                    return turn[st.slot] * per + (k + (before - st.back) * per)

                def rstd(s, n, src, eps, dst, ready):
                    w = src.shape[-1]
                    gp.tensor_tensor(VAR[s][0:n, 0:w], src, EPS[0:n, eps:eps + w], ALU.add).then_inc(var_ready, 1)
                    gp.wait_ge(var_ready, it * NG + st.g + 1)
                    gp.tensor_tensor(dst[0:n, 0:w], VAR[s][0:n, 0:w], NHALF[0:n, 0:w], ALU.pow).then_inc(ready, 1)

                for st in steps:
                    s, blk, i = st.slot, st.block, st.i
                    if st.name == "cnorm":
                        gp.wait_ge(csquare_done[s], seq(1, 1))
                        rstd(s, C, SS[s][0:C, 0:1].to_broadcast([C, 2]), 1, CRSTD[s], crstd_ready[s])
                    if st.name == "xnorm":
                        gp.wait_ge(square_done[s], seq(3, SQUARE_NO[st.name, blk]))
                        rstd(s, P, SS[s][:, 2:4], 0 if blk == "0" else 2, RSTD[s], rstd_ready[s])
                    if st.name == "outnorm":
                        gp.wait_ge(square_done[s], seq(3, SQUARE_NO[st.name, blk]))
                        rstd(s, P, SS[s][:, 2:4], 0, RSTD[s], rstd_ready[s])
                    if st.name == "ln":
                        gp.wait_ge(moments[s], seq(4, LN_NO[blk]))
                        rstd(s, P, MV[s][:, :, 1:2].rearrange("p a b -> p (a b)"), 4, RSTD[s],
                             rstd_ready[s])
                    if st.name == "scale" and blk == "C":
                        gp.wait_ge(x_ready[s], seq(5, 3))
                        gp.tensor_tensor(XN[s][:, :, :], X[s][:, :, :],
                                         ROW[:, ROWS.index("b_ff2"):ROWS.index("b_ff2") + 1, :].to_broadcast([P, 2, D]),
                                         ALU.add).then_inc(yb_ready[s], 1)
                    if st.name == "km":
                        if i >= 2:
                            last = max(n for n, u in enumerate(units(blk)) if u[0] == i - 2)
                            gp.wait_ge(d_full, it * ND + found["S", blk, last, s, st.back][1] + 1)
                        if i == 0:
                            src = found[{"0": "k", "1": "k", "S": "kpT", "C": "ckT", "3": "k3"}[blk], blk, 0, s, st.back][1]
                            gp.wait_ge(d_empty, it * ND + src + 1 + RING)
                        if i == 2 and blk == "3":
                            gp.wait_ge(d_empty, it * ND + found["k3", "3", 1, s, st.back][1] + 1 + RING)
                        n = keys(blk)
                        if blk == "3":
                            dst = KM[s][:, i % 2, 0:4 * n].rearrange("p (m h n) -> p m h n", m=2, h=2)
                            src = KT[s][:, 2 * i:2 * i + 2, None, :].to_broadcast([P, 2, 2, n])
                            sel = HM3[:, None, :, None].to_broadcast([P, 2, 2, n])
                        else:
                            dst = KM[s][:, i % 2, 0:4 * n].rearrange("p (h n) -> p h n", h=4)
                            src = kt(s, blk)[:, i // 2:i // 2 + 1, :].to_broadcast([P, 4, n])
                            sel = HM[:, (i % 2) * 4:(i % 2) * 4 + 4, None].to_broadcast([P, 4, n])
                        gp.tensor_tensor(dst, src, sel, ALU.mult).then_inc(km_ready[s], 1)
                    if st.name == "N":
                        gp.wait_ge(recip_ready[s], seq(N_L3, i + 1))
                        p = PB[s][:, i % RING, 0:4 * C].rearrange("p (h n) -> p h n", h=4)
                        gp.tensor_tensor(p, p, REC[s][:, i % RING, 0, :, None].to_broadcast([P, 4, C]), ALU.mult)\
                          .then_inc(p_scaled[s], 1)

            three_passes(gp, steps_of)

        @block.scalar
        def _(act):
            act.dma_start(COLS[:, :], cols).then_inc(cols_in, 16)
            at = 0
            for blk, width in BLOCK_WIDTHS:
                act.dma_start(W[:, at:at + width], wall[:, at:at + width]).then_inc(weights_in[blk], 16)
                at += width
                if blk == "0":
                    for s in range(2):
                        act.wait_ge(ctx_loaded[s], 64)
                        act.wait_ge(x_loaded[s], 16)
                if blk == "1":
                    act.dma_start(ROW[:, :, :], rows.rearrange("(a r) c -> a r c", a=1).to_broadcast([P, len(ROWS), D]))\
                       .then_inc(rows_in, 16)
            act.sem_inc(a_empty, RING)
            act.wait_ge(cols_in, 16)
            act.wait_ge(consts, 8)
            act.wait_ge(vec, 6)

            def steps_of(steps, it, turn, before):
                found = table(steps)

                def seq(per, k):
                    return turn[st.slot] * per + (k + (before - st.back) * per)

                def bank(a):
                    act.wait_ge(a_full, it * NA + a + 1)
                    return PA[:, a % RING, :]

                for st in steps:
                    s, blk, i, a = st.slot, st.block, st.i, st.a
                    if st.name == "cnorm":
                        act.wait_ge(ctx_loaded[s], seq(64, 64))
                        act.activation(CN[s][:, 0, :], CX[s][:, :], ACT.Square, scale=1 / 16, accum_out=SS[s][0:C, 0:1])\
                           .then_inc(csquare_done[s], 1)
                    if st.name == "cscale":
                        act.wait_ge(crstd_ready[s], seq(1, 1))
                        act.activation(CN[s][:, 0, :], CX[s][:, :], ACT.Copy, scale=CRSTD[s][0:C, 0:1])
                        act.activation(CN[s][:, 1, :], CX[s][:, :], ACT.Copy, scale=CRSTD[s][0:C, 1:2])\
                           .then_inc(cn_ready[s], 1)
                    if st.name == "cT":
                        b = bank(a).rearrange("p (j n) -> p j n", n=P)
                        act.activation(CT[s][:, 0:2, :], b[:, 0:2, 0:C], ACT.Copy)
                        for k in range(2):
                            ins = act.activation(CT[s][:, 2 + k, :], b[:, 2 + k, 0:C], ACT.Copy, scale=COLS[:, 2 + k:3 + k])
                        ins.then_inc(a_empty, 1)
                        b = bank(a + 1).rearrange("p (j n) -> p j n", n=P)
                        for k in range(2):
                            ins = act.activation(CT[s][:, 4 + k, :], b[:, k, 0:C], ACT.Copy, scale=COLS[:, 6 + k:7 + k])
                        ins.then_inc(a_empty, 1)
                    if st.name == "xT":
                        b = bank(a).rearrange("p (k n) -> p k n", n=T)
                        if blk in "01":
                            c = 0 if blk == "0" else 4
                            for k in range(2):
                                ins = act.activation(XT[s][:, k, :], b[:, k, :], ACT.Copy, scale=COLS[:, c + k:c + k + 1])
                            ins.then_inc(a_empty, 1)
                        else:
                            act.activation(XT[s][:, :, :], b, ACT.Copy).then_inc(a_empty, 1)
                    if st.name == "q" or st.name == "qpT":
                        b = bank(a).rearrange("p (k n) -> p k n", n=T)
                        act.activation(QT[s][:, :, :], b, ACT.Copy).then_inc(a_empty, 1)
                    if st.name == "ONT":
                        b = bank(a).rearrange("p (k n) -> p k n", n=T)
                        act.activation(XT[s][:, :, :], b, ACT.Copy).then_inc(a_empty, 1)
                    if st.name == "v":
                        b = bank(a)[0:C, 0:D].rearrange("p (h d) -> p h d", d=HD)
                        if blk == "0":
                            act.wait_ge(masks_ready[s], seq(1, 1))
                            act.activation(VA[s][0:C, :, HD], ONEF[0:C, :], ACT.Copy, scale=MASK[s][:, 0:1])
                            act.activation(VA[s][0:C, :, 0:HD], b, ACT.Copy, scale=MASK[s][:, 0:1]).then_inc(a_empty, 1)
                        else:
                            act.activation(VA[s][0:C, :, HD], ONEF[0:C, :], ACT.Copy)
                            act.activation(VA[s][0:C, :, 0:HD], b, ACT.Copy).then_inc(a_empty, 1)
                    if st.name == "v3":
                        act.activation(V3[s][0:C, i, :], bank(a)[0:C, :], ACT.Copy).then_inc(a_empty, 1)
                    if st.name == "ckv":
                        act.activation(CN[s][:, i, :], bank(a)[0:C, 0:D], ACT.Copy).then_inc(a_empty, 1)
                    if st.name == "qkv":
                        w = WIDE[s][:, 0:6 * D].rearrange("p (k c) -> p k c", k=2)
                        if i < 2:
                            act.activation(w[:, i, 0:2 * D], bank(a), ACT.Copy).then_inc(a_empty, 1)
                        else:
                            b = bank(a).rearrange("p (k c) -> p k c", k=2)
                            act.activation(w[:, :, 2 * D:3 * D], b, ACT.Copy).then_inc(a_empty, 1)
                    if st.name == "qc":
                        b = bank(a)
                        act.activation(WIDE[s][:, 0:2 * D], b, ACT.Copy).then_inc(a_empty, 1)
                    if st.name == "f1":
                        b = bank(a).rearrange("p (k n) -> p k n", n=T)
                        for k in range(2):
                            m = 2 * i + k
                            ins = act.activation(WIDE[s][:, m * T:(m + 1) * T], b[:, k, :], ACT.Relu,
                                                 bias=COLS[:, 8 + m:9 + m])
                        ins.then_inc(a_empty, 1)
                    if st.name == "q3" or st.name == "PV3":
                        b = bank(a)
                        act.activation(WIDE[s][:, i * 512:(i + 1) * 512], b, ACT.Copy).then_inc(a_empty, 1)
                    if st.name == "E":
                        g, qt, half = units(blk)[i]
                        act.wait_ge(d_empty, it * ND + found["S", blk, i, s, st.back][1] + 1 + RING)
                        n = 4 * C if blk in "0C3" else 512
                        p = PB[s][:, i % RING, 0:n]
                        if blk == "1":
                            dst = PT[s][0:C, g % 2, 2 * half:2 * half + 2, 0:2, :].rearrange("p h q n -> p h (q n)")
                            act.activation(dst, PB[s][0:C, i % RING, :].rearrange("p (h n) -> p h n", h=2), ACT.Square,
                                           scale=0.25).then_inc(exp_done[s], 1)
                        else:
                            act.activation(p, p, ACT.Exp, scale=0.125 if blk == "3" else 0.25).then_inc(exp_done[s], 1)
                    if st.name == "T":
                        g, qt, half = units(blk)[i]
                        n = P if blk == "S" else C
                        b = bank(a)[0:n, :]
                        if blk == "S" and qt == 1:
                            dst = PT[s][:, g % 2, 2 * half:2 * half + 2, 1:3, :].rearrange("p h t n -> p h (t n)")
                            act.activation(dst, b.rearrange("p (h n) -> p h n", h=2), ACT.Copy).then_inc(a_empty, 1)
                        else:
                            act.activation(PT[s][0:n, g % 2, :, qt, :], b.rearrange("p (h n) -> p h n", h=4), ACT.Copy)\
                               .then_inc(a_empty, 1)
                    if st.name in ("xnorm", "outnorm"):
                        if st.name == "outnorm":
                            act.wait_ge(d_empty, it * ND + found["OUT", "0", 0, s, st.back][1] + 1 + RING)
                        elif blk == "1":
                            act.wait_ge(x_ready[s], seq(5, 1))
                        else:
                            act.wait_ge(x_loaded[s], seq(16, 16))
                            if steps is LOOP:
                                act.wait_ge(stored[s], turn[s] * 16 + 16)
                        for t in range(2):
                            ins = act.activation(XN[s][:, t, :], X[s][:, t, :], ACT.Square, scale=1 / 16,
                                                 accum_out=SS[s][:, 2 + t:3 + t])
                        ins.then_inc(square_done[s], 1)
                    if st.name == "xscale":
                        act.wait_ge(rstd_ready[s], seq(N_RSTD, SQUARE_NO["xnorm", blk]))
                        for t in range(2):
                            ins = act.activation(XN[s][:, t, :], X[s][:, t, :], ACT.Copy, scale=RSTD[s][:, t:t + 1])
                        ins.then_inc(xn_ready[s], 1)

            def after_first():
                act.wait_ge(a_empty, A1 + RING)
                act.sem_inc(a_empty, NA - A1)

            three_passes(act, steps_of, after_first)

        @block.vector
        def _(dve):
            dve.sem_inc(d_empty, RING)
            for s in range(2):
                dve.memset(VA[s][:, :, :], 0.0).then_inc(vec, 1)
                dve.memset(BIAS[s][:, :], 0.0)
                dve.memset(VS[s][:, :, :, :], 0.0).then_inc(vec, 1)
            dve.wait_ge(consts, 8)
            dve.wait_ge(vec, 4)
            for s in range(2):
                dve.memset(VS[s][:, :, :, HD], 1.0).then_inc(vec, 1)

            def steps_of(steps, it, turn, before):
                found = table(steps)

                def seq(per, k):
                    return turn[st.slot] * per + (k + (before - st.back) * per)

                def own(ins):
                    count[0] += 1
                    ins.then_inc(vec_own, 1)
                    dve.wait_ge(vec_own, it * NV + count[0])

                def bank(d):
                    dve.wait_ge(d_full, it * ND + d + 1)
                    return PD[:, d % RING, :]

                for st in steps:
                    s, blk, i, d = st.slot, st.block, st.i, st.d
                    count = [st.v]
                    if st.name == "masks":
                        dve.wait_ge(ctx_loaded[s], seq(64, 64))
                        dve.tensor_scalar(BIAS[s][0:1, :], MROW[s][:, :], -1.0, BIG, ALU.add, ALU.mult)
                        dve.tensor_copy(MASK[s][:, :], MCOL[s][:, :])
                        own(dve.tensor_scalar(BAND[s][:, :], IDX[s][:, :], KEY[0:C, 0:1], None, ALU.add))
                        own(dve.tensor_tensor(BAND[s][:, :], BAND[s][:, :], BAND[s][:, :], ALU.mult))
                        dve.tensor_scalar(BAND[s][:, :], BAND[s][:, :], 1.0, None, ALU.is_le).then_inc(masks_ready[s], 1)
                    if st.name == "k" or st.name == "ckT":
                        b = bank(d).rearrange("p (k n) -> p k n", n=T)[:, :, 0:C]
                        dve.tensor_copy(KT[s][:, 0:2, :], b).then_inc(d_empty, 1)
                    if st.name == "kpT":
                        b = bank(d).rearrange("p (k n) -> p k n", n=T)
                        dve.tensor_copy(kt(s, "S"), b).then_inc(d_empty, 1)
                    if st.name == "k3":
                        b = bank(d)[:, 0:4 * C].rearrange("p (m n) -> p m n", m=4)
                        dve.tensor_copy(KT[s][:, 4 * i:4 * i + 4, :], b).then_inc(d_empty, 1)
                    if st.name == "S":
                        b = bank(d)
                        if blk == "1":
                            if i == 0:
                                dve.wait_ge(masks_ready[s], seq(1, 1))
                            for h in range(2):
                                ins = dve.scalar_tensor_tensor(
                                    out=PB[s][0:C, i % RING, h * T:(h + 1) * T], in0=b[0:C, h * T:(h + 1) * T],
                                    scalar=0.0, in1=BAND[s][:, :], op0=ALU.max, op1=ALU.mult)
                            ins.then_inc(d_empty, 1)
                        else:
                            g, qt, half = units(blk)[i]
                            nh = 2 if blk == "S" and qt == 1 else 4
                            n = C if blk != "S" else T if qt == 1 else P
                            b = b[:, 0:nh * n].rearrange("p (h n) -> p h n", h=nh)
                            own(dve.tensor_reduce(NM[s][:, i % RING, 0:nh], b, AX.X, ALU.max, negate=True))
                            dve.tensor_tensor(PB[s][:, i % RING, 0:nh * n].rearrange("p (h n) -> p h n", h=nh), b,
                                              NM[s][:, i % RING, 0:nh, None].to_broadcast([P, nh, n]), ALU.add)\
                               .then_inc(d_empty, 1)
                    if st.name == "N":
                        dve.wait_ge(exp_done[s], seq(N_EXP, 36 + i + 1))
                        own(dve.tensor_reduce(SUM[s][:, i % RING, 0, :],
                                              PB[s][:, i % RING, 0:4 * C].rearrange("p (h n) -> p h n", h=4), AX.X, ALU.add))
                        dve.reciprocal(REC[s][:, i % RING, 0, :], SUM[s][:, i % RING, 0, :]).then_inc(recip_ready[s], 1)
                    if st.name == "PV":
                        b = bank(d)[:, 0:T]
                        dve.tensor_copy(OT[s][:, i % 2, :], b).then_inc(d_empty, 1)
                    if st.name == "OTT":
                        b = bank(d)[:, 0:2 * P].rearrange("p (t h c) -> p t h c", t=2, h=4)
                        own(dve.tensor_scalar(SUM[s][:, i, :, :], b[:, :, :, HD], DEN1 if blk == "1" else DEN0, None,
                                              ALU.max))
                        own(dve.reciprocal(REC[s][:, i, :, :], SUM[s][:, i, :, :]))
                        dve.tensor_tensor(XN[s][:, :, i * 64:(i + 1) * 64].rearrange("p t (h c) -> p t h c", h=4),
                                          b[:, :, :, 0:HD], REC[s][:, i, :, :, None].to_broadcast([P, 2, 4, HD]),
                                          ALU.mult).then_inc(d_empty, 1)
                    if st.name == "OUT3":
                        dve.tensor_tensor(X[s][:, i, :], bank(d)[:, 0:D], X[s][:, i, :], ALU.add).then_inc(d_empty, 1)
                    if st.name == "OUT":
                        b = bank(d).rearrange("p (t c) -> p t c", t=2)
                        dve.tensor_tensor(X[s][:, :, :], b, X[s][:, :, :], ALU.add).then_inc(d_empty, 1)
                    if st.name == "f2":
                        if i == 0:
                            dve.wait_ge(yb_ready[s], seq(1, 1))
                        dve.tensor_tensor(X[s][:, i, :], bank(d)[:, 0:D], XN[s][:, i, :], ALU.add).then_inc(d_empty, 1)
                    if st.name == "outscale":
                        if steps is FIRST:
                            dve.wait_ge(rows_in, 16)
                        dve.wait_ge(rstd_ready[s], seq(N_RSTD, 2))
                        for t in range(2):
                            ins = dve.scalar_tensor_tensor(out=X[s][:, t, :], in0=X[s][:, t, :], scalar=RSTD[s][:, t:t + 1],
                                                           in1=row("g_out"), op0=ALU.mult, op1=ALU.mult)
                        ins.then_inc(x_ready[s], 1)
                    if st.name == "ln":
                        name, n = {"S": ("OUT", 0), "C": ("OUT", 0), "F": ("f2", 1), "3": ("OUT3", 1)}[blk]
                        src = found[name, blk, n, s, st.back][1]
                        dve.wait_ge(d_empty, it * ND + src + 1 + RING)
                        for t in range(2):
                            own(dve.bn_stats(BN[s][:, t, :], X[s][:, t, :]))
                        dve.sem_inc(stats_done, 1)
                        for t in range(2):
                            ins = dve.bn_aggr(MV[s][:, t, :], BN[s][:, t, :])
                        ins.then_inc(moments[s], 1)
                    if st.name == "scale":
                        dve.wait_ge(rstd_ready[s], seq(N_RSTD, 3 + LN_NO[blk]))
                        dve.wait_ge(moments[s], seq(4, LN_NO[blk]))
                        if blk == "3":
                            for t in range(2):
                                ins = dve.tensor_scalar(XN[s][:, t, :], X[s][:, t, :], MV[s][:, t, 0:1],
                                                        RSTD[s][:, t:t + 1], ALU.subtract, ALU.mult)
                            ins.then_inc(x_ready[s], 1)
                        else:
                            gain, shift = {"S": ("g1", "b1"), "C": ("g2", "b2"), "F": ("g3", "b3")}[blk]
                            for t in range(2):
                                own(dve.scalar_tensor_tensor(out=X[s][:, t, :], in0=X[s][:, t, :],
                                                             scalar=MV[s][:, t, 0:1], in1=row(gain),
                                                             op0=ALU.subtract, op1=ALU.mult))
                            for t in range(2):
                                ins = dve.scalar_tensor_tensor(out=X[s][:, t, :], in0=X[s][:, t, :],
                                                               scalar=RSTD[s][:, t:t + 1], in1=row(shift),
                                                               op0=ALU.mult, op1=ALU.add)
                            ins.then_inc(x_ready[s], 1)

            def after_first():
                dve.wait_ge(d_empty, D1 + RING)
                dve.sem_inc(d_empty, ND - D1)

            three_passes(dve, steps_of, after_first)

        @block.tensor
        def _(pe):
            pe.wait_ge(consts, 8)
            pe.wait_ge(vec, 6)

            def steps_of(steps, it, turn, before):
                found = table(steps)

                def seq(per, k):
                    return turn[st.slot] * per + (k + (before - st.back) * per)

                def by_a(name, blk, i, s, k=1):
                    return found[name, blk, i, s, st.back][0] + k + RING

                def by_d(name, blk, i, s, k=1):
                    return found[name, blk, i, s, st.back][1] + k + RING

                def bank_a(a, *data):
                    pe.wait_ge(a_empty, it * NA + max([a + 1, *data]))
                    return PA[:, a % RING, :]

                def bank_d(d, *data):
                    pe.wait_ge(d_empty, it * ND + max([d + 1, *data]))
                    return PD[:, d % RING, :]

                def after_a(*counts):
                    pe.wait_ge(a_empty, it * NA + max(counts))

                def after_d(count):
                    pe.wait_ge(d_empty, it * ND + count)

                def product(out, lhs, rhs):
                    for k in range(len(lhs)):
                        ins = pe.matmul(out, lhs[k], rhs[k], start=(k == 0), stop=(k == len(lhs) - 1))
                    return ins

                waited = set()
                for st in steps:
                    s, blk, i, a, d = st.slot, st.block, st.i, st.a, st.d
                    if steps is FIRST and blk not in waited:
                        pe.wait_ge(weights_in[blk], 16)
                        waited.add(blk)
                    if st.name == "cT":
                        pe.wait_ge(cn_ready[s], seq(1, 1))
                        b = bank_a(a)
                        for j in range(4):
                            src = CX[s][:, (j % 2) * P:(j % 2 + 1) * P] if j < 2 else CN[s][:, 0, (j % 2) * P:(j % 2 + 1) * P]
                            ins = pe.transpose(b[:, j * P:j * P + C], src, ID[0:C, 0:C])
                        ins.then_inc(a_full, 1)
                        b = bank_a(a + 1)
                        for j in range(2):
                            ins = pe.transpose(b[:, j * P:j * P + C], CN[s][:, 1, j * P:(j + 1) * P], ID[0:C, 0:C])
                        ins.then_inc(a_full, 1)
                    if st.name == "xT":
                        if blk in "01":
                            pe.wait_ge(xn_ready[s], seq(2, 1 + (blk == "1")))
                            src = XN[s]
                        else:
                            src = X[s]
                            if blk == "S":
                                after_d(by_d("OUT", "1", 0, s))
                            else:
                                pe.wait_ge(x_ready[s], seq(5, {"C": 2, "F": 3, "3": 4}[blk]))
                        b = bank_a(a)
                        for k in range(2):
                            for t in range(2):
                                ins = pe.transpose(b[:, k * T + t * P:k * T + (t + 1) * P], src[:, t, k * P:(k + 1) * P], ID[:, :])
                        ins.then_inc(a_full, 1)
                    if st.name == "k":
                        after_a(by_a("cT", "0", 0, s, 1 if blk == "0" else 2))
                        b = bank_d(d)
                        c = 2 if blk == "0" else 4
                        for m in range(2):
                            ins = product(b[:, m * T:m * T + C], [WK[blk][:, k, m * P:(m + 1) * P] for k in range(2)],
                                          [CT[s][:, c + k, :] for k in range(2)])
                        ins.then_inc(d_full, 1)
                    if st.name == "v":
                        b = bank_a(a, by_a("cT", "0", 0, s, 1 if blk == "0" else 2))
                        c = 2 if blk == "0" else 4
                        product(b[0:C, 0:D], [CT[s][:, c + k, :] for k in range(2)],
                                [WV[blk][:, k, :] for k in range(2)]).then_inc(a_full, 1)
                    if st.name == "q":
                        b = bank_a(a, by_a("xT", blk, 0, s))
                        for m in range(2):
                            ins = product(b[:, m * T:(m + 1) * T], [WQ[blk][:, k, m * P:(m + 1) * P] for k in range(2)],
                                          [XT[s][:, k, :] for k in range(2)])
                        ins.then_inc(a_full, 1)
                    if st.name == "ckv":
                        b = bank_a(a)
                        product(b[0:C, 0:D], [CT[s][:, k, :] for k in range(2)],
                                [WKVC[:, k, i * D:(i + 1) * D] for k in range(2)]).then_inc(a_full, 1)
                    if st.name == "qkv":
                        b = bank_a(a, by_a("xT", blk, 0, s))
                        if i < 2:
                            product(b, [XT[s][:, k, i * P:(i + 1) * P] for k in range(2)],
                                    [WQKV[:, k, 0:2 * D] for k in range(2)]).then_inc(a_full, 1)
                        else:
                            for t in range(2):
                                ins = product(b[:, t * D:(t + 1) * D], [XT[s][:, k, t * P:(t + 1) * P] for k in range(2)],
                                              [WQKV[:, k, 2 * D:3 * D] for k in range(2)])
                            ins.then_inc(a_full, 1)
                    if st.name == "qc":
                        b = bank_a(a, by_a("xT", blk, 0, s))
                        for t in range(2):
                            ins = product(b[:, t * D:(t + 1) * D], [XT[s][:, k, t * P:(t + 1) * P] for k in range(2)],
                                          [WQC[:, k, :] for k in range(2)])
                        ins.then_inc(a_full, 1)
                    if st.name == "qpT" or st.name == "kpT":
                        if st.name == "qpT":
                            if blk == "S":
                                pe.wait_ge(self_in[s], seq(96, 96))
                            else:
                                pe.wait_ge(qc_in[s], seq(32, 32))
                        src, b = (XT[s], bank_a(a)) if st.name == "qpT" else (XN[s], bank_d(d))
                        for m in range(2):
                            for t in range(2):
                                ins = pe.transpose(b[:, m * T + t * P:m * T + (t + 1) * P], src[:, t, m * P:(m + 1) * P], ID[:, :])
                        ins.then_inc(a_full if st.name == "qpT" else d_full, 1)
                    if st.name == "ckT":
                        pe.wait_ge(ckv_in[s], seq(32, 32))
                        b = bank_d(d)
                        for m in range(2):
                            ins = pe.transpose(b[:, m * T:m * T + C], KP[s][:, m * P:(m + 1) * P], ID[0:C, 0:C])
                        ins.then_inc(d_full, 1)
                    if st.name == "S":
                        g, qt, half = units(blk)[i]
                        if blk == "3" and qt == 0:
                            after_a(by_a("q3", "3", g, s))
                        elif i == 0:
                            after_a(by_a("q" if blk in "01" else "qpT", blk, 0, s))
                        if i == 0 or units(blk)[i - 1][0] != g:
                            pe.wait_ge(km_ready[s], seq(N_KM, GROUP_NO[blk] + g + 1))
                        b = bank_d(d)
                        if blk in "0C":
                            if blk == "0" and i == 0:
                                pe.wait_ge(masks_ready[s], seq(1, 1))
                            ins = pe.matmul(b[:, 0:4 * C], QT[s][:, g // 2, qt * P:(qt + 1) * P], KM[s][:, g % 2, 0:4 * C],
                                            start=True, stop=(blk == "C"))
                            if blk == "0":
                                ins = pe.matmul(b[:, 0:4 * C].rearrange("p (h n) -> p h n", h=4), TOP[:, :],
                                                BIAS[s][:, None, :].to_broadcast([P, 4, C]), start=False, stop=True)
                        elif blk == "1":
                            for j in range(2):
                                h = 2 * half + j
                                ins = pe.matmul(b[0:C, j * T:(j + 1) * T], KM[s][:, g % 2, h * C:(h + 1) * C],
                                                QT[s][:, g // 2, :], start=True, stop=True)
                        elif blk == "3":
                            for j in range(2):
                                m = 2 * g + j
                                ins = pe.matmul(b[:, j * 2 * C:(j + 1) * 2 * C], WIDE[s][:, m * T + qt * P:m * T + (qt + 1) * P],
                                                KM[s][:, g % 2, j * 2 * C:(j + 1) * 2 * C], start=True, stop=True)
                        else:
                            k = KM[s][:, g % 2, :].rearrange("p (h n) -> p h n", h=4)
                            q = QT[s][:, g // 2, qt * P:(qt + 1) * P]
                            if qt == 0:
                                pe.matmul(b.rearrange("p (h n) -> p h n", h=4), q, k[:, :, 0:P], start=True, stop=False)
                                ins = pe.matmul(b.rearrange("p (h n) -> p h n", h=4), IDB[:, :],
                                                CAUSAL[:, None, :].to_broadcast([P, 4, P]), start=False, stop=True)
                            else:
                                pe.matmul(b.rearrange("p (h n) -> p h n", h=2), q, k[:, 2 * half:2 * half + 2, :],
                                          start=True, stop=False)
                                ins = pe.matmul(b.rearrange("p (h n) -> p h n", h=2)[:, :, P:T], IDB[:, :],
                                                CAUSAL[:, None, :].to_broadcast([P, 2, P]), start=False, stop=True)
                        ins.then_inc(d_full, 1)
                    if st.name == "T":
                        g, qt, half = units(blk)[i]
                        if blk == "3":
                            pe.wait_ge(p_scaled[s], seq(N_L3, i + 1))
                        else:
                            pe.wait_ge(exp_done[s], seq(N_EXP, EXP_NO[blk] + i + 1))
                        n = P if blk == "S" else C
                        b = bank_a(a)
                        for j in range(4):
                            ins = pe.transpose(b[0:n, j * P:(j + 1) * P], PB[s][:, i % RING, j * n:(j + 1) * n], ID[:, :])
                        ins.then_inc(a_full, 1)
                    if st.name in ("PV", "PV3"):
                        if blk == "1":
                            pe.wait_ge(exp_done[s], seq(N_EXP, 8 + 2 * i + 2))
                            ready = [by_a("v", blk, 0, s)]
                        else:
                            ready = [by_a("T", blk, max(n for n, u in enumerate(units(blk)) if u[0] == i), s)]
                        if blk == "3":
                            b = bank_a(a, *ready)
                            for j in range(4):
                                h, r = 4 * i + j, 64 * (j % 2)
                                ins = pe.matmul(b[r:r + D3, (j // 2) * T:(j // 2 + 1) * T], V3[s][0:C, h // 8, (h % 8) * D3:(h % 8 + 1) * D3],
                                                PT[s][0:C, i % 2, j, 0:2, :].rearrange("p t n -> p (t n)"),
                                                start=True, stop=True)
                            ins.then_inc(a_full, 1)
                        else:
                            after_a(*ready)
                            b = bank_d(d)
                            for j in range(4):
                                h, r = 4 * i + j, 32 * j
                                p = PT[s][:, i % 2, j, :, :]
                                if blk == "S":
                                    pe.matmul(b[r:r + 32, 0:T], VS[s][:, 0, h, :], p[:, 0:2, :].rearrange("p t n -> p (t n)"),
                                              start=True, stop=False)
                                    ins = pe.matmul(b[r:r + 32, P:T], VS[s][:, 1, h, :], p[:, 2, :], start=False, stop=True)
                                else:
                                    ins = pe.matmul(b[r:r + 32, 0:T], VA[s][0:C, h, :],
                                                    p[0:C, 0:2, :].rearrange("p t n -> p (t n)"), start=True, stop=True)
                            ins.then_inc(d_full, 1)
                    if st.name == "OTT":
                        b = bank_d(d, by_d("PV", blk, i, s))
                        for t in range(2):
                            ins = pe.transpose(b[:, t * P:(t + 1) * P], OT[s][:, i % 2, t * P:(t + 1) * P], ID[:, :])
                        ins.then_inc(d_full, 1)
                    if st.name == "ONT":
                        after_d(by_d("OTT", blk, G - 1, s))
                        b = bank_a(a)
                        for k in range(2):
                            for t in range(2):
                                ins = pe.transpose(b[:, k * T + t * P:k * T + (t + 1) * P], XN[s][:, t, k * P:(k + 1) * P], ID[:, :])
                        ins.then_inc(a_full, 1)
                    if st.name == "OUT":
                        after_a(by_a("ONT", blk, 0, s))
                        b = bank_d(d)
                        for t in range(2):
                            ins = product(b[:, t * D:(t + 1) * D], [XT[s][:, k, t * P:(t + 1) * P] for k in range(2)],
                                          [WO[blk][:, k, :] for k in range(2)])
                        ins.then_inc(d_full, 1)
                    if st.name == "f1" or st.name == "q3":
                        w = W1 if st.name == "f1" else W3Q
                        b = bank_a(a, by_a("xT", blk, 0, s))
                        for m in range(2):
                            ins = product(b[:, m * T:(m + 1) * T],
                                          [w[:, k, (2 * i + m) * P:(2 * i + m + 1) * P] for k in range(2)],
                                          [XT[s][:, k, :] for k in range(2)])
                        ins.then_inc(a_full, 1)
                    if st.name == "f2" or st.name == "OUT3":
                        if i == 0:
                            after_a(by_a("f1", "F", 3, s) if st.name == "f2" else by_a("PV3", "3", G - 1, s))
                        w = W2 if st.name == "f2" else W3O
                        b = bank_d(d)
                        product(b[:, 0:D], [WIDE[s][:, k * T + i * P:k * T + (i + 1) * P] for k in range(8)],
                                [w[:, k, :] for k in range(8)]).then_inc(d_full, 1)
                    if st.name == "k3":
                        b = bank_d(d)
                        for m in range(4):
                            mm = 4 * i + m
                            ins = product(b[:, m * C:(m + 1) * C], [W3K[:, k, mm * P:(mm + 1) * P] for k in range(2)],
                                          [CT[s][:, k, :] for k in range(2)])
                        ins.then_inc(d_full, 1)
                    if st.name == "v3":
                        b = bank_a(a)
                        product(b[0:C, :], [CT[s][:, k, :] for k in range(2)],
                                [W3V[:, k, i * 512:(i + 1) * 512] for k in range(2)]).then_inc(a_full, 1)

            def after_first():
                pe.wait_ge(a_full, A1)
                pe.sem_inc(a_full, NA - A1)
                pe.wait_ge(d_full, D1)
                pe.sem_inc(d_full, ND - D1)

            three_passes(pe, steps_of, after_first)


def kernel(**inputs):
    import numpy as np
    import concourse.bacc as bacc
    from concourse.bass_utils import run_bass_kernel_spmd as run

    v = {k: np.asarray(a) for k, a in inputs.items()}

    def tiles(w):
        k, n = w.shape
        return w.reshape(k // P, P, n).transpose(1, 0, 2).reshape(P, -1)

    L0, L1, L2, L3 = "L0_xattn_", "L1_xattn_", "L2_xattn_", "L3_xattn_"
    parts = [v[L0 + "Wq"], v[L0 + "Wk"], v[L0 + "Wv"], v[L0 + "Wo"],
             v[L1 + "Wq"].T, v[L1 + "Wk"].T, v[L1 + "Wv"].T, v[L1 + "Wo"].T,
             v[L2 + "w_qkv"].T, v[L2 + "w_sa_out"].T, v[L2 + "wq"].T,
             np.concatenate([v[L2 + "wk"].T, v[L2 + "wv"].T], axis=1), v[L2 + "w_ca_out"].T,
             v[L2 + "w_ff1"].T, v[L2 + "w_ff2"].T, v[L3 + "W_Q"], v[L3 + "W_K"], v[L3 + "W_V"], v[L3 + "W_O"]]
    wall = np.ascontiguousarray(np.concatenate([tiles(w) for w in parts], axis=1))
    cols = np.ascontiguousarray(np.concatenate(
        [v[n].reshape(-1, P).T for n in (L0 + "g_q", L0 + "g_c", L1 + "gamma_q", L1 + "gamma_kv", L2 + "b_ff1")], axis=1))
    rows = np.stack([v[n] for n in (L0 + "g_out", L2 + "g1", L2 + "b1", L2 + "g2", L2 + "b2", L2 + "b_ff2", L2 + "g3",
                                    L2 + "b3")])
    arrays = {"x": v["x"], "ctx": v["ctx_1024"], "idx": v["itok_BxS_0_255"], "mask": v["mask_BxS2_bf1"].view(np.uint8),
              "wall": wall, "cols": cols, "rows": rows}
    arrays = {k: np.ascontiguousarray(a) for k, a in arrays.items()}

    nc = bacc.Bacc("TRN2", target_bir_lowering=False, num_devices=1, dynamic_dma_scratch_size=1024)
    args = [nc.dram_tensor(n, a.shape, mybir.dt.from_np(a.dtype), kind="ExternalInput").ap() for n, a in arrays.items()]
    scratch = nc.dram_tensor("scratch", (2, 5, T, D), F32, kind="Internal").ap()
    out = nc.dram_tensor("out", (B, T, D), F32, kind="ExternalOutput").ap()
    build(nc, *args, scratch, out)
    r = run(nc, [arrays], core_ids=[0])
    return r.results[0]["out"]
```
